# Optimizing a Trainium2 kernel written in Bass

```python
import numpy as np
import jax
import jax.numpy as jnp

def _softmax(x, axis=-1):
    return jax.nn.softmax(x, axis=axis)

def _gelu(x):
    return jax.nn.gelu(x, approximate=True)

def _silu(x):
    return jax.nn.silu(x)

def _sigmoid(x):
    return jax.nn.sigmoid(x)

def _layernorm(x, axis=-1, eps=1e-05):
    m = jnp.mean(x, axis=axis, keepdims=True)
    v = jnp.var(x, axis=axis, keepdims=True)
    return (x - m) / jnp.sqrt(v + eps)

def _scatter_add(tgt, idx, src, axis=0):
    return tgt.at[idx].add(src)

def _segment_sum(src, seg, n):
    return jax.ops.segment_sum(src, seg, n)
kernel_name = 'mk_xattn_ffn_d4_seqx_r4_f7476f'

def setup_inputs(seed: int=0):
    np.random.seed(seed)
    _w = jnp.asarray

    def _rec_inputs():
        import jax
        import jax.numpy as jnp
        _rk = jax.random.key(seed)
        x = -0.0002928 + 1 * jax.random.normal(jax.random.fold_in(_rk, 1), (2, 512, 256), jnp.float32)
        _lenS = 512 - jax.random.randint(jax.random.fold_in(_rk, 7), (2,), 0, max(1, 512 // 4) + 1, jnp.int32)
        _lenS2 = 1024 - jax.random.randint(jax.random.fold_in(_rk, 8), (2,), 0, max(1, 1024 // 4) + 1, jnp.int32)
        _ctx_1024P = jax.random.normal(jax.random.fold_in(_rk, 11), (2, 16, 256), jnp.float32)
        _ctx_1024c = jax.random.dirichlet(jax.random.fold_in(_rk, 511), 0.3 * jnp.ones((16,), jnp.float32), (2, 1024))
        _ctx_1024t = jnp.einsum('bsk,bkd->bsd', _ctx_1024c, _ctx_1024P)
        _ctx_1024t = _ctx_1024t * jax.lax.rsqrt(jnp.mean(jnp.square(_ctx_1024t)) + 1e-12) * 0.953939
        ctx_1024 = -1.39393e-06 + 0.999914 * (_ctx_1024t + 0.3 * jax.random.normal(jax.random.fold_in(_rk, 611), (2, 1024, 256), jnp.float32))
        fside_BxSxS2_0 = -1.47943e-05 + 1.00017 * jax.random.normal(jax.random.fold_in(_rk, 13), (2, 512, 1024), jnp.float32)
        _validS = jnp.arange(512)[None, :] < _lenS[:, None]
        _validS2 = jnp.arange(1024)[None, :] < _lenS2[:, None]
        _causal = jnp.tril(jnp.ones((512, 512), dtype=bool))
        mask_BxSxS2_if1 = jnp.where(jnp.ones((2, 512, 1024), dtype=bool), 1, 0).astype(jnp.int32)
        return (x, ctx_1024, fside_BxSxS2_0, mask_BxSxS2_if1)
    x, ctx_1024, fside_BxSxS2_0, mask_BxSxS2_if1 = _rec_inputs()

    def _L0_xattn_setup():
        import jax, jax.numpy as jnp
        import numpy as np
        EMB, HEADS = (256, 16)
        HEAD_DIM = EMB // HEADS

        def _linear(x, W, b):
            return jnp.einsum('bse,oe->bso', x, W) + b
        key = jax.random.key(seed)
        ks = jax.random.split(key, 11)
        B, S = (2, 512)
        sc = 1.0 / np.sqrt(EMB)
        inp = {'x': jax.random.normal(ks[0], (B, S, EMB), dtype=jnp.float32), 'y': jax.random.normal(ks[1], (B, S, EMB), dtype=jnp.float32), 'mask': jnp.ones((B, S, S), dtype=jnp.int32), 'Wq': jax.random.normal(ks[2], (EMB, EMB), dtype=jnp.float32) * sc, 'bq': jax.random.normal(ks[3], (EMB,), dtype=jnp.float32) * sc, 'Wk': jax.random.normal(ks[4], (EMB, EMB), dtype=jnp.float32) * sc, 'bk': jax.random.normal(ks[5], (EMB,), dtype=jnp.float32) * sc, 'Wv': jax.random.normal(ks[6], (EMB, EMB), dtype=jnp.float32) * sc, 'bv': jax.random.normal(ks[7], (EMB,), dtype=jnp.float32) * sc, 'Wo': jax.random.normal(ks[8], (EMB, EMB), dtype=jnp.float32) * sc, 'bo': jax.random.normal(ks[9], (EMB,), dtype=jnp.float32) * sc}
        return inp
    _L0_xattn_all = _L0_xattn_setup()
    _L0_xattn_in = {k: v for k, v in _L0_xattn_all.items() if k in ('Wq', 'bq', 'Wk', 'bk', 'Wv', 'bv', 'Wo', 'bo')}
    del _L0_xattn_all

    def _L0_ffn_setup():
        import jax, jax.numpy as jnp
        import numpy as np
        B, S, H = (2, 256, 256)
        E, F = (8, 1024)
        GATE_TEMP = 0.1
        key = jax.random.key(seed)
        ks = jax.random.split(key, 6)
        s_h = 1.0 / np.sqrt(H)
        s_f = 1.0 / np.sqrt(F)
        return {'hidden_states': jax.random.normal(ks[0], (B, S, H), dtype=jnp.float32), 'w_router': jax.random.normal(ks[1], (H, E), dtype=jnp.float32) * s_h, 'w_gating': jax.random.normal(ks[2], (H, E), dtype=jnp.float32) * s_h, 'w_gate': jax.random.normal(ks[3], (E, H, F), dtype=jnp.float32) * s_h, 'w_up': jax.random.normal(ks[4], (E, H, F), dtype=jnp.float32) * s_h, 'w_down': jax.random.normal(ks[5], (E, F, H), dtype=jnp.float32) * s_f}
    _L0_ffn_all = _L0_ffn_setup()
    _L0_ffn_in = {k: v for k, v in _L0_ffn_all.items() if k in ('w_router', 'w_gating', 'w_gate', 'w_up', 'w_down')}
    del _L0_ffn_all

    def _L1_xattn_setup():
        import jax, jax.numpy as jnp
        import numpy as np
        D1, D2, D3 = (256, 256, 256)
        key = jax.random.key(seed)
        k1, k2, kw, kb = jax.random.split(key, 4)
        x1 = jax.random.normal(k1, (8, 512, D1), dtype=jnp.float32)
        x2 = jax.random.normal(k2, (8, 512, D2), dtype=jnp.float32)
        bound = 1.0 / np.sqrt(D1 + D2)
        W = jax.random.uniform(kw, (D3, D1 + D2), minval=-bound, maxval=bound, dtype=jnp.float32)
        b = jax.random.uniform(kb, (D3,), minval=-bound, maxval=bound, dtype=jnp.float32)
        return {'x1': x1, 'x2': x2, 'W': W, 'b': b}
    _L1_xattn_all = _L1_xattn_setup()
    _L1_xattn_in = {k: v for k, v in _L1_xattn_all.items() if k in ('W', 'b')}
    del _L1_xattn_all

    def _L1_ffn_setup():
        import jax, jax.numpy as jnp
        import numpy as np
        B, S, D = (4, 128, 256)
        E, K, H = (64, 8, 64)
        ES, HS = (2, 512)
        key = jax.random.key(seed)
        ks = jax.random.split(key, 8)
        scale = 0.02
        rn = lambda k, shape, s: jax.random.normal(k, shape, jnp.float32) * s
        return {'x': rn(ks[0], (B, S, D), 1.0), 'router_w': rn(ks[1], (D, E), scale), 'router_b': jnp.zeros((E,), jnp.float32), 'w1': rn(ks[2], (E, D, H), scale), 'b1': jnp.zeros((E, H), jnp.float32), 'w2': rn(ks[3], (E, H, D), scale), 'b2': jnp.zeros((E, D), jnp.float32), 'sw1': rn(ks[4], (ES, D, HS), scale), 'sb1': jnp.zeros((ES, HS), jnp.float32), 'sw2': rn(ks[5], (ES, HS, D), scale), 'sb2': jnp.zeros((ES, D), jnp.float32)}
    _L1_ffn_all = _L1_ffn_setup()
    _L1_ffn_in = {k: v for k, v in _L1_ffn_all.items() if k in ('router_w', 'router_b', 'w1', 'b1', 'w2', 'b2', 'sw1', 'sb1', 'sw2', 'sb2')}
    del _L1_ffn_all

    def _L2_xattn_setup():
        import jax, jax.numpy as jnp
        import numpy as np
        D = 256
        key = jax.random.key(seed)
        ks = jax.random.split(key, 13)
        B, S, d = (4, 512, D)
        inp = {'q_in': jax.random.normal(ks[0], (B, S, d), jnp.float32), 'k_in': jax.random.normal(ks[1], (B, S, d), jnp.float32), 'v_in': jax.random.normal(ks[2], (B, S, d), jnp.float32), 'phi_risk': jax.random.normal(ks[3], (B, S, S), jnp.float32), 'phi_prio': jax.random.normal(ks[4], (B, S, S), jnp.float32), 'phi_impl': jax.random.normal(ks[5], (B, S, S), jnp.float32), 'Wq': jax.random.normal(ks[6], (d, d), jnp.float32) / np.sqrt(d), 'bq': jax.random.normal(ks[7], (d,), jnp.float32) * 0.01, 'Wk': jax.random.normal(ks[8], (d, d), jnp.float32) / np.sqrt(d), 'bk': jax.random.normal(ks[9], (d,), jnp.float32) * 0.01, 'Wv': jax.random.normal(ks[10], (d, d), jnp.float32) / np.sqrt(d), 'bv': jax.random.normal(ks[11], (d,), jnp.float32) * 0.01, 'beta_risk': jnp.float32(0.1), 'beta_prio': jnp.float32(0.1), 'beta_impl': jnp.float32(0.1)}
        return inp
    _L2_xattn_all = _L2_xattn_setup()
    _L2_xattn_in = {k: v for k, v in _L2_xattn_all.items() if k in ('Wq', 'bq', 'Wk', 'bk', 'Wv', 'bv', 'beta_risk', 'beta_prio', 'beta_impl')}
    del _L2_xattn_all

    def _L2_ffn_setup():
        import jax, jax.numpy as jnp
        import numpy as np
        N_EXPERTS = 8
        TOP_K = 2
        D_MODEL = 256
        HIDDEN = 1024
        ROUTED_H = 256
        BATCH, SEQ = (2, 1024)
        key = jax.random.key(seed)
        ks = jax.random.split(key, 8)
        std = 0.02
        return {'x': jax.random.normal(ks[0], (BATCH, SEQ, D_MODEL), dtype=jnp.float32), 'w12': std * jax.random.normal(ks[1], (N_EXPERTS, 2 * ROUTED_H, D_MODEL), dtype=jnp.float32), 'w3': std * jax.random.normal(ks[2], (N_EXPERTS, D_MODEL, ROUTED_H), dtype=jnp.float32), 'shared_w1': std * jax.random.normal(ks[3], (HIDDEN, D_MODEL), dtype=jnp.float32), 'shared_w2': std * jax.random.normal(ks[4], (HIDDEN, D_MODEL), dtype=jnp.float32), 'shared_w3': std * jax.random.normal(ks[5], (D_MODEL, HIDDEN), dtype=jnp.float32), 'router_w': std * jax.random.normal(ks[6], (N_EXPERTS, D_MODEL), dtype=jnp.float32), 'expert_bias': jnp.zeros((N_EXPERTS,), dtype=jnp.float32)}
    _L2_ffn_all = _L2_ffn_setup()
    _L2_ffn_in = {k: v for k, v in _L2_ffn_all.items() if k in ('w12', 'w3', 'shared_w1', 'shared_w2', 'shared_w3', 'router_w', 'expert_bias')}
    del _L2_ffn_all

    def _L3_xattn_setup():
        import jax, jax.numpy as jnp
        import numpy as np
        B, S, H = (32, 577, 256)
        key = jax.random.key(seed)
        ks = jax.random.split(key, 12)
        w = lambda k, shape: jax.random.normal(k, shape, dtype=jnp.float32) * 0.02
        return {'hidden_states': jax.random.normal(ks[0], (B, S, H), dtype=jnp.float32), 'hidden_states_multi': jax.random.normal(ks[1], (B, S, H), dtype=jnp.float32), 'Wg': w(ks[2], (H, 2)), 'Wq': w(ks[3], (H, H)), 'Wk': w(ks[4], (H, H)), 'Wv': w(ks[5], (H, H)), 'Wo': w(ks[6], (H, H)), 'W1': w(ks[7], (H, H)), 'b1': jnp.zeros((H,), dtype=jnp.float32), 'W2': w(ks[8], (H, H)), 'b2': jnp.zeros((H,), dtype=jnp.float32)}
    _L3_xattn_all = _L3_xattn_setup()
    _L3_xattn_in = {k: v for k, v in _L3_xattn_all.items() if k in ('Wg', 'Wq', 'Wk', 'Wv', 'Wo', 'W1', 'b1', 'W2', 'b2')}
    del _L3_xattn_all

    def _L3_ffn_setup():
        import jax, jax.numpy as jnp
        import numpy as np
        INT8_MAX = 127.0

        def _absmax_scale(x, axes):
            amax = jnp.max(jnp.abs(x), axis=axes, keepdims=True)
            return jnp.maximum(amax, 1e-12) / INT8_MAX
        key = jax.random.key(seed)
        k1, k2 = jax.random.split(key)
        lhs = jax.random.normal(k1, (4, 2048, 256), dtype=jnp.float32)
        rhs = jax.random.normal(k2, (256, 256), dtype=jnp.float32)
        return {'lhs': lhs, 'rhs': rhs}
    _L3_ffn_all = _L3_ffn_setup()
    _L3_ffn_in = {k: v for k, v in _L3_ffn_all.items() if k in ('rhs',)}
    del _L3_ffn_all
    return {'x': x, 'ctx_1024': ctx_1024, 'fside_BxSxS2_0': fside_BxSxS2_0, 'mask_BxSxS2_if1': mask_BxSxS2_if1, 'L0_xattn_Wq': _L0_xattn_in['Wq'], 'L0_xattn_bq': _L0_xattn_in['bq'], 'L0_xattn_Wk': _L0_xattn_in['Wk'], 'L0_xattn_bk': _L0_xattn_in['bk'], 'L0_xattn_Wv': _L0_xattn_in['Wv'], 'L0_xattn_bv': _L0_xattn_in['bv'], 'L0_xattn_Wo': _L0_xattn_in['Wo'], 'L0_xattn_bo': _L0_xattn_in['bo'], 'L0_ffn_w_router': _L0_ffn_in['w_router'], 'L0_ffn_w_gating': _L0_ffn_in['w_gating'], 'L0_ffn_w_gate': _L0_ffn_in['w_gate'], 'L0_ffn_w_up': _L0_ffn_in['w_up'], 'L0_ffn_w_down': _L0_ffn_in['w_down'], 'L1_xattn_W': _L1_xattn_in['W'], 'L1_xattn_b': _L1_xattn_in['b'], 'L1_ffn_router_w': _L1_ffn_in['router_w'], 'L1_ffn_router_b': _L1_ffn_in['router_b'], 'L1_ffn_w1': _L1_ffn_in['w1'], 'L1_ffn_b1': _L1_ffn_in['b1'], 'L1_ffn_w2': _L1_ffn_in['w2'], 'L1_ffn_b2': _L1_ffn_in['b2'], 'L1_ffn_sw1': _L1_ffn_in['sw1'], 'L1_ffn_sb1': _L1_ffn_in['sb1'], 'L1_ffn_sw2': _L1_ffn_in['sw2'], 'L1_ffn_sb2': _L1_ffn_in['sb2'], 'L2_xattn_Wq': _L2_xattn_in['Wq'], 'L2_xattn_bq': _L2_xattn_in['bq'], 'L2_xattn_Wk': _L2_xattn_in['Wk'], 'L2_xattn_bk': _L2_xattn_in['bk'], 'L2_xattn_Wv': _L2_xattn_in['Wv'], 'L2_xattn_bv': _L2_xattn_in['bv'], 'L2_xattn_beta_risk': _L2_xattn_in['beta_risk'], 'L2_xattn_beta_prio': _L2_xattn_in['beta_prio'], 'L2_xattn_beta_impl': _L2_xattn_in['beta_impl'], 'L2_ffn_w12': _L2_ffn_in['w12'], 'L2_ffn_w3': _L2_ffn_in['w3'], 'L2_ffn_shared_w1': _L2_ffn_in['shared_w1'], 'L2_ffn_shared_w2': _L2_ffn_in['shared_w2'], 'L2_ffn_shared_w3': _L2_ffn_in['shared_w3'], 'L2_ffn_router_w': _L2_ffn_in['router_w'], 'L2_ffn_expert_bias': _L2_ffn_in['expert_bias'], 'L3_xattn_Wg': _L3_xattn_in['Wg'], 'L3_xattn_Wq': _L3_xattn_in['Wq'], 'L3_xattn_Wk': _L3_xattn_in['Wk'], 'L3_xattn_Wv': _L3_xattn_in['Wv'], 'L3_xattn_Wo': _L3_xattn_in['Wo'], 'L3_xattn_W1': _L3_xattn_in['W1'], 'L3_xattn_b1': _L3_xattn_in['b1'], 'L3_xattn_W2': _L3_xattn_in['W2'], 'L3_xattn_b2': _L3_xattn_in['b2'], 'L3_ffn_rhs': _L3_ffn_in['rhs']}

def reference(x, ctx_1024, fside_BxSxS2_0, mask_BxSxS2_if1, L0_xattn_Wq, L0_xattn_bq, L0_xattn_Wk, L0_xattn_bk, L0_xattn_Wv, L0_xattn_bv, L0_xattn_Wo, L0_xattn_bo, L0_ffn_w_router, L0_ffn_w_gating, L0_ffn_w_gate, L0_ffn_w_up, L0_ffn_w_down, L1_xattn_W, L1_xattn_b, L1_ffn_router_w, L1_ffn_router_b, L1_ffn_w1, L1_ffn_b1, L1_ffn_w2, L1_ffn_b2, L1_ffn_sw1, L1_ffn_sb1, L1_ffn_sw2, L1_ffn_sb2, L2_xattn_Wq, L2_xattn_bq, L2_xattn_Wk, L2_xattn_bk, L2_xattn_Wv, L2_xattn_bv, L2_xattn_beta_risk, L2_xattn_beta_prio, L2_xattn_beta_impl, L2_ffn_w12, L2_ffn_w3, L2_ffn_shared_w1, L2_ffn_shared_w2, L2_ffn_shared_w3, L2_ffn_router_w, L2_ffn_expert_bias, L3_xattn_Wg, L3_xattn_Wq, L3_xattn_Wk, L3_xattn_Wv, L3_xattn_Wo, L3_xattn_W1, L3_xattn_b1, L3_xattn_W2, L3_xattn_b2, L3_ffn_rhs):
    import jax
    import jax.numpy as jnp

    def _L0_xattn_ref(x, y, mask, Wq, bq, Wk, bk, Wv, bv, Wo, bo):
        import jax, jax.numpy as jnp
        import numpy as np
        EMB, HEADS = (256, 16)
        HEAD_DIM = EMB // HEADS

        def _linear(x, W, b):
            return jnp.einsum('bse,oe->bso', x, W) + b
        B, S, _ = x.shape
        q = _linear(x, Wq, bq).reshape(B, S, HEADS, HEAD_DIM).transpose(0, 2, 1, 3)
        k = _linear(y, Wk, bk).reshape(B, -1, HEADS, HEAD_DIM).transpose(0, 2, 1, 3)
        v = _linear(y, Wv, bv).reshape(B, -1, HEADS, HEAD_DIM).transpose(0, 2, 1, 3)
        score = jnp.einsum('bhqd,bhkd->bhqk', q, k) / jnp.sqrt(jnp.float32(HEAD_DIM))
        weights = jax.nn.softmax(score, axis=-1)
        attn = jnp.einsum('bhqk,bhkd->bhqd', weights, v)
        attn = attn.transpose(0, 2, 1, 3).reshape(B, S, EMB)
        return _linear(attn, Wo, bo)

    def _L0_ffn_ref(hidden_states, w_router, w_gating, w_gate, w_up, w_down):
        import jax, jax.numpy as jnp
        import numpy as np
        B, S, H = (2, 256, 256)
        E, F = (8, 1024)
        GATE_TEMP = 0.1
        x = hidden_states
        router_probs = jax.nn.softmax(jnp.einsum('bsh,he->bse', x, w_router), axis=-1)
        gate_weights = jax.nn.softmax(jnp.einsum('bsh,he->bse', x, w_gating) / GATE_TEMP, axis=-1)
        g = jnp.einsum('bsh,ehf->ebsf', x, w_gate)
        u = jnp.einsum('bsh,ehf->ebsf', x, w_up)
        h = jax.nn.silu(g) * u
        expert_out = jnp.einsum('ebsf,efh->ebsh', h, w_down)
        cw = router_probs * gate_weights
        cw = cw / (jnp.sum(cw, axis=-1, keepdims=True) + 1e-09)
        out = jnp.einsum('ebsh,bse->bsh', expert_out, cw)
        return out

    def _L1_xattn_ref(x1, x2, W, b):
        import jax, jax.numpy as jnp
        import numpy as np
        D1, D2, D3 = (256, 256, 256)
        d1 = x1.shape[-1]
        W1 = W[:, :d1]
        W2 = W[:, d1:]
        part1 = jnp.einsum('bld,ed->ble', x1, W1)
        part2 = jnp.einsum('bld,ed->be', x2, W2) / x2.shape[1]
        return part1 + part2[:, None, :] + b

    def _L1_ffn_ref(x, router_w, router_b, w1, b1, w2, b2, sw1, sb1, sw2, sb2):
        import jax, jax.numpy as jnp
        import numpy as np
        B, S, D = (4, 128, 256)
        E, K, H = (64, 8, 64)
        ES, HS = (2, 512)
        b_, s_, d_ = x.shape
        xf = x.reshape(-1, d_)
        probs = jax.nn.softmax(xf @ router_w + router_b, axis=-1)
        tw, ti = jax.lax.top_k(probs, K)
        tw = tw / jnp.sum(tw, axis=-1, keepdims=True)

        def body(acc, p):
            W1, B1, W2, B2, e = p
            h = jax.nn.silu(xf @ W1 + B1) @ W2 + B2
            cw = jnp.sum(jnp.where(ti == e, tw, 0.0), axis=-1)
            return (acc + cw[:, None] * h, None)
        routed, _ = jax.lax.scan(body, jnp.zeros_like(xf), (w1, b1, w2, b2, jnp.arange(w1.shape[0])))

        def shared_mlp(W1, B1, W2, B2):
            return jax.nn.silu(xf @ W1 + B1) @ W2 + B2
        shared = jnp.sum(jax.vmap(shared_mlp)(sw1, sb1, sw2, sb2), axis=0)
        return (routed + shared).reshape(b_, s_, d_)

    def _L2_xattn_ref(q_in, k_in, v_in, phi_risk, phi_prio, phi_impl, Wq, bq, Wk, bk, Wv, bv, beta_risk, beta_prio, beta_impl):
        import jax, jax.numpy as jnp
        import numpy as np
        D = 256
        d = q_in.shape[-1]
        scale = jnp.asarray(d, q_in.dtype) ** (-0.5)
        Q = q_in @ Wq.T + bq
        K = k_in @ Wk.T + bk
        V = v_in @ Wv.T + bv
        att = jnp.einsum('bsd,btd->bst', Q, K) * scale
        att = att + beta_risk * phi_risk + beta_prio * phi_prio - beta_impl * phi_impl
        w = jax.nn.softmax(att, axis=-1)
        return jnp.einsum('bst,btd->bsd', w, V)

    def _L2_ffn_ref(x, w12, w3, shared_w1, shared_w2, shared_w3, router_w, expert_bias):
        import jax, jax.numpy as jnp
        import numpy as np
        N_EXPERTS = 8
        TOP_K = 2
        D_MODEL = 256
        HIDDEN = 1024
        ROUTED_H = 256
        BATCH, SEQ = (2, 1024)
        b, s, d = x.shape
        xf = x.reshape(-1, d)
        shared = jax.nn.silu(xf @ shared_w1.T) * (xf @ shared_w2.T) @ shared_w3.T
        scores = jax.nn.sigmoid(xf @ router_w.T)
        _, top_idx = jax.lax.top_k(scores + expert_bias, TOP_K)
        mask = jax.nn.one_hot(top_idx, N_EXPERTS, dtype=xf.dtype).sum(axis=-2)
        gates = scores * mask
        h12 = jnp.einsum('td,ehd->teh', xf, w12)
        h1, h2 = jnp.split(h12, 2, axis=-1)
        h = jax.nn.silu(h1) * h2 * gates[:, :, None]
        routed = jnp.einsum('teh,edh->td', h, w3)
        return (shared + routed).reshape(b, s, d)

    def _L3_xattn_ref(hidden_states, hidden_states_multi, Wg, Wq, Wk, Wv, Wo, W1, b1, W2, b2):
        import jax, jax.numpy as jnp
        import numpy as np
        B, S, H = (32, 577, 256)
        x = hidden_states
        xm = hidden_states_multi
        logits = x[:, 0, :] @ Wg
        top_idx = jnp.argmax(logits, axis=-1)
        scale = 1.0 / jnp.sqrt(jnp.asarray(H, dtype=x.dtype))
        q = jnp.einsum('bsh,hd->bsd', x, Wq)
        k = jnp.einsum('bsh,hd->bsd', xm, Wk)
        v = jnp.einsum('bsh,hd->bsd', xm, Wv)
        attn = jax.nn.softmax(jnp.einsum('bqd,bkd->bqk', q, k) * scale, axis=-1)
        e0 = jnp.einsum('bqk,bkd->bqd', attn, v) @ Wo
        e1 = jax.nn.gelu(x @ W1 + b1, approximate=False) @ W2 + b2
        sel0 = (top_idx == 0)[:, None, None]
        final_hidden_states = jnp.where(sel0, e0, e1)
        return final_hidden_states

    def _L3_ffn_ref(lhs, rhs):
        import jax, jax.numpy as jnp
        import numpy as np
        INT8_MAX = 127.0

        def _absmax_scale(x, axes):
            amax = jnp.max(jnp.abs(x), axis=axes, keepdims=True)
            return jnp.maximum(amax, 1e-12) / INT8_MAX
        lhs_scale = _absmax_scale(lhs, (2,))
        rhs_scale = _absmax_scale(rhs, (0,))
        q_lhs = jnp.clip(jnp.round(lhs / lhs_scale), -INT8_MAX, INT8_MAX).astype(jnp.int8)
        q_rhs = jnp.clip(jnp.round(rhs / rhs_scale), -INT8_MAX, INT8_MAX).astype(jnp.int8)
        acc = jax.lax.dot_general(q_lhs, q_rhs, (((2,), (0,)), ((), ())), preferred_element_type=jnp.int32)
        return acc.astype(jnp.float32) * lhs_scale * rhs_scale
    x = x + _L0_xattn_ref(_layernorm(x, axis=-1), ctx_1024, mask_BxSxS2_if1, L0_xattn_Wq, L0_xattn_bq, L0_xattn_Wk, L0_xattn_bk, L0_xattn_Wv, L0_xattn_bv, L0_xattn_Wo, L0_xattn_bo)
    x = x + _L0_ffn_ref(_layernorm(x, axis=-1), L0_ffn_w_router, L0_ffn_w_gating, L0_ffn_w_gate, L0_ffn_w_up, L0_ffn_w_down)
    x = x + _L1_xattn_ref(_layernorm(x, axis=-1), ctx_1024, L1_xattn_W, L1_xattn_b)
    x = x + _L1_ffn_ref(_layernorm(x, axis=-1), L1_ffn_router_w, L1_ffn_router_b, L1_ffn_w1, L1_ffn_b1, L1_ffn_w2, L1_ffn_b2, L1_ffn_sw1, L1_ffn_sb1, L1_ffn_sw2, L1_ffn_sb2)
    x = x + _L2_xattn_ref(_layernorm(x, axis=-1), ctx_1024, ctx_1024, fside_BxSxS2_0, fside_BxSxS2_0, fside_BxSxS2_0, L2_xattn_Wq, L2_xattn_bq, L2_xattn_Wk, L2_xattn_bk, L2_xattn_Wv, L2_xattn_bv, L2_xattn_beta_risk, L2_xattn_beta_prio, L2_xattn_beta_impl)
    x = x + _L2_ffn_ref(_layernorm(x, axis=-1), L2_ffn_w12, L2_ffn_w3, L2_ffn_shared_w1, L2_ffn_shared_w2, L2_ffn_shared_w3, L2_ffn_router_w, L2_ffn_expert_bias)
    x = x + _L3_xattn_ref(_layernorm(x, axis=-1), ctx_1024, L3_xattn_Wg, L3_xattn_Wq, L3_xattn_Wk, L3_xattn_Wv, L3_xattn_Wo, L3_xattn_W1, L3_xattn_b1, L3_xattn_W2, L3_xattn_b2)
    x = x + _L3_ffn_ref(_layernorm(x, axis=-1), L3_ffn_rhs)
    return x

_drawn_inputs = setup_inputs


def setup_inputs(seed=0):
    import zlib

    import numpy as np

    out = dict(_drawn_inputs(seed))
    spreads = {'L1_ffn_router_b': (0.0, 0.413),
     'L1_ffn_b1': (0.0, 0.8),
     'L1_ffn_b2': (0.0, 0.3),
     'L1_ffn_sb1': (0.0, 0.311),
     'L1_ffn_sb2': (0.0, 0.1),
     'L2_ffn_expert_bias': (0.0, 0.62),
     'L3_xattn_b1': (0.0, 1.979),
     'L3_xattn_b2': (0.0, 0.334)}
    factors = {'fside_BxSxS2_0': 8.0,
     'L0_xattn_bq': 3.819,
     'L0_xattn_bk': 200.0,
     'L1_xattn_b': 3.344,
     'L1_ffn_w1': 5.925,
     'L1_ffn_w2': 5.718,
     'L2_xattn_bq': 8.0,
     'L2_xattn_bk': 200.0,
     'L2_xattn_bv': 6.013,
     'L2_ffn_w12': 4.902,
     'L2_ffn_w3': 4.863,
     'L2_ffn_router_w': 5.989,
     'L3_xattn_Wq': 23.044,
     'L3_xattn_Wk': 23.987,
     'L2_ffn_shared_w1': 4.119,
     'L2_ffn_shared_w2': 4.034,
     'L2_ffn_shared_w3': 4.046,
     'L3_xattn_W1': 3.395,
     'L3_xattn_Wv': 2.693,
     'L3_xattn_Wo': 2.693}
    for name, (base, spread) in spreads.items():
        noise = np.random.default_rng([zlib.crc32(name.encode()), seed]).standard_normal(out[name].shape)
        drawn = base * np.exp(spread * noise) if base else spread * noise
        out[name] = jnp.asarray(drawn.astype(out[name].dtype))
    for name, factor in factors.items():
        out[name] = (out[name] * factor).astype(out[name].dtype)
    return out
```

```python
from contextlib import ExitStack

import numpy as np

import concourse.bass as bass
from concourse import mybir

F32 = mybir.dt.float32
F32R = mybir.dt.float32r
BF16 = mybir.dt.bfloat16
ALU = mybir.AluOpType
ACT = mybir.ActivationFunctionType
X = mybir.AxisListType.X

P = 128
B, S, D = 2, 512, 256
SC = 1024
T = B * S
TC = T // P
CT = B * SC
KC = D // P
EPS = 1e-5

HEADS, HD = 16, 16
HG = 4
GROUPS = HEADS // HG
PART_PAIRS = [(0, 0), (0, 1), (1, 0), (1, 1), (0, 2), (2, 0)]
MAXROW = HD * len(PART_PAIRS)

E0, F0 = 8, 1024
FU = 256
U0 = E0 * F0 // FU
E1, H1, K1 = 64, 64, 8
ES1, HS1 = 2, 512
PAIRS1 = E1 // 2
U1 = PAIRS1 + ES1 * HS1 // P
E2, H2 = 8, 256
FS2 = 1024
U2 = E2 + FS2 // FU
NEG = -1.0e30
ROUND = 1.5 * 2.0 ** 23
INT8_MAX = 127.0

BQ0, BK0, BQ2, BK2, B1_3 = range(5)
ROWS = {}
_at = 0
for _name, _n in (("bv0", D), ("b_x1", D), ("rb1", E1), ("bv2", D), ("eb2", E2), ("b2_3", D)):
    ROWS[_name] = (_at, _at + _n)
    _at += _n
NROWS = _at


def f32(ap):
    return ap.bitcast(F32)


def mm3(pe, out, lhs, rhs, start, stop):
    pe.matmul(out, lhs[0], rhs[0], start=start, stop=False, skip_group_check=True)
    pe.matmul(out, lhs[0], rhs[1], start=False, stop=False, skip_group_check=True)
    return pe.matmul(out, lhs[1], rhs[0], start=False, stop=stop, skip_group_check=True)


class Chain:

    def __init__(self, eng, sem):
        self.eng, self.sem, self.n, self.loop = eng, sem, 0, 0

    def step(self, ins):
        ins.then_inc(self.sem, 1)
        self.n += 1

    def wait(self):
        self.eng.wait_ge(self.sem, self.loop + self.n)

    def link(self, ins):
        self.step(ins)
        self.wait()


class Shared:
    pass


def allocate_shared(nc, ctx, g):
    def sb(name, shape, dt=F32):
        return ctx.enter_context(nc.sbuf_tensor(f"{name}_sb", shape, dt))

    g.x = sb("x", [P, TC, D])
    g.ctxT_hi = sb("ctxT_hi", [P, KC, CT], F32R)
    g.ctxT_lo = sb("ctxT_lo", [P, KC, CT], F32R)
    g.ctx_sum = sb("ctx_sum", [P, KC, B])
    g.ident = sb("ident", [P, P])
    g.bias_cols = sb("bias_cols", [P, 5, KC])
    g.bias_rows = sb("bias_rows", [P, NROWS])
    g.rhs_q = sb("rhs_q", [P, KC, D], BF16)
    g.rhs_scale = sb("rhs_scale", [P, D])
    g.betas = sb("betas", [P, 3])
    g.phi_scale = sb("phi_scale", [P, 1])
    g.eps = sb("eps", [P, 1])


def row(g, name):
    a, b = ROWS[name]
    return g.bias_rows[:, a:b]


def load_phase(nc, g, d):
    with ExitStack() as ctx:
        ctxT = ctx.enter_context(nc.sbuf_tensor("ctxT_sb", [P, KC, CT], F32))
        rhsT = ctx.enter_context(nc.sbuf_tensor("rhsT_sb", [P, KC, D], F32))
        rhs_step = ctx.enter_context(nc.sbuf_tensor("rhs_step", [P, KC, 1], F32))
        rhs_inverse = ctx.enter_context(nc.sbuf_tensor("rhs_inverse", [P, KC, 1], F32))
        rhs_round = ctx.enter_context(nc.sbuf_tensor("rhs_round", [P, KC, D], F32))
        step_wide = ctx.enter_context(nc.sbuf_tensor("step_wide", [P, KC, P], F32))
        turned = ctx.enter_context(nc.psum_tensor("turned", [P, 2, KC * D], F32))
        ctx_loaded = [g.sem(f"ctx_loaded{k}") for k in range(KC)]
        x_loaded, rhs_loaded, consts_loaded = g.sem("x_loaded"), g.sem("rhs_loaded"), g.sem("consts_loaded")
        ctx_hi_done, rhs_rounded, rhs_turned = g.sem("ctx_hi_done"), g.sem("rhs_rounded"), g.sem("rhs_turned")
        dve_steps = g.sem("load_dve_steps")
        with nc.Block() as block:
            @block.sync
            def _(sp):
                sp.dma_start(g.x[:, :, :], d["x"]).then_inc(x_loaded, 16)
                for k in range(KC):
                    sp.dma_start(ctxT[:, k, :], d["ctxT"][:, k, :]).then_inc(ctx_loaded[k], 16)
                sp.dma_start(rhsT[:, :, :], d["rhsT"]).then_inc(rhs_loaded, 16)
                sp.dma_start(g.ident[:, :], d["ident"]).then_inc(consts_loaded, 16)
                sp.dma_start(g.bias_cols[:, :, :], d["bias_cols"]).then_inc(consts_loaded, 16)
                sp.dma_start(g.bias_rows[:, :], d["bias_rows"]).then_inc(consts_loaded, 16)
                sp.dma_start(g.betas[:, :], d["betas"]).then_inc(consts_loaded, 16)
                sp.wait_ge(x_loaded, 16)

            @block.scalar
            def _(act):
                for k in range(KC):
                    act.wait_ge(ctx_loaded[k], 16)
                    act.activation(g.ctxT_hi[:, k, :], ctxT[:, k, :], ACT.Copy).then_inc(ctx_hi_done, 1)

            @block.gpsimd
            def _(pool):
                pool.memset(g.eps[:, :], EPS)

            @block.vector
            def _(dve):
                own = Chain(dve, dve_steps)
                dve.wait_ge(rhs_loaded, 16)
                own.link(dve.tensor_reduce(rhs_step[:, :, 0], rhsT[:, :, :], X, ALU.max, apply_absolute_value=True))
                own.link(dve.tensor_scalar(rhs_step[:, :, 0], rhs_step[:, :, 0], 1e-12, 1.0 / INT8_MAX, ALU.max, ALU.mult))
                own.link(dve.reciprocal(rhs_inverse[:, :, 0], rhs_step[:, :, 0]))
                for k in range(KC):
                    own.link(dve.tensor_scalar(rhs_round[:, k, :], rhsT[:, k, :], rhs_inverse[:, k, :], ROUND,
                                               ALU.mult, ALU.add))
                own.link(dve.tensor_scalar(rhs_round[:, :, :], rhs_round[:, :, :], ROUND, INT8_MAX,
                                           ALU.subtract, ALU.min))
                dve.tensor_scalar(rhs_round[:, :, :], rhs_round[:, :, :], -INT8_MAX, None,
                                  ALU.max).then_inc(rhs_rounded, 1)
                for k in range(KC):
                    dve.tensor_copy(step_wide[:, k, :], rhs_step[:, k, :].to_broadcast([P, P])).then_inc(rhs_rounded, 1)
                for k in range(KC):
                    dve.wait_ge(ctx_hi_done, k + 1)
                    dve.tensor_tensor(g.ctxT_lo[:, k, :], ctxT[:, k, :], f32(g.ctxT_hi[:, k, :]), ALU.subtract)
                    dve.tensor_reduce(g.ctx_sum[:, k, :], ctxT[:, k, :].rearrange("p (b s) -> p b s", b=B), X, ALU.add)
                dve.wait_ge(consts_loaded, 64)
                own.link(dve.tensor_tensor(g.phi_scale[:, :], g.betas[:, 0:1], g.betas[:, 1:2], ALU.add))
                own.link(dve.tensor_tensor(g.phi_scale[:, :], g.phi_scale[:, :], g.betas[:, 2:3], ALU.subtract))
                own.link(dve.tensor_scalar(g.phi_scale[:, :], g.phi_scale[:, :], float(D) ** 0.5, None, ALU.mult))
                dve.wait_ge(rhs_turned, 1)
                dve.tensor_copy(g.rhs_q[:, :, :], turned[:, 0, :].rearrange("p (k n) -> p k n", k=KC))
                dve.tensor_copy(g.rhs_scale[:, :], turned[:, 1, 0:D])

            @block.tensor
            def _(pe):
                pe.wait_ge(consts_loaded, 64)
                pe.wait_ge(rhs_rounded, 1 + KC)
                for n in range(KC):
                    for k in range(KC):
                        pe.transpose(turned[:, 0, k * D + n * P:k * D + (n + 1) * P],
                                     rhs_round[:, n, k * P:(k + 1) * P], g.ident[:, :])
                    last = pe.transpose(turned[:, 1, n * P:(n + 1) * P], step_wide[:, n, :], g.ident[:, :])
                last.then_inc(rhs_turned, 1)


def allocate_turned(nc, ctx, g, tag):
    g.xnT_hi = ctx.enter_context(nc.sbuf_tensor(f"xnT_hi_{tag}", [P, KC, T], F32R))
    g.xnT_lo = ctx.enter_context(nc.sbuf_tensor(f"xnT_lo_{tag}", [P, KC, T], F32R))


def deviation(act, g, mv, rstd, moments_done, deviation_done):
    act.wait_ge(moments_done, TC)
    act.activation(rstd[:, :], mv[:, :, 1], ACT.Sqrt, bias=g.eps[:, 0:1]).then_inc(deviation_done, 1)


def normalise_steps(dve, own, g, stats, mv, rstd, xn, moments_done, deviation_done, normal_done):
    for c in range(TC):
        own.step(dve.bn_stats(stats[:, c, :], g.x[:, c, :]))
    own.wait()
    for c in range(TC):
        dve.bn_aggr(mv[:, c, :], stats[:, c, :]).then_inc(moments_done, 1)
    dve.wait_ge(moments_done, TC)
    dve.wait_ge(deviation_done, 1)
    own.link(dve.reciprocal(rstd[:, :], rstd[:, :]))
    for c in range(TC):
        dve.tensor_scalar(xn[:, c, :], g.x[:, c, :], mv[:, c, 0:1], rstd[:, c:c + 1],
                          ALU.subtract, ALU.mult).then_inc(normal_done, 1)


def normaliser(nc, ctx, g, tag, turned):
    def sb(name, shape, dt=F32):
        return ctx.enter_context(nc.sbuf_tensor(f"{name}_{tag}", shape, dt))

    xn = sb("xn", [P, TC, D])
    stats, mv, rstd = sb("stats", [P, TC, 6]), sb("mv", [P, TC, 2]), sb("rstd", [P, TC])
    own_steps, normal_done = g.sem(f"norm_steps_{tag}"), g.sem(f"normal_done_{tag}")
    turned_done = g.sem(f"turned_done_{tag}")
    moments_done, deviation_done = g.sem(f"moments_done_{tag}"), g.sem(f"deviation_done_{tag}")
    n = Shared()
    n.hi_done, n.lo_done = g.sem(f"norm_hi_done_{tag}"), g.sem(f"norm_lo_done_{tag}")

    def on_vector(dve):
        normalise_steps(dve, Chain(dve, own_steps), g, stats, mv, rstd, xn, moments_done, deviation_done, normal_done)
        for h in range(2):
            for k in range(KC):
                dve.wait_ge(n.hi_done, h * KC + k + 1)
                dve.tensor_tensor(g.xnT_lo[:, k, h * 512:(h + 1) * 512], turned[:, h, k, :],
                                  f32(g.xnT_hi[:, k, h * 512:(h + 1) * 512]), ALU.subtract).then_inc(n.lo_done, 1)

    def on_tensor(pe):
        for c in range(TC):
            pe.wait_ge(normal_done, c + 1)
            for k in range(KC):
                last = pe.transpose(turned[:, c // 4, k, (c % 4) * P:(c % 4 + 1) * P],
                                    xn[:, c, k * P:(k + 1) * P], g.ident[:, :])
            if c % 4 == 3:
                last.then_inc(turned_done, 1)

    def on_scalar(act):
        deviation(act, g, mv, rstd, moments_done, deviation_done)
        for h in range(2):
            act.wait_ge(turned_done, h + 1)
            for k in range(KC):
                act.activation(g.xnT_hi[:, k, h * 512:(h + 1) * 512], turned[:, h, k, :],
                               ACT.Copy).then_inc(n.hi_done, 1)

    def wait_half(pe, h):
        pe.wait_ge(n.hi_done, KC * (h + 1))
        pe.wait_ge(n.lo_done, KC * (h + 1))

    n.on_vector, n.on_tensor, n.on_scalar, n.wait_half = on_vector, on_tensor, on_scalar, wait_half
    return n


def normalise_phase(nc, g, tag):
    with ExitStack() as ctx:
        turned = ctx.enter_context(nc.psum_tensor(f"turned_{tag}", [P, 2, KC, 4 * P], F32))
        norm = normaliser(nc, ctx, g, tag, turned)
        with nc.Block() as block:
            block.vector(norm.on_vector)
            block.tensor(norm.on_tensor)
            block.scalar(norm.on_scalar)


def split_weights(nc, g, ctx, tag, name, shape):
    def sb(n, dt):
        return ctx.enter_context(nc.sbuf_tensor(f"{name}_{n}_{tag}", shape, dt))

    return sb("raw", F32), sb("hi", F32R), sb("lo", F32R)


def l0_project_phase(nc, g, d):
    with ExitStack() as ctx:
        def sb(name, shape, dt=F32):
            return ctx.enter_context(nc.sbuf_tensor(name, shape, dt))

        w_raw, w_hi, w_lo = split_weights(nc, g, ctx, "p0", "wqkv0", [P, 3, KC, D])
        exact, rest = sb("kq_exact", [P, 3, 512]), sb("kq_rest", [P, 3, 512])
        parts = sb("kq_parts", [P, 3, 3, 512], BF16)
        acc = ctx.enter_context(nc.psum_tensor("acc_p0", [P, 8, 512], F32))
        w_loaded, w_hi_done, w_lo_done = g.sem("w0_loaded"), g.sem("w0_hi_done"), g.sem("w0_lo_done")
        tile_done, exact_done, part1_done = g.sem("kq_tile_done"), g.sem("kq_exact_done"), g.sem("kq_part1_done")
        rest_done, part2_done, part3_done = g.sem("kq_rest_done"), g.sem("kq_part2_done"), g.sem("kq_part3_done")
        parts_stored = [g.sem(f"kq_parts_stored{i}") for i in range(3)]
        tiles = [(1, fc, b, h) for b in range(B) for h in range(2) for fc in range(KC)]
        tiles += [(0, fc, b, 0) for b in range(B) for fc in range(KC)]
        NT = len(tiles)
        NV = CT // P // 2
        with nc.Block() as block:
            @block.sync
            def _(sp):
                sp.dma_start(w_raw[:, :, :, :], d["wqkv0"]).then_inc(w_loaded, 16)
                for n, (which, fc, b, h) in enumerate(tiles):
                    dram = g.q_parts if which == 0 else g.k_parts
                    sp.wait_ge(part3_done, n + 1)
                    sp.dma_start(dram[:, b * D + fc * P:b * D + (fc + 1) * P, h * 512:(h + 1) * 512]
                                 .rearrange("a p s -> p a s"), parts[:, n % 3, :, :]).then_inc(parts_stored[n % 3], 16)
                for i in range(3):
                    sp.wait_ge(parts_stored[i], 16 * ((NT - i + 2) // 3))

            @block.tensor
            def _(pe):
                pe.wait_ge(w_hi_done, 1)
                pe.wait_ge(w_lo_done, 1)
                for n, (which, fc, b, h) in enumerate(tiles):
                    if n >= 8:
                        pe.wait_ge(exact_done, n - 7)
                    for k in range(KC):
                        if which == 0:
                            rhs = (g.xnT_hi[:, k, b * S:(b + 1) * S], g.xnT_lo[:, k, b * S:(b + 1) * S])
                        else:
                            a = b * SC + h * 512
                            rhs = (g.ctxT_hi[:, k, a:a + 512], g.ctxT_lo[:, k, a:a + 512])
                        cols = slice(fc * P, (fc + 1) * P)
                        last = mm3(pe, acc[:, n % 8, :], (w_hi[:, which, k, cols], w_lo[:, which, k, cols]),
                                   rhs, k == 0, k == KC - 1)
                    last.then_inc(tile_done, 1)
                for m in range(NV):
                    n = NT + m
                    if n - 8 < NT:
                        pe.wait_ge(exact_done, n - 7)
                    else:
                        pe.wait_ge(g.v0_done, n - 7 - NT)
                    for j in range(2):
                        t = slice((2 * m + j) * P, (2 * m + j + 1) * P)
                        for k in range(KC):
                            last = mm3(pe, acc[:, n % 8, j * D:(j + 1) * D], (g.ctxT_hi[:, k, t], g.ctxT_lo[:, k, t]),
                                       (w_hi[:, 2, k, :], w_lo[:, 2, k, :]), j == 0 and k == 0, k == KC - 1)
                    last.then_inc(tile_done, 1)

            @block.scalar
            def _(act):
                act.wait_ge(w_loaded, 16)
                act.activation(w_hi[:, :, :, :], w_raw[:, :, :, :], ACT.Copy).then_inc(w_hi_done, 1)
                for n in range(NT + 1):
                    if n < NT:
                        which, fc = tiles[n][:2]
                        bias = g.bias_cols[:, BQ0 if which == 0 else BK0, fc:fc + 1]
                        act.wait_ge(tile_done, n + 1)
                        if n >= 3:
                            act.wait_ge(rest_done, n - 2)
                            act.wait_ge(parts_stored[n % 3], 16 * (n // 3))
                        act.activation(exact[:, n % 3, :], acc[:, n % 8, :], ACT.Identity, bias=bias).then_inc(exact_done, 1)
                        act.wait_ge(exact_done, n + 1)
                        act.activation(parts[:, n % 3, 0, :], exact[:, n % 3, :], ACT.Copy).then_inc(part1_done, 1)
                    if n >= 1:
                        m = (n - 1) % 3
                        act.wait_ge(rest_done, n)
                        act.activation(parts[:, m, 1, :], rest[:, m, :], ACT.Copy).then_inc(part2_done, 1)

            @block.vector
            def _(dve):
                dve.wait_ge(w_hi_done, 1)
                dve.tensor_tensor(w_lo[:, :, :, :], w_raw[:, :, :, :], f32(w_hi[:, :, :, :]), ALU.subtract).then_inc(w_lo_done, 1)
                for n in range(NT + 1):
                    if n < NT:
                        m = n % 3
                        dve.wait_ge(part1_done, n + 1)
                        dve.tensor_tensor(rest[:, m, :], exact[:, m, :], parts[:, m, 0, :], ALU.subtract).then_inc(rest_done, 1)
                    if n >= 1:
                        m = (n - 1) % 3
                        dve.wait_ge(part2_done, n)
                        dve.tensor_tensor(parts[:, m, 2, :], rest[:, m, :], parts[:, m, 1, :], ALU.subtract).then_inc(part3_done, 1)
                bv = row(g, "bv0").rearrange("p (g e) -> p g e", g=GROUPS)
                for m in range(NV):
                    dve.wait_ge(tile_done, NT + m + 1)
                    for j in range(2):
                        b, t = divmod(2 * m + j, SC // P)
                        last = dve.tensor_tensor(g.v0[:, b, :, t, :],
                                                 acc[:, (NT + m) % 8, j * D:(j + 1) * D].rearrange("p (g e) -> p g e", g=GROUPS),
                                                 bv, ALU.add)
                    last.then_inc(g.v0_done, 1)


def l0_attention_phase(nc, g, d):
    NR = B * GROUPS
    KT = SC // P
    AU = 4 * HG * 2
    BU = 2 * KT
    SCALE = float(HD) ** -0.5
    T1_AT, T0_AT = 2, 9
    with ExitStack() as ctx:
        def sb(name, shape, dt=F32):
            return ctx.enter_context(nc.sbuf_tensor(name, shape, dt))

        k_stack = [sb(f"k_stack{i}", [P, HG, SC], BF16) for i in range(3)]
        q_stack = [sb(f"q_stack{i}", [P, HG, S], BF16) for i in range(3)]
        v_aug = [sb(f"v_aug{i}", [P, KT, HG, 32]) for i in range(3)]
        probs = [sb(f"probs0_{i}", [P, HG, 256]) for i in range(2)]
        maxima = [sb(f"maxima{h}", [P, 8, 2]) for h in range(2)]
        row_max = [sb(f"row_max{h}", [P, 8]) for h in range(2)]
        neg_parts = [sb(f"neg_parts{h}", [8, 3, P], BF16) for h in range(2)]
        neg_rest = [sb(f"neg_rest{h}", [8, P]) for h in range(2)]
        a_scores = ctx.enter_context(nc.psum_tensor("a_scores", [P, 2, 512], F32))
        b_scores = ctx.enter_context(nc.psum_tensor("b_scores", [P, 2, HG, 256], F32))
        weighted = ctx.enter_context(nc.psum_tensor("weighted", [P, 512], F32))
        max_turned = ctx.enter_context(nc.psum_tensor("max_turned", [P, 512], F32))
        stacks_loaded = [g.sem(f"stacks_loaded{i}") for i in range(3)]
        ones_set, v_aug_set, v_aug_done = g.sem("ones_set"), g.sem("v_aug_set"), g.sem("v_aug_done")
        a_ready, a_read, b_ready = g.sem("a_ready"), g.sem("a_read"), g.sem("b_ready")
        exp_done = g.sem("exp_done")
        av_done = g.sem("av_done")
        avs_done = g.sem("avs_done")
        row_max_done, turn_done = g.sem("row_max_done"), g.sem("turn_done")
        neg_done = g.sem("neg_done")
        max_loaded = [g.sem(f"max_loaded{h}") for h in range(2)]
        dve_steps = g.sem("a0_dve_steps")
        LOADS = 2 * len(PART_PAIRS) * 16
        MAX_LOADS = 6 * 16
        o = g.out0

        with nc.Block() as block:
            @block.sync
            def _(sp):
                def load_stacks(r):
                    if r >= 3:
                        sp.wait_ge(avs_done, r - 1)
                    for t, (qp, kp) in enumerate(PART_PAIRS):
                        rows = slice(HD * t, HD * (t + 1))
                        feat = slice(r * HG * HD, (r + 1) * HG * HD)
                        sp.dma_start(k_stack[r % 3][rows, :, :], g.k_parts[kp, feat, :].rearrange("(h e) s -> e h s", h=HG)).then_inc(stacks_loaded[r % 3], 16)
                        sp.dma_start(q_stack[r % 3][rows, :, :], g.q_parts[qp, feat, :].rearrange("(h e) s -> e h s", h=HG)).then_inc(stacks_loaded[r % 3], 16)

                def load_max(r, h):
                    sp.wait_ge(neg_done, 2 * r + h + 1)
                    for part in range(3):
                        for qc in range(2):
                            at = h * 256 + qc * P
                            sp.dma_start(q_stack[r % 3][MAXROW + part:MAXROW + part + 1, :, at:at + P],
                                         neg_parts[h][4 * qc:4 * qc + 4, part, :]).then_inc(max_loaded[h], 16)

                for r in range(3):
                    load_stacks(r)
                sp.dma_start(o.w_raw[:, :, :], d["wo0"]).then_inc(o.loaded, 16)
                sp.dma_start(o.spread[:, :], d["spread"]).then_inc(o.loaded, 16)
                for r in range(NR):
                    load_max(r, 0)
                    if r >= 2:
                        sp.wait_ge(avs_done, r)
                        gather_sums(sp, g, r - 2)
                    load_max(r, 1)
                    if r >= 1 and r + 2 < NR:
                        load_stacks(r + 2)
                sp.wait_ge(avs_done, NR)
                gather_sums(sp, g, NR - 2)
                sp.wait_ge(o.inverse_done, 1)
                for r in range(NR - 1):
                    return_inverses(sp, g, r)

            @block.gpsimd
            def _(pool):
                for i in range(3):
                    pool.memset(k_stack[i][MAXROW:MAXROW + 3, :, :], 1.0).then_inc(ones_set, 1)
                    pool.wait_ge(ones_set, i + 1)
                for i in range(3):
                    pool.memset(v_aug[i][:, :, :, :], 0.0).then_inc(v_aug_set, 1)
                    pool.wait_ge(v_aug_set, 2 * i + 1)
                    pool.memset(v_aug[i][:, :, :, HD:HD + 1], 1.0).then_inc(v_aug_set, 1)
                    pool.wait_ge(v_aug_set, 2 * i + 2)
                for r in range(NR):
                    if r >= 1:
                        pool.wait_ge(v_aug_done, r)
                    if r >= 3:
                        pool.wait_ge(avs_done, r - 1)
                    pool.tensor_copy(v_aug[r % 3][:, :, :, 0:HD],
                                     g.v0[:, r // GROUPS, r % GROUPS, :, :].rearrange("p t (h e) -> p t h e", h=HG)).then_inc(v_aug_done, 1)
                    if r == 2:
                        pool.wait_ge(v_aug_done, r + 1)
                        split_on_pool(pool, o.w_raw, o.w_hi, o.w_lo, o.loaded, o.split_done, 32)

            @block.tensor
            def _(pe):
                def turn_max(r, half):
                    pe.wait_ge(row_max_done, 2 * r + half + 1)
                    pe.transpose(max_turned[0:8, half * P:(half + 1) * P], row_max[half][:, :], g.ident[:, :]).then_inc(turn_done, 1)

                def b_unit(r, buf, u):
                    half, kt = divmod(u, KT)
                    if kt == 0:
                        pe.wait_ge(max_loaded[half], MAX_LOADS * (r + 1))
                    pe.wait_ge(exp_done, BU * r + u + 1)
                    for h in range(HG):
                        last = pe.matmul(b_scores[:, u % 2, h, :], k_stack[buf][0:MAXROW + 3, h, kt * P:(kt + 1) * P],
                                         q_stack[buf][0:MAXROW + 3, h, half * 256:(half + 1) * 256],
                                         start=True, stop=True, skip_group_check=True)
                    last.then_inc(b_ready, 1)

                def av_unit(r, buf, u):
                    half, kt = divmod(u, KT)
                    if u == 0:
                        pe.wait_ge(avs_done, r + 1)
                        pe.wait_ge(v_aug_done, r + 1)
                    pe.wait_ge(exp_done, BU * r + u + 3)
                    for h in range(HG):
                        last = pe.matmul(weighted[32 * h:32 * h + 32, half * 256:(half + 1) * 256],
                                         v_aug[buf][:, kt, h, :], probs[u % 2][:, h, :],
                                         start=kt == 0, stop=kt == KT - 1, skip_group_check=True)
                    last.then_inc(av_done, 1)

                def period(r, buf, uses, last):
                    nxt = (buf + 1) % 3
                    for u in range(BU):
                        if not last:
                            if u == 0:
                                pe.wait_ge(stacks_loaded[nxt], LOADS * uses)
                            for k in (2 * u, 2 * u + 1):
                                a_tile(r + 1, nxt, k)
                        b_unit(r, buf, u)
                        if u >= 1:
                            av_unit(r, buf, u - 1)
                        if u == T1_AT:
                            turn_max(r, 1)
                        if u == T0_AT and not last:
                            turn_max(r + 1, 0)
                    av_unit(r, buf, BU - 1)

                def a_tile(r, buf, k, first=False):
                    half, qc, h, kh = k // 16, k // 8 % 2, k // 2 % 4, k % 2
                    if not (first and k < 2):
                        pe.wait_ge(a_read, AU * r + k - 1)
                    at = half * 256 + qc * P
                    pe.matmul(a_scores[:, k % 2, :], q_stack[buf][0:MAXROW, h, at:at + P],
                              k_stack[buf][0:MAXROW, h, kh * 512:(kh + 1) * 512], start=True, stop=True).then_inc(a_ready, 1)

                pe.sem_inc(exp_done, 2)
                pe.sem_inc(av_done, 2)
                pe.sem_inc(avs_done, 1)
                pe.wait_ge(ones_set, 3)
                pe.wait_ge(stacks_loaded[0], LOADS)
                for k in range(AU):
                    a_tile(0, 0, k, first=True)
                    if k == 19:
                        turn_max(0, 0)
                with pe.Fori(0, 2) as j:
                    for k in range(3):
                        period(3 * j + k, k, j + 1 if k < 2 else j + 2, False)
                period(6, 0, 3, False)
                period(7, 1, 0, True)

            @block.scalar
            def _(act):
                def period(r):
                    for u in range(BU):
                        act.wait_ge(b_ready, BU * r + u + 1)
                        act.wait_ge(av_done, BU * r + u + 1)
                        act.activation(probs[u % 2][:, :, :], b_scores[:, u % 2, :, :], ACT.Exp, scale=SCALE).then_inc(exp_done, 1)
                    act.wait_ge(av_done, BU * r + BU + 2)
                    act.activation(g.avs[:, r, :], weighted[:, :], ACT.Copy).then_inc(avs_done, 1)

                with act.Fori(0, NR) as r:
                    period(r)

            @block.vector
            def _(dve):
                own = Chain(dve, dve_steps)

                def tile_max(r, k):
                    dve.wait_ge(a_ready, AU * r + k + 1)
                    i = k % 16
                    dve.tensor_reduce(maxima[k // 16][:, i // 2, i % 2:i % 2 + 1], a_scores[:, k % 2, :], X, ALU.max).then_inc(a_read, 1)
                    if i == 15:
                        dve.wait_ge(a_read, AU * r + k + 1)
                        dve.tensor_reduce(row_max[k // 16][:, :], maxima[k // 16][:, :, :], X, ALU.max).then_inc(row_max_done, 1)

                def negate(r, half):
                    turned = max_turned[0:8, half * P:(half + 1) * P]
                    dve.wait_ge(turn_done, 2 * r + half + 1)
                    own.link(dve.tensor_scalar(neg_parts[half][:, 0, :], turned, -1.0, None, ALU.mult))
                    own.link(dve.scalar_tensor_tensor(neg_rest[half][:, :], turned, -1.0, neg_parts[half][:, 0, :], ALU.mult, ALU.subtract))
                    own.link(dve.tensor_copy(neg_parts[half][:, 1, :], neg_rest[half][:, :]))
                    dve.tensor_tensor(neg_parts[half][:, 2, :], neg_rest[half][:, :], neg_parts[half][:, 1, :], ALU.subtract).then_inc(neg_done, 1)

                def maxes(r, in_period):
                    for k in range(AU):
                        tile_max(r, k)
                        if k == 2 * T1_AT + 1 and in_period:
                            negate(r - 1, 1)
                        if k == 2 * T0_AT + 1:
                            negate(r, 0)

                maxes(0, False)
                n0 = own.n
                with dve.Fori(0, NR - 1) as r:
                    own.loop = 6 * r
                    maxes(r + 1, True)
                assert own.n == n0 + 6
                own.loop = 6 * (NR - 2)
                negate(NR - 1, 1)
                dve.wait_ge(o.sums_gathered, 16 * HG * (NR - 1))
                dve.reciprocal(o.sums[:, 0:NR - 1, :], o.sums[:, 0:NR - 1, :]).then_inc(o.inverse_done, 1)


def l0_output_buffers(nc, ctx, g):
    def sb(name, shape, dt=F32):
        return ctx.enter_context(nc.sbuf_tensor(name, shape, dt))

    NR = B * GROUPS
    o = g.out0 = Shared()
    o.w_raw, o.w_hi, o.w_lo = split_weights(nc, g, ctx, "o0", "wo0", [P, GROUPS, D])
    o.spread = sb("spread_sb", [HG, P])
    o.sums = sb("sums0", [P, NR, S // 32])
    o.inverse_rows = sb("inverse_rows", [HG, NR, S])
    o.loaded, o.split_done = g.sem("o0_loaded"), g.sem("o0_split_done")
    o.sums_gathered, o.inverse_done = g.sem("sums_gathered"), g.sem("inverse0_done")
    o.inverses_returned = [g.sem(f"inverses_returned{i}") for i in range(2)]


def gather_sums(sp, g, r):
    for h in range(HG):
        sp.dma_start(g.out0.sums[32 * h:32 * h + 32, r, :],
                     g.avs[32 * h + HD:32 * h + HD + 1, r, :]).then_inc(g.out0.sums_gathered, 16)


def return_inverses(sp, g, r):
    last = r == B * GROUPS - 1
    sp.dma_start(g.out0.inverse_rows[:, r, :], g.out0.sums[:, r, :]).then_inc(g.out0.inverses_returned[last], 16)


def l0_output_phase(nc, g, d):
    NR = B * GROUPS
    o = g.out0
    with ExitStack() as ctx:
        def sb(name, shape, dt=F32):
            return ctx.enter_context(nc.sbuf_tensor(name, shape, dt))

        attn = sb("attn0", [P, 2, 512])
        attn_hi, attn_lo = sb("attn0_hi", [P, NR, 512], F32R), sb("attn0_lo", [P, NR, 512], F32R)
        inverse = ctx.enter_context(nc.psum_tensor("inverse0", [P, 4, 512], F32))
        out = ctx.enter_context(nc.psum_tensor("out0", [P, TC // 2, 2, D], F32))
        spread_done, attn_done = g.sem("spread0_done"), g.sem("attn0_done")
        hi_done, lo_done, out_done = g.sem("attn0_hi_done"), g.sem("attn0_lo_done"), g.sem("out0_done")
        with nc.Block() as block:
            @block.sync
            def _(sp):
                gather_sums(sp, g, NR - 1)
                sp.wait_ge(o.inverse_done, 2)
                return_inverses(sp, g, NR - 1)

            @block.scalar
            def _(act):
                for r in range(NR):
                    act.wait_ge(attn_done, r + 1)
                    act.activation(attn_hi[:, r, :], attn[:, r % 2, :], ACT.Copy).then_inc(hi_done, 1)

            @block.tensor
            def _(pe):
                def spread_inverse(r):
                    if r >= 4:
                        pe.wait_ge(attn_done, r - 3)
                    pe.matmul(inverse[:, r % 4, :], o.spread[:, :], o.inverse_rows[:, r, :], start=True, stop=True).then_inc(spread_done, 1)

                def project(b):
                    for m in range(2):
                        for j in range(2):
                            q = 2 * m + j
                            for gr in range(GROUPS):
                                r = b * GROUPS + gr
                                pe.wait_ge(hi_done, r + 1)
                                pe.wait_ge(lo_done, r + 1)
                                lhs = (attn_hi[:, r, q * P:(q + 1) * P], attn_lo[:, r, q * P:(q + 1) * P])
                                last = mm3(pe, out[:, 2 * b + m, j, :], lhs, (o.w_hi[:, gr, :], o.w_lo[:, gr, :]),
                                           j == 0 and gr == 0, gr == GROUPS - 1)
                        last.then_inc(out_done, 1)

                pe.wait_ge(o.split_done, 2)
                pe.wait_ge(o.inverses_returned[0], 16 * (NR - 1))
                for r in range(NR - 1):
                    spread_inverse(r)
                project(0)
                pe.wait_ge(o.inverses_returned[1], 16)
                spread_inverse(NR - 1)
                project(1)

            @block.vector
            def _(dve):
                def low(r):
                    dve.wait_ge(hi_done, r + 1)
                    dve.tensor_tensor(attn_lo[:, r, :], attn[:, r % 2, :], f32(attn_hi[:, r, :]), ALU.subtract).then_inc(lo_done, 1)

                for r in range(NR):
                    dve.wait_ge(spread_done, r + 1)
                    if r >= 2:
                        dve.wait_ge(hi_done, r - 1)
                        dve.wait_ge(lo_done, r - 1)
                    dve.tensor_tensor(attn[:, r % 2, :], g.avs[:, r, :], inverse[:, r % 4, :], ALU.mult).then_inc(attn_done, 1)
                    if r >= 1:
                        low(r - 1)
                    if r == 2:
                        dve.wait_ge(o.sums_gathered, 16 * HG * NR)
                        dve.reciprocal(o.sums[:, NR - 1, :], o.sums[:, NR - 1, :]).then_inc(o.inverse_done, 1)
                low(NR - 1)
                for m in range(TC // 2):
                    dve.wait_ge(out_done, m + 1)
                    dve.tensor_tensor(g.x[:, 2 * m:2 * m + 2, :], g.x[:, 2 * m:2 * m + 2, :], out[:, m, :, :], ALU.add)


def split_on_pool(pool, raw, hi, lo, loaded, split_done, load_count=16):
    pool.wait_ge(loaded, load_count)
    pool.tensor_copy(hi[:, :, :], raw[:, :, :]).then_inc(split_done, 1)
    pool.wait_ge(split_done, 1)
    pool.tensor_tensor(lo[:, :, :], raw[:, :, :], f32(hi[:, :, :]), ALU.subtract).then_inc(split_done, 1)
    pool.wait_ge(split_done, 2)


def router_logits(pe, logits, n, xT, w, k_first=True):
    for c in range(TC):
        t = slice(c * P, (c + 1) * P)
        for k in range(KC):
            last = mm3(pe, logits[:, c, 0:n], (xT[0][:, k, t], xT[1][:, k, t]),
                       (w[0][:, k, :], w[1][:, k, :]), c == 0 and k == 0, k == KC - 1)
    return last


def l0_router(nc, ctx, g, d, logits, logits_read):
    def sb(name, shape, dt=F32):
        return ctx.enter_context(nc.sbuf_tensor(name, shape, dt))

    N = 2 * E0
    w_raw, w_hi, w_lo = split_weights(nc, g, ctx, "r0", "wr0", [P, KC, N])
    top, shifted = sb("top0", [P, TC, 2]), sb("shifted0", [P, TC, 2, E0])
    exps, sums, inv = sb("exps0", [P, TC, 2, E0]), sb("sums_r0", [P, TC, 2]), sb("inv_r0", [P, TC, 2])
    both, total = sb("both0", [P, TC, E0]), sb("total0", [P, TC])
    loaded, split_done = g.sem("r0_loaded"), g.sem("r0_split_done")
    logits_done, shifted_done, exp_done = g.sem("logits0_done"), g.sem("shifted0_done"), g.sem("exp_r0_done")
    dve_steps = g.sem("r0_dve_steps")

    def on_sync(sp):
        sp.dma_start(w_raw[:, :, :], d["wr0"]).then_inc(loaded, 16)

    def on_gpsimd(pool):
        split_on_pool(pool, w_raw, w_hi, w_lo, loaded, split_done)

    def on_scalar(act):
        act.wait_ge(shifted_done, 1)
        act.activation(exps[:, :, 0, :], shifted[:, :, 0, :], ACT.Exp).then_inc(exp_done, 1)
        act.activation(exps[:, :, 1, :], shifted[:, :, 1, :], ACT.Exp, scale=10.0).then_inc(exp_done, 1)

    def on_tensor(pe):
        pe.wait_ge(split_done, 2)
        router_logits(pe, logits, N, (g.xnT_hi, g.xnT_lo), (w_hi, w_lo)).then_inc(logits_done, 1)

    def on_vector(dve):
        own = Chain(dve, dve_steps)
        dve.wait_ge(logits_done, 1)
        own.link(dve.tensor_reduce(top[:, :, :], logits[:, :, :].rearrange("p c (w e) -> p c w e", w=2), X, ALU.max))
        wide = [P, TC, E0]
        own.link(dve.tensor_tensor(shifted[:, :, 0, :], logits[:, :, 0:E0], top[:, :, 0:1].to_broadcast(wide), ALU.subtract))
        own.link(dve.tensor_tensor(shifted[:, :, 1, :], logits[:, :, E0:2 * E0], top[:, :, 1:2].to_broadcast(wide), ALU.subtract))
        dve.sem_inc(shifted_done, 1)
        dve.sem_inc(logits_read, 4)
        dve.wait_ge(exp_done, 2)
        own.link(dve.tensor_reduce(sums[:, :, :], exps[:, :, :, :], X, ALU.add))
        own.link(dve.reciprocal(inv[:, :, :], sums[:, :, :]))
        for w in range(2):
            own.step(dve.tensor_tensor(exps[:, :, w, :], exps[:, :, w, :], inv[:, :, w:w + 1].to_broadcast(wide), ALU.mult))
        own.wait()
        own.link(dve.tensor_tensor(both[:, :, :], exps[:, :, 0, :], exps[:, :, 1, :], ALU.mult))
        own.link(dve.tensor_reduce(total[:, :], both[:, :, :], X, ALU.add))
        own.link(dve.tensor_scalar(total[:, :], total[:, :], 1e-9, None, ALU.add))
        own.link(dve.reciprocal(total[:, :], total[:, :]))
        per = U0 // E0
        for i in range(per):
            own.step(dve.tensor_tensor(g.cw[:, :, 0:U0].rearrange("p c (e i) -> p c e i", i=per)[:, :, :, i], both[:, :, :],
                                       total[:, :].rearrange("p (c o) -> p c o", o=1).to_broadcast(wide), ALU.mult))
        own.wait()

    r = Shared()
    r.on_sync, r.on_gpsimd, r.on_scalar, r.on_tensor, r.on_vector = on_sync, on_gpsimd, on_scalar, on_tensor, on_vector
    return r


def l2_router(nc, ctx, g, d, logits, logits_read):
    def sb(name, shape, dt=F32):
        return ctx.enter_context(nc.sbuf_tensor(name, shape, dt))

    w_raw, w_hi, w_lo = split_weights(nc, g, ctx, "r2", "wr2", [P, KC, E2])
    scores, biased = sb("scores2", [P, TC, E2]), sb("biased2", [P, TC, 2 * E2])
    largest, taken, left = sb("largest2", [P, TC, 8]), sb("taken2", [P, TC, 8]), sb("left2", [P, TC, 2 * E2])
    mask = sb("mask2", [P, TC, E2])
    loaded, split_done = g.sem("r2_loaded"), g.sem("r2_split_done")
    logits_done, scores_done, dve_steps = g.sem("logits2_done"), g.sem("scores2_done"), g.sem("r2_dve_steps")

    def on_sync(sp):
        sp.dma_start(w_raw[:, :, :], d["wr2"]).then_inc(loaded, 16)

    def on_gpsimd(pool):
        split_on_pool(pool, w_raw, w_hi, w_lo, loaded, split_done)

    def on_scalar(act):
        act.wait_ge(logits_done, 1)
        act.activation(scores[:, :, :], logits[:, :, 0:E2], ACT.Sigmoid).then_inc(scores_done, 1)

    def on_tensor(pe):
        pe.wait_ge(split_done, 2)
        router_logits(pe, logits, E2, (g.xnT_hi, g.xnT_lo), (w_hi, w_lo)).then_inc(logits_done, 1)

    def on_vector(dve):
        own = Chain(dve, dve_steps)
        own.step(dve.memset(biased[:, :, :], NEG))
        own.step(dve.memset(taken[:, :, :], NEG))
        own.link(dve.memset(g.cw[:, :, :], 1.0))
        dve.wait_ge(scores_done, 1)
        dve.sem_inc(logits_read, 4)
        own.link(dve.tensor_tensor(biased[:, :, 0:E2], scores[:, :, :],
                                   row(g, "eb2").rearrange("p (o e) -> p o e", o=1).to_broadcast([P, TC, E2]), ALU.add))
        for c in range(TC):
            own.step(dve.max(largest[:, c, :], biased[:, c, :]))
        own.wait()
        own.link(dve.tensor_copy(taken[:, :, 0:2], largest[:, :, 0:2]))
        for c in range(TC):
            own.step(dve.match_replace(left[:, c, :], taken[:, c, :], biased[:, c, :], 2 * NEG))
        own.wait()
        own.link(dve.tensor_scalar(mask[:, :, :], left[:, :, 0:E2], 1.5 * NEG, None, ALU.is_lt))
        own.link(dve.tensor_tensor(g.cw[:, :, 0:E2], mask[:, :, :], scores[:, :, :], ALU.mult))

    r = Shared()
    r.on_sync, r.on_gpsimd, r.on_scalar, r.on_tensor, r.on_vector = on_sync, on_gpsimd, on_scalar, on_tensor, on_vector
    return r


def gated_layer_phase(nc, g, d, tag, N, weights, make_router):
    FC = FU // P
    Q = 2 * FC
    with ExitStack() as ctx:
        def sb(name, shape, dt=F32):
            return ctx.enter_context(nc.sbuf_tensor(f"{name}_{tag}", shape, dt))

        def two(name, shape, dt=F32):
            return [sb(f"{name}{i}", shape, dt) for i in range(2)]

        gu_raw, gu_hi, gu_lo = two("gu_raw", [P, 2, KC, FU]), two("gu_hi", [P, 2, KC, FU], F32R), two("gu_lo", [P, 2, KC, FU], F32R)
        dn_raw, dn_hi, dn_lo = two("dn_raw", [P, FC, D]), two("dn_hi", [P, FC, D], F32R), two("dn_lo", [P, FC, D], F32R)
        h_hi, h_lo = two("h_hi", [P, FC, T], F32R), two("h_lo", [P, FC, T], F32R)
        silu, hidden = sb("silu", [P, 2, 512]), sb("hidden", [P, 2, 512])
        gate = ctx.enter_context(nc.psum_tensor(f"gate_{tag}", [P, 2, 512], F32))
        up = ctx.enter_context(nc.psum_tensor(f"up_{tag}", [P, 2, 512], F32))
        out = ctx.enter_context(nc.psum_tensor(f"out_{tag}", [P, TC // 2, 2, D], F32))

        def sem(name):
            return g.sem(f"{name}_{tag}")

        gu_loaded, dn_loaded = [sem("gu_loaded0"), sem("gu_loaded1")], [sem("dn_loaded0"), sem("dn_loaded1")]
        gu_hi_done, gu_lo_done, dn_hi_done, dn_lo_done = sem("gu_hi_done"), sem("gu_lo_done"), sem("dn_hi_done"), sem("dn_lo_done")
        gu_done, silu_done, hidden_done = sem("gu_done"), sem("silu_done"), sem("hidden_done")
        h_hi_done, h_lo_done = sem("h_hi_done"), sem("h_lo_done")
        out_done = sem("out_done")
        out_free = sem("out_free")

        norm = normaliser(nc, ctx, g, tag, out[:, :, :, :].rearrange("p (h k) j e -> p h k (j e)", h=2))
        router = make_router(nc, ctx, g, d, out[:, 0, :, :].rearrange("p j e -> p (j e)")[:, 0:TC * 16].rearrange("p (c n) -> p c n", c=TC), out_free)

        def periods(eng, period, route):
            period(0, 0, 1, 1)
            route(eng)
            with eng.Fori(0, (N - 2) // 2) as i:
                period(2 * i + 1, 1, i + 1, i + 2)
                period(2 * i + 2, 0, i + 2, i + 2)
            period(N - 1, 1, N // 2, None)
            period(N, 0, None, None)

        with nc.Block() as block:
            @block.sync
            def _(sp):
                def load_gu(n, s):
                    sp.dma_start(gu_raw[s][:, :, :, :], weights[n, :, 0:2, :, :]).then_inc(gu_loaded[s], 16)

                def load_dn(n, s):
                    sp.dma_start(dn_raw[s][:, :, :], weights[n, :, 2, :, :]).then_inc(dn_loaded[s], 16)

                load_gu(0, 0)
                router.on_sync(sp)
                load_dn(0, 0)
                load_gu(1, 1)
                load_dn(1, 1)
                with sp.Fori(0, (N - 2) // 2) as i:
                    for s in range(2):
                        sp.wait_ge(gu_lo_done, 2 * i + s + 1)
                        load_gu(2 * i + s + 2, s)
                        sp.wait_ge(dn_lo_done, 2 * i + s + 1)
                        load_dn(2 * i + s + 2, s)

            @block.tensor
            def _(pe):
                def period(n, s, uses, next_uses):
                    first, has_gu = isinstance(n, int) and n == 0, uses is not None
                    if has_gu:
                        pe.wait_ge(gu_hi_done, n + 1)
                        pe.wait_ge(gu_lo_done, n + 1)
                        for q in range(Q):
                            fc, half = divmod(q, 2)
                            if first and fc == 0:
                                norm.wait_half(pe, half)
                            if not (first and q < 2):
                                pe.wait_ge(silu_done, Q * n + q - 1)
                                pe.wait_ge(hidden_done, Q * n + q - 1)
                            t, f = slice(half * 512, (half + 1) * 512), slice(fc * P, (fc + 1) * P)
                            for which, bank in ((0, gate), (1, up)):
                                for k in range(KC):
                                    last = mm3(pe, bank[:, q % 2, :], (gu_hi[s][:, which, k, f], gu_lo[s][:, which, k, f]),
                                               (g.xnT_hi[:, k, t], g.xnT_lo[:, k, t]), k == 0, k == KC - 1)
                            last.then_inc(gu_done, 1)
                    if not first:
                        o = 1 - s
                        pe.wait_ge(dn_hi_done, n)
                        pe.wait_ge(dn_lo_done, n)
                        pe.wait_ge(h_hi_done, Q * n)
                        pe.wait_ge(h_lo_done, Q * n)
                        for b in range(TC // 2):
                            pe.wait_ge(out_free, 4 * (n - 1) + b + 1)
                            for j in range(2):
                                t = slice((2 * b + j) * P, (2 * b + j + 1) * P)
                                for fc in range(FC):
                                    last = mm3(pe, out[:, b, j, :], (h_hi[o][:, fc, t], h_lo[o][:, fc, t]),
                                               (dn_hi[o][:, fc, :], dn_lo[o][:, fc, :]), j == 0 and fc == 0, fc == FC - 1)
                            last.then_inc(out_done, 1)

                norm.on_tensor(pe)
                pe.sem_inc(out_done, 4)
                periods(pe, period, router.on_tensor)

            @block.scalar
            def _(act):
                def split_gu(n, s, uses):
                    act.wait_ge(gu_loaded[s], 16 * uses)
                    act.activation(gu_hi[s][:, :, :, :], gu_raw[s][:, :, :, :], ACT.Copy).then_inc(gu_hi_done, 1)

                def period(n, s, uses, next_uses):
                    if uses is None:
                        return

                    def silu_of(q):
                        act.wait_ge(gu_done, Q * n + q + 1)
                        act.activation(silu[:, q % 2, :], gate[:, q % 2, :], ACT.Silu).then_inc(silu_done, 1)

                    def high(q):
                        fc, half = divmod(q, 2)
                        act.wait_ge(hidden_done, Q * n + q + 1)
                        act.activation(h_hi[s][:, fc, half * 512:(half + 1) * 512], hidden[:, q % 2, :], ACT.Copy).then_inc(h_hi_done, 1)

                    silu_of(0)
                    silu_of(1)
                    if not (isinstance(n, int) and n == 0):
                        act.wait_ge(out_done, 4 * n)
                    high(0)
                    if next_uses is not None:
                        split_gu(n + 1, 1 - s, next_uses)
                    silu_of(2)
                    high(1)
                    silu_of(3)
                    high(2)
                    high(3)
                    act.wait_ge(dn_loaded[s], 16 * uses)
                    act.activation(dn_hi[s][:, :, :], dn_raw[s][:, :, :], ACT.Copy).then_inc(dn_hi_done, 1)

                norm.on_scalar(act)
                periods(act, period, router.on_scalar)

            @block.gpsimd
            def _(pool):
                def split_gu(n, s):
                    pool.wait_ge(gu_hi_done, n + 1)
                    pool.tensor_tensor(gu_lo[s][:, :, :, :], gu_raw[s][:, :, :, :], f32(gu_hi[s][:, :, :, :]), ALU.subtract).then_inc(gu_lo_done, 1)

                def period(n, s, uses, next_uses):
                    if uses is None:
                        return
                    if not (isinstance(n, int) and n == 0):
                        pool.wait_ge(dn_lo_done, n)
                    if next_uses is not None:
                        split_gu(n + 1, 1 - s)
                        pool.wait_ge(gu_lo_done, n + 2)
                    if uses is not None:
                        pool.wait_ge(dn_hi_done, n + 1)
                        pool.tensor_tensor(dn_lo[s][:, :, :], dn_raw[s][:, :, :], f32(dn_hi[s][:, :, :]), ALU.subtract).then_inc(dn_lo_done, 1)

                pool.wait_ge(gu_loaded[0], 16)
                pool.tensor_copy(gu_hi[0][:, :, :, :], gu_raw[0][:, :, :, :]).then_inc(gu_hi_done, 1)
                split_gu(0, 0)
                pool.wait_ge(gu_lo_done, 1)
                router.on_gpsimd(pool)
                periods(pool, period, lambda pool: None)

            @block.vector
            def _(dve):
                def period(n, s, uses, next_uses):
                    first = isinstance(n, int) and n == 0

                    def product(q):
                        dve.wait_ge(silu_done, Q * n + q + 1)
                        if not (first and q < 2):
                            dve.wait_ge(h_hi_done, Q * n + q - 1)
                            dve.wait_ge(h_lo_done, Q * n + q - 1)
                        dve.tensor_tensor(hidden[:, q % 2, :], silu[:, q % 2, :], up[:, q % 2, :], ALU.mult).then_inc(hidden_done, 1)

                    def low(q):
                        fc, half = divmod(q, 2)
                        t = slice(half * 512, (half + 1) * 512)
                        dve.wait_ge(h_hi_done, Q * n + q + 1)
                        dve.tensor_tensor(h_lo[s][:, fc, t], hidden[:, q % 2, :], f32(h_hi[s][:, fc, t]), ALU.subtract).then_inc(h_lo_done, 1)

                    if uses is not None:
                        product(0)
                        product(1)
                        low(0)
                        product(2)
                        low(1)
                        product(3)
                        low(2)
                        low(3)
                    if not first:
                        dve.wait_ge(out_free, 4 * n)
                        for b in range(TC // 2):
                            dve.wait_ge(out_done, 4 * n + b + 1)
                            for j in range(2):
                                c = 2 * b + j
                                weight = g.cw[:, c, bass.ds(n - 1, 1)]
                                last = dve.scalar_tensor_tensor(g.x[:, c, :], out[:, b, j, :], weight, g.x[:, c, :], ALU.mult, ALU.add)
                            last.then_inc(out_free, 1)

                norm.on_vector(dve)
                periods(dve, period, router.on_vector)


def l1_shift_phase(nc, g, d):
    with ExitStack() as ctx:
        def sb(name, shape, dt=F32):
            return ctx.enter_context(nc.sbuf_tensor(name, shape, dt))

        w_raw, w_hi, w_lo = split_weights(nc, g, ctx, "s1", "wx1", [P, 2, KC, D])
        mean, mean_hi, mean_lo = sb("mean", [P, KC, B, P]), sb("mean_hi", [P, KC, B, P], F32R), sb("mean_lo", [P, KC, B, P], F32R)
        out = ctx.enter_context(nc.psum_tensor("out_s1", [P, TC // 2, 2, D], F32))
        loaded, hi_done, lo_done = g.sem("s1_loaded"), g.sem("s1_hi_done"), g.sem("s1_lo_done")
        mean_done, out_done, dve_steps = g.sem("mean_done"), g.sem("out_s1_done"), g.sem("s1_dve_steps")
        with nc.Block() as block:
            @block.sync
            def _(sp):
                sp.dma_start(w_raw[:, :, :, :], d["wx1"]).then_inc(loaded, 16)

            @block.scalar
            def _(act):
                act.wait_ge(mean_done, 1)
                act.activation(mean_hi[:, :, :, :], mean[:, :, :, :], ACT.Copy).then_inc(hi_done, 1)
                act.wait_ge(loaded, 16)
                act.activation(w_hi[:, :, :, :], w_raw[:, :, :, :], ACT.Copy).then_inc(hi_done, 1)

            @block.vector
            def _(dve):
                dve.tensor_scalar(mean[:, :, :, :], g.ctx_sum[:, :, :].rearrange("p k (b o) -> p k b o", o=1).to_broadcast([P, KC, B, P]),
                                  1.0 / SC, None, ALU.mult).then_inc(mean_done, 1)
                dve.wait_ge(hi_done, 1)
                dve.tensor_tensor(mean_lo[:, :, :, :], mean[:, :, :, :], f32(mean_hi[:, :, :, :]), ALU.subtract).then_inc(lo_done, 1)
                dve.wait_ge(hi_done, 2)
                dve.tensor_tensor(w_lo[:, :, :, :], w_raw[:, :, :, :], f32(w_hi[:, :, :, :]), ALU.subtract).then_inc(lo_done, 1)
                own = Chain(dve, dve_steps)
                own.link(dve.tensor_tensor(g.x[:, :, :], g.x[:, :, :], row(g, "b_x1").rearrange("p (o e) -> p o e", o=1).to_broadcast([P, TC, D]), ALU.add))
                for m in range(TC // 2):
                    dve.wait_ge(out_done, m + 1)
                    dve.tensor_tensor(g.x[:, 2 * m:2 * m + 2, :], g.x[:, 2 * m:2 * m + 2, :], out[:, m, :, :], ALU.add)

            @block.tensor
            def _(pe):
                pe.wait_ge(lo_done, 2)
                for m in range(TC // 2):
                    for j in range(2):
                        c = 2 * m + j
                        b, t = c * P // S, slice(c * P, (c + 1) * P)
                        for k in range(KC):
                            mm3(pe, out[:, m, j, :], (g.xnT_hi[:, k, t], g.xnT_lo[:, k, t]),
                                (w_hi[:, 0, k, :], w_lo[:, 0, k, :]), j == 0 and k == 0, False)
                        for k in range(KC):
                            last = mm3(pe, out[:, m, j, :], (mean_hi[:, k, b, :], mean_lo[:, k, b, :]),
                                       (w_hi[:, 1, k, :], w_lo[:, 1, k, :]), False, k == KC - 1)
                    last.then_inc(out_done, 1)


def l1_router_phase(nc, g, d):
    HALF = E1 // 2
    with ExitStack() as ctx:
        def sb(name, shape, dt=F32):
            return ctx.enter_context(nc.sbuf_tensor(name, shape, dt))

        w_raw, w_hi, w_lo = split_weights(nc, g, ctx, "r1", "wr1", [P, KC, E1])
        shifted, exps, left = sb("shifted1", [P, TC, E1]), sb("exps1", [P, TC, E1]), sb("left1", [P, TC, E1])
        logit, top, largest = sb("logit1", [P, TC, E1]), sb("top1", [P, TC]), sb("largest1", [P, TC, 8])
        total = sb("total1", [P, TC])
        parts = sb("cw_parts", [P, TC, 2, 3, HALF], BF16)
        ident16 = sb("ident16", [P, P], BF16)
        logits = ctx.enter_context(nc.psum_tensor("logits1", [P, TC, E1], F32))
        cw_turned = ctx.enter_context(nc.psum_tensor("cw_turned", [P, TC, P], F32))
        parts_turned = ctx.enter_context(nc.psum_tensor("parts_turned", [P, 2, TC, P], BF16))
        loaded, hi_done, lo_done = g.sem("r1_loaded"), g.sem("r1_hi_done"), g.sem("r1_lo_done")
        logits_done, shifted_done, exp_done = g.sem("logits1_done"), g.sem("shifted1_done"), g.sem("exp_r1_done")
        cw_done, turned_done, dve_steps = g.sem("cw1_done"), g.sem("cw1_turned_done"), g.sem("r1_dve_steps")
        sel_loaded = g.sem("sel_loaded")
        with nc.Block() as block:
            @block.sync
            def _(sp):
                sp.dma_start(w_raw[:, :, :], d["wr1"]).then_inc(loaded, 16)
                sp.dma_start(g.select[:, :, :], d["select"]).then_inc(sel_loaded, 16)
                sp.wait_ge(sel_loaded, 16)

            @block.gpsimd
            def _(pool):
                pool.memset(g.cwT[E1:E1 + ES1, :], 1.0)
                pool.memset(g.cw_partsT[3 * HALF:3 * HALF + 1, :, :], 1.0)

            @block.scalar
            def _(act):
                act.wait_ge(loaded, 16)
                act.activation(w_hi[:, :, :], w_raw[:, :, :], ACT.Copy).then_inc(hi_done, 1)
                act.wait_ge(shifted_done, 1)
                act.activation(exps[:, :, :], shifted[:, :, :], ACT.Exp).then_inc(exp_done, 1)
                act.wait_ge(turned_done, 1)
                for h in range(2):
                    act.activation(g.cw_partsT[0:3 * HALF, h, :], parts_turned[0:3 * HALF, h, :, :], ACT.Copy)

            @block.tensor
            def _(pe):
                pe.wait_ge(hi_done, 1)
                pe.wait_ge(lo_done, 1)
                router_logits(pe, logits, E1, (g.xnT_hi, g.xnT_lo), (w_hi, w_lo)).then_inc(logits_done, 1)
                pe.wait_ge(cw_done, 1)
                for c in range(TC):
                    pe.transpose(cw_turned[0:E1, c, :], exps[:, c, :], g.ident[:, :])
                    for h in range(2):
                        last = pe.transpose(parts_turned[0:3 * HALF, h, c, :], parts[:, c, h, :, :].rearrange("p a e -> p (a e)"), ident16[:, :])
                last.then_inc(turned_done, 1)

            @block.vector
            def _(dve):
                own = Chain(dve, dve_steps)
                dve.wait_ge(hi_done, 1)
                dve.tensor_tensor(w_lo[:, :, :], w_raw[:, :, :], f32(w_hi[:, :, :]), ALU.subtract).then_inc(lo_done, 1)
                own.step(dve.tensor_copy(ident16[:, :], g.ident[:, :]))
                dve.wait_ge(logits_done, 1)
                own.link(dve.tensor_tensor(logit[:, :, :], logits[:, :, :], row(g, "rb1").rearrange("p (o e) -> p o e", o=1).to_broadcast([P, TC, E1]), ALU.add))
                own.link(dve.tensor_reduce(top[:, :], logit[:, :, :], X, ALU.max))
                wide = [P, TC, E1]
                dve.tensor_tensor(shifted[:, :, :], logit[:, :, :], top[:, :].rearrange("p (c o) -> p c o", o=1).to_broadcast(wide), ALU.subtract).then_inc(shifted_done, 1)
                dve.wait_ge(exp_done, 1)
                own.link(dve.tensor_reduce(total[:, :], exps[:, :, :], X, ALU.add))
                own.link(dve.reciprocal(total[:, :], total[:, :]))
                own.link(dve.tensor_tensor(exps[:, :, :], exps[:, :, :], total[:, :].rearrange("p (c o) -> p c o", o=1).to_broadcast(wide), ALU.mult))
                for c in range(TC):
                    own.step(dve.max(largest[:, c, :], exps[:, c, :]))
                own.wait()
                for c in range(TC):
                    own.step(dve.match_replace(left[:, c, :], largest[:, c, :], exps[:, c, :], 0.0))
                own.wait()
                own.link(dve.tensor_tensor(exps[:, :, :], exps[:, :, :], left[:, :, :], ALU.subtract))
                own.link(dve.tensor_reduce(total[:, :], exps[:, :, :], X, ALU.add))
                own.link(dve.reciprocal(total[:, :], total[:, :]))
                own.link(dve.tensor_tensor(exps[:, :, :], exps[:, :, :], total[:, :].rearrange("p (c o) -> p c o", o=1).to_broadcast(wide), ALU.mult))
                halves = exps[:, :, :].rearrange("p c (h e) -> p c h e", h=2)
                rest = shifted[:, :, :].rearrange("p c (h e) -> p c h e", h=2)
                own.link(dve.tensor_copy(parts[:, :, :, 0, :], halves))
                own.link(dve.tensor_tensor(rest, halves, parts[:, :, :, 0, :], ALU.subtract))
                own.link(dve.tensor_copy(parts[:, :, :, 1, :], rest))
                dve.tensor_tensor(parts[:, :, :, 2, :], rest, parts[:, :, :, 1, :], ALU.subtract).then_inc(cw_done, 1)
                dve.wait_ge(turned_done, 1)
                dve.tensor_copy(g.cwT[0:E1, :], cw_turned[0:E1, :, :])


def l1_units_phase(nc, g, d):
    N = U1
    Q = 2
    with ExitStack() as ctx:
        def sb(name, shape, dt=F32):
            return ctx.enter_context(nc.sbuf_tensor(f"{name}_l1", shape, dt))

        def two(name, shape, dt=F32):
            return [sb(f"{name}{i}", shape, dt) for i in range(2)]

        up_raw, up_hi, up_lo = two("up_raw", [P, D + 1]), two("up_hi", [P, KC, P], F32R), two("up_lo", [P, KC, P], F32R)
        b1 = two("b1", [P, 1])
        dn_raw, dn_hi, dn_lo = two("dn_raw", [P, D]), two("dn_hi", [P, D], F32R), two("dn_lo", [P, D], F32R)
        h_hi, h_lo = two("h_hi", [P, T], F32R), two("h_lo", [P, T], F32R)
        silu, hidden = sb("silu", [P, 2, 512]), sb("hidden", [P, 2, 512])
        b2 = sb("b2", [E1 + ES1, D])
        up = ctx.enter_context(nc.psum_tensor("up_l1", [P, 2, 512], F32))
        weight = ctx.enter_context(nc.psum_tensor("weight_l1", [P, 2, 512], F32))
        out = ctx.enter_context(nc.psum_tensor("out_l1", [P, TC // 2, 2, D], F32))

        def sem(name):
            return g.sem(f"{name}_l1")

        b2_loaded = sem("b2_loaded")
        up_loaded, dn_loaded = [sem("up_loaded0"), sem("up_loaded1")], [sem("dn_loaded0"), sem("dn_loaded1")]
        up_hi_done, up_lo_done, dn_hi_done, dn_lo_done = sem("up_hi_done"), sem("up_lo_done"), sem("dn_hi_done"), sem("dn_lo_done")
        up_done, silu_done, hidden_done = sem("up_done"), sem("silu_done"), sem("hidden_done")
        h_hi_done, h_lo_done = sem("h_hi_done"), sem("h_lo_done")
        down_free = sem("down_free")

        def periods(eng, period):
            period(0, 0, 1, 1, 0)
            with eng.Fori(0, (N - 2) // 2) as i:
                period(2 * i + 1, 1, i + 1, i + 2, i)
                period(2 * i + 2, 0, i + 2, i + 2, i + 1)
            period(N - 1, 1, N // 2, None, N // 2 - 1)
            period(N, 0, None, None, None)

        with nc.Block() as block:
            @block.sync
            def _(sp):
                def load_up(n, s):
                    sp.dma_start(up_raw[s][:, :], d["w1"][n, :, 0:D + 1]).then_inc(up_loaded[s], 16)

                def load_dn(n, s):
                    sp.dma_start(dn_raw[s][:, :], d["w1"][n, :, D + 1:2 * D + 1]).then_inc(dn_loaded[s], 16)

                for s in range(2):
                    load_up(s, s)
                    load_dn(s, s)
                sp.dma_start(b2[:, :], d["b2"]).then_inc(b2_loaded, 16)
                with sp.Fori(0, (N - 2) // 2) as i:
                    for s in range(2):
                        sp.wait_ge(up_lo_done, 2 * i + s + 1)
                        load_up(2 * i + s + 2, s)
                        sp.wait_ge(dn_lo_done, 2 * i + s + 1)
                        load_dn(2 * i + s + 2, s)

            @block.tensor
            def _(pe):
                def period(n, s, uses, next_uses, pair):
                    first, has_up = isinstance(n, int) and n == 0, uses is not None
                    if has_up:
                        pe.wait_ge(up_hi_done, n + 1)
                        pe.wait_ge(up_lo_done, n + 1)
                        for q in range(Q):
                            if not first:
                                pe.wait_ge(silu_done, Q * n + q - 1)
                                pe.wait_ge(hidden_done, Q * n + q - 1)
                            t = slice(q * 512, (q + 1) * 512)
                            for k in range(KC):
                                mm3(pe, up[:, q, :], (up_hi[s][:, k, :], up_lo[s][:, k, :]),
                                    (g.xnT_hi[:, k, t], g.xnT_lo[:, k, t]), k == 0, k == KC - 1)
                            pe.matmul(weight[:, q, :], g.select[0:97, bass.ds(pair, 1), :].rearrange("p o m -> p (o m)"),
                                      g.cw_partsT[0:97, s, t], start=True, stop=True).then_inc(up_done, 1)
                    if not first:
                        o = 1 - s
                        pe.wait_ge(dn_hi_done, n)
                        pe.wait_ge(dn_lo_done, n)
                        pe.wait_ge(h_hi_done, Q * n)
                        pe.wait_ge(h_lo_done, Q * n)
                        for c in range(TC):
                            t = slice(c * P, (c + 1) * P)
                            last = mm3(pe, out[:, c // 2, c % 2, :], (h_hi[o][:, t], h_lo[o][:, t]),
                                       (dn_hi[o][:, :], dn_lo[o][:, :]), False, not has_up)
                        last.then_inc(down_free, 1)

                pe.sem_inc(down_free, 2)
                pe.wait_ge(b2_loaded, 16)
                for c in range(TC):
                    pe.matmul(out[:, c // 2, c % 2, :], g.cwT[0:E1 + ES1, c * P:(c + 1) * P], b2[:, :],
                              start=c % 2 == 0, stop=False, skip_group_check=True)
                periods(pe, period)

            @block.scalar
            def _(act):
                def split_up(n, s, uses):
                    act.wait_ge(up_loaded[s], 16 * uses)
                    act.activation(b1[s][:, :], up_raw[s][:, D:D + 1], ACT.Copy)
                    act.activation(up_hi[s][:, :, :], up_raw[s][:, 0:D], ACT.Copy).then_inc(up_hi_done, 1)

                def period(n, s, uses, next_uses, pair):
                    if uses is None:
                        return

                    def silu_of(q):
                        act.wait_ge(up_done, Q * n + q + 1)
                        act.activation(silu[:, q, :], up[:, q, :], ACT.Silu, bias=b1[s][:, :]).then_inc(silu_done, 1)

                    def high(q):
                        act.wait_ge(hidden_done, Q * n + q + 1)
                        act.activation(h_hi[s][:, q * 512:(q + 1) * 512], hidden[:, q, :], ACT.Copy).then_inc(h_hi_done, 1)

                    silu_of(0)
                    if next_uses is not None:
                        split_up(n + 1, 1 - s, next_uses)
                    silu_of(1)
                    act.wait_ge(down_free, n + 1)
                    high(0)
                    high(1)
                    act.wait_ge(dn_loaded[s], 16 * uses)
                    act.activation(dn_hi[s][:, :], dn_raw[s][:, :], ACT.Copy).then_inc(dn_hi_done, 1)

                split_up(0, 0, 1)
                periods(act, period)

            @block.gpsimd
            def _(pool):
                def split_up(n, s):
                    pool.wait_ge(up_hi_done, n + 1)
                    pool.tensor_tensor(up_lo[s][:, :, :], up_raw[s][:, 0:D].rearrange("p (k f) -> p k f", k=KC), f32(up_hi[s][:, :, :]), ALU.subtract).then_inc(up_lo_done, 1)

                def period(n, s, uses, next_uses, pair):
                    if uses is None:
                        return
                    if not (isinstance(n, int) and n == 0):
                        pool.wait_ge(dn_lo_done, n)
                    if next_uses is not None:
                        split_up(n + 1, 1 - s)
                        pool.wait_ge(up_lo_done, n + 2)
                    if uses is not None:
                        pool.wait_ge(dn_hi_done, n + 1)
                        pool.tensor_tensor(dn_lo[s][:, :], dn_raw[s][:, :], f32(dn_hi[s][:, :]), ALU.subtract).then_inc(dn_lo_done, 1)

                split_up(0, 0)
                periods(pool, period)

            @block.vector
            def _(dve):
                def period(n, s, uses, next_uses, pair):
                    first = isinstance(n, int) and n == 0
                    if uses is None:
                        return
                    for q in range(Q):
                        dve.wait_ge(silu_done, Q * n + q + 1)
                        if not first:
                            dve.wait_ge(h_hi_done, Q * n + q - 1)
                            dve.wait_ge(h_lo_done, Q * n + q - 1)
                        dve.tensor_tensor(hidden[:, q, :], silu[:, q, :], weight[:, q, :], ALU.mult).then_inc(hidden_done, 1)
                    for q in range(Q):
                        t = slice(q * 512, (q + 1) * 512)
                        dve.wait_ge(h_hi_done, Q * n + q + 1)
                        dve.tensor_tensor(h_lo[s][:, t], hidden[:, q, :], f32(h_hi[s][:, t]), ALU.subtract).then_inc(h_lo_done, 1)

                periods(dve, period)
                dve.wait_ge(down_free, N + 2)
                for m in range(TC // 2):
                    dve.tensor_tensor(g.x[:, 2 * m:2 * m + 2, :], g.x[:, 2 * m:2 * m + 2, :], out[:, m, :, :], ALU.add)


def project_phase(nc, g, d, tag, weights, bq, bk):
    with ExitStack() as ctx:
        w_raw, w_hi, w_lo = split_weights(nc, g, ctx, tag, "wqkv", [P, 3, KC, D])
        acc = ctx.enter_context(nc.psum_tensor(f"acc_{tag}", [P, 8, 512], F32))
        loaded, w_hi_done, w_lo_done = g.sem(f"w_loaded_{tag}"), g.sem(f"w_hi_done_{tag}"), g.sem(f"w_lo_done_{tag}")
        tile_done, hi_done, lo_done = g.sem(f"tile_done_{tag}"), g.sem(f"tile_hi_done_{tag}"), g.sem(f"tile_lo_done_{tag}")
        tiles = [(1, fc, t) for t in range(0, CT, 512) for fc in range(KC)]
        tiles += [(0, fc, t) for t in range(0, T, 512) for fc in range(KC)]
        tiles += [(2, None, m) for m in range(CT // P // 2)]

        def place(n):
            which, fc, t = tiles[n]
            if which == 2:
                return g.v_hi[:, 2 * t:2 * t + 2, :], g.v_lo[:, 2 * t:2 * t + 2, :], None
            hi, lo = (g.qT_hi, g.qT_lo) if which == 0 else (g.kT_hi, g.kT_lo)
            bias = bq if which == 0 else bk
            return hi[:, fc, t:t + 512], lo[:, fc, t:t + 512], None if bias is None else g.bias_cols[:, bias, fc:fc + 1]

        with nc.Block() as block:
            @block.sync
            def _(sp):
                sp.dma_start(w_raw[:, :, :, :], weights).then_inc(loaded, 16)

            @block.tensor
            def _(pe):
                pe.wait_ge(w_hi_done, 1)
                pe.wait_ge(w_lo_done, 1)
                for n, (which, fc, t) in enumerate(tiles):
                    if n >= 8:
                        pe.wait_ge(lo_done, n - 7)
                    if which == 2:
                        for j in range(2):
                            a = (2 * t + j) * P
                            for k in range(KC):
                                last = mm3(pe, acc[:, n % 8, j * D:(j + 1) * D], (g.ctxT_hi[:, k, a:a + P], g.ctxT_lo[:, k, a:a + P]),
                                           (w_hi[:, 2, k, :], w_lo[:, 2, k, :]), j == 0 and k == 0, k == KC - 1)
                    else:
                        src = (g.xnT_hi, g.xnT_lo) if which == 0 else (g.ctxT_hi, g.ctxT_lo)
                        f = slice(fc * P, (fc + 1) * P)
                        for k in range(KC):
                            last = mm3(pe, acc[:, n % 8, :], (w_hi[:, which, k, f], w_lo[:, which, k, f]),
                                       (src[0][:, k, t:t + 512], src[1][:, k, t:t + 512]), k == 0, k == KC - 1)
                    last.then_inc(tile_done, 1)

            @block.scalar
            def _(act):
                act.wait_ge(loaded, 16)
                act.activation(w_hi[:, :, :, :], w_raw[:, :, :, :], ACT.Copy).then_inc(w_hi_done, 1)
                for n in range(len(tiles)):
                    hi, _, bias = place(n)
                    act.wait_ge(tile_done, n + 1)
                    if bias is None:
                        act.activation(hi, acc[:, n % 8, :], ACT.Copy).then_inc(hi_done, 1)
                    else:
                        act.activation(hi, acc[:, n % 8, :], ACT.Identity, bias=bias).then_inc(hi_done, 1)

            @block.vector
            def _(dve):
                dve.wait_ge(w_hi_done, 1)
                dve.tensor_tensor(w_lo[:, :, :, :], w_raw[:, :, :, :], f32(w_hi[:, :, :, :]), ALU.subtract).then_inc(w_lo_done, 1)
                for n in range(len(tiles)):
                    hi, lo, bias = place(n)
                    dve.wait_ge(hi_done, n + 1)
                    dve.scalar_tensor_tensor(lo, acc[:, n % 8, :], 0.0 if bias is None else bias, f32(hi),
                                             ALU.add, ALU.subtract).then_inc(lo_done, 1)


def attend_phase(nc, g, d, tag, phi, out_weight):
    NU = TC
    KT = SC // P
    SCALE = float(D) ** -0.5
    with ExitStack() as ctx:
        def sb(name, shape, dt=F32):
            return ctx.enter_context(nc.sbuf_tensor(f"{name}_{tag}", shape, dt))

        def two(name, shape, dt=F32):
            return [sb(f"{name}{i}", shape, dt) for i in range(2)]

        q_hi, q_lo = two("q_hi", [P, KC, P], F32R), two("q_lo", [P, KC, P], F32R)
        probs = sb("probs", [P, SC])
        pT_hi, pT_lo = sb("pT_hi", [P, KT, P], F32R), sb("pT_lo", [P, KT, P], F32R)
        neg_max, total, inverse = two("neg_max", [P, 1]), two("total", [P, 1]), two("inverse", [P, 1])
        if phi is not None:
            phi_sb, biased = two("phi", [P, SC]), sb("biased", [P, SC])
        if out_weight is not None:
            wo_raw, wo_hi, wo_lo = split_weights(nc, g, ctx, tag, "wo", [P, KC, D])
            attn = sb("attn", [P, D])
            aT_hi, aT_lo = sb("aT_hi", [P, KC, P], F32R), sb("aT_lo", [P, KC, P], F32R)
        scores = ctx.enter_context(nc.psum_tensor(f"scores_{tag}", [P, 2, SC], F32))
        turned = ctx.enter_context(nc.psum_tensor(f"turned_p_{tag}", [P, KT, P], F32))
        out = ctx.enter_context(nc.psum_tensor(f"attn_out_{tag}", [P, D], F32, ))
        extra = ctx.enter_context(nc.psum_tensor(f"extra_{tag}", [P, 2, D], F32))

        def sem(name):
            return g.sem(f"{name}_{tag}")

        staged, scores_done, max_done, exp_done = sem("staged"), sem("scores_done"), sem("max_done"), sem("exp_done")
        turned_done, pT_hi_done, pT_lo_done, out_done = sem("turned_p_done"), sem("pT_hi_done"), sem("pT_lo_done"), sem("attn_out_done")
        added = sem("added")
        phi_loaded, phi_read = [sem("phi_loaded0"), sem("phi_loaded1")], sem("phi_read")
        wo_loaded, wo_split = sem("wo_loaded"), sem("wo_split")
        attn_done, aT_done, aT_hi_done, aT_lo_done, e_done = sem("attn_done"), sem("aT_done"), sem("aT_hi_done"), sem("aT_lo_done"), sem("e_done")
        dve_steps = sem("attend_steps")

        with nc.Block() as block:
            @block.sync
            def _(sp):
                if out_weight is not None:
                    sp.dma_start(wo_raw[:, :, :], out_weight).then_inc(wo_loaded, 16)
                if phi is not None:
                    for b in range(B):
                        sp.dma_start(phi_sb[b][:, :], phi[b * 4]).then_inc(phi_loaded[b], 16)
                    with sp.Fori(0, 3) as i:
                        for b in range(B):
                            sp.wait_ge(phi_read, 2 * i + b + 1)
                            sp.dma_start(phi_sb[b][:, :], phi[bass.ds(b * 4 + i + 1, 1), :, :].rearrange("o p s -> (o p) s")).then_inc(phi_loaded[b], 16)

            @block.gpsimd
            def _(pool):
                def stage(i, b):
                    t = bass.ds(b * S + i * P, P)
                    own.link(pool.tensor_copy(q_hi[b][:, :, :], f32(g.qT_hi[:, :, t])))
                    own.link(pool.tensor_copy(q_lo[b][:, :, :], f32(g.qT_lo[:, :, t])))

                own = Chain(pool, staged)
                stage(0, 0)
                stage(0, 1)
                with pool.Fori(0, 3) as i:
                    own.loop = 4 * i
                    for b in range(B):
                        pool.wait_ge(scores_done, 2 * i + b + 1)
                        stage(i + 1, b)

            @block.tensor
            def _(pe):
                def take_scores(n, b):
                    pe.wait_ge(staged, 2 * n + 2)
                    for h in range(2):
                        s = slice(b * SC + h * 512, b * SC + (h + 1) * 512)
                        for k in range(KC):
                            last = mm3(pe, scores[:, b, h * 512:(h + 1) * 512], (q_hi[b][:, k, :], q_lo[b][:, k, :]),
                                       (g.kT_hi[:, k, s], g.kT_lo[:, k, s]), k == 0, k == KC - 1)
                    last.then_inc(scores_done, 1)

                def period(n, b, more):
                    pe.wait_ge(exp_done, n + 1)
                    for t in range(KT):
                        last = pe.transpose(turned[:, t, :], probs[:, t * P:(t + 1) * P], g.ident[:, :])
                    last.then_inc(turned_done, 1)
                    if more:
                        take_scores(n + 1, 1 - b)
                    pe.wait_ge(pT_hi_done, n + 1)
                    pe.wait_ge(pT_lo_done, n + 1)
                    for t in range(KT):
                        last = mm3(pe, out[:, :], (pT_hi[:, t, :], pT_lo[:, t, :]),
                                   (g.v_hi[:, b * KT + t, :], g.v_lo[:, b * KT + t, :]), t == 0, t == KT - 1)
                    last.then_inc(out_done, 1)
                    if out_weight is not None:
                        pe.wait_ge(attn_done, n + 1)
                        for k in range(KC):
                            last = pe.transpose(extra[:, 0, k * P:(k + 1) * P], attn[:, k * P:(k + 1) * P], g.ident[:, :])
                        last.then_inc(aT_done, 1)
                        pe.wait_ge(aT_hi_done, n + 1)
                        pe.wait_ge(aT_lo_done, n + 1)
                        for k in range(KC):
                            last = mm3(pe, extra[:, 1, :], (aT_hi[:, k, :], aT_lo[:, k, :]), (wo_hi[:, k, :], wo_lo[:, k, :]), k == 0, k == KC - 1)
                        last.then_inc(e_done, 1)

                if out_weight is not None:
                    pe.wait_ge(wo_split, 2)
                take_scores(0, 0)
                with pe.Fori(0, 3) as i:
                    for b in range(B):
                        period(2 * i + b, b, True)
                period(6, 0, True)
                period(7, 1, False)

            @block.scalar
            def _(act):
                def exponentials(n, b):
                    act.wait_ge(max_done, n + 1)
                    src = biased[:, :] if phi is not None else scores[:, b, :]
                    act.activation(probs[:, :], src, ACT.Exp, bias=neg_max[b][:, :], scale=SCALE, accum_out=total[b][:, :]).then_inc(exp_done, 1)

                def period(n, b, more):
                    act.wait_ge(turned_done, n + 1)
                    act.activation(pT_hi[:, :, :], turned[:, :, :], ACT.Copy).then_inc(pT_hi_done, 1)
                    if more:
                        exponentials(n + 1, 1 - b)
                    if out_weight is not None:
                        act.wait_ge(aT_done, n + 1)
                        act.activation(aT_hi[:, :, :], extra[:, 0, :], ACT.Copy).then_inc(aT_hi_done, 1)

                if out_weight is not None:
                    act.wait_ge(wo_loaded, 16)
                    act.activation(wo_hi[:, :, :], wo_raw[:, :, :], ACT.Copy).then_inc(wo_split, 1)
                exponentials(0, 0)
                with act.Fori(0, 3) as i:
                    for b in range(B):
                        period(2 * i + b, b, True)
                period(6, 0, True)
                period(7, 1, False)

            @block.vector
            def _(dve):
                own = Chain(dve, dve_steps)

                def maximum(n, b, uses):
                    dve.wait_ge(scores_done, n + 1)
                    if phi is not None:
                        dve.wait_ge(phi_loaded[b], 16 * uses)
                        if not (isinstance(n, int) and n == 0):
                            dve.wait_ge(exp_done, n)
                        dve.scalar_tensor_tensor(biased[:, :], phi_sb[b][:, :], g.phi_scale[:, 0:1], scores[:, b, :], ALU.mult, ALU.add).then_inc(phi_read, 1)
                        dve.wait_ge(phi_read, n + 1)
                        own.link(dve.tensor_reduce(neg_max[b][:, :], biased[:, :], X, ALU.max))
                    else:
                        own.link(dve.tensor_reduce(neg_max[b][:, :], scores[:, b, :], X, ALU.max))
                    dve.tensor_scalar(neg_max[b][:, :], neg_max[b][:, :], -SCALE, None, ALU.mult).then_inc(max_done, 1)

                def period(n, b, i, more, uses):
                    dve.wait_ge(pT_hi_done, n + 1)
                    dve.tensor_tensor(pT_lo[:, :, :], turned[:, :, :], f32(pT_hi[:, :, :]), ALU.subtract).then_inc(pT_lo_done, 1)
                    if more:
                        maximum(n + 1, 1 - b, uses)
                    own.link(dve.reciprocal(inverse[b][:, :], total[b][:, :]))
                    dve.wait_ge(out_done, n + 1)
                    c = bass.ds(b * 4 + i, 1)
                    xc = g.x[:, c, :].rearrange("p o e -> p (o e)")
                    if out_weight is None:
                        own.link(dve.scalar_tensor_tensor(xc, out[:, :], inverse[b][:, :], xc, ALU.mult, ALU.add))
                    else:
                        dve.tensor_scalar(attn[:, :], out[:, :], inverse[b][:, :], None, ALU.mult).then_inc(attn_done, 1)
                        dve.wait_ge(aT_hi_done, n + 1)
                        dve.tensor_tensor(aT_lo[:, :, :], extra[:, 0, :], f32(aT_hi[:, :, :]), ALU.subtract).then_inc(aT_lo_done, 1)
                        dve.wait_ge(e_done, n + 1)
                        own.link(dve.scalar_tensor_tensor(xc, extra[:, 1, :], g.share0[:, b:b + 1], xc, ALU.mult, ALU.add))

                if out_weight is not None:
                    dve.wait_ge(wo_split, 1)
                    dve.tensor_tensor(wo_lo[:, :, :], wo_raw[:, :, :], f32(wo_hi[:, :, :]), ALU.subtract).then_inc(wo_split, 1)
                if phi is not None:
                    own.link(dve.tensor_tensor(g.x[:, :, :], g.x[:, :, :], row(g, "bv2").rearrange("p (o e) -> p o e", o=1).to_broadcast([P, TC, D]), ALU.add))
                maximum(0, 0, 1)
                per = 6
                n0 = own.n
                with dve.Fori(0, 3) as i:
                    own.loop = per * i
                    period(2 * i, 0, i, True, i + 1)
                    period(2 * i + 1, 1, i, True, i + 2)
                assert own.n == n0 + per
                own.loop = per * 2
                period(6, 0, 3, True, 4)
                period(7, 1, 3, False, None)


def l3_mlp_phase(nc, g, d):
    with ExitStack() as ctx:
        def sb(name, shape, dt=F32):
            return ctx.enter_context(nc.sbuf_tensor(name, shape, dt))

        w_raw, w_hi, w_lo = split_weights(nc, g, ctx, "m3", "w12_3", [P, 2, KC, D])
        wg_raw, wg_hi, wg_lo = split_weights(nc, g, ctx, "m3", "wg3", [P, KC, 2])
        first_hi, first_lo = sb("first_hi", [P, B, KC, P], F32R), sb("first_lo", [P, B, KC, P], F32R)
        hidden = sb("hidden3", [P, KC, T])
        h_hi, h_lo = sb("h3_hi", [P, KC, T], F32R), sb("h3_lo", [P, KC, T], F32R)
        share1, vote = sb("share1", [P, B]), sb("vote", [P, B, 2])
        biased = sb("biased3", [P, 2, D])
        acc = ctx.enter_context(nc.psum_tensor("acc_m3", [P, 4, 512], F32))
        out = ctx.enter_context(nc.psum_tensor("out_m3", [P, 2, 2, D], F32))
        votes = ctx.enter_context(nc.psum_tensor("votes", [P, B, 2], F32))
        loaded, hi_done, lo_done = g.sem("m3_loaded"), g.sem("m3_hi_done"), g.sem("m3_lo_done")
        first_done, votes_done, acc_done = g.sem("first_done"), g.sem("votes_done"), g.sem("acc3_done")
        gelu_done, h_hi_done, h_lo_done = g.sem("gelu_done"), g.sem("h3_hi_done"), g.sem("h3_lo_done")
        out_done, out_read, dve_steps = g.sem("out3_done"), g.sem("out3_read"), g.sem("m3_dve_steps")
        tiles = [(fc, h) for h in range(2) for fc in range(KC)]
        with nc.Block() as block:
            @block.sync
            def _(sp):
                sp.dma_start(w_raw[:, :, :, :], d["w12_3"]).then_inc(loaded, 16)
                sp.dma_start(wg_raw[:, :, :], d["wg3"]).then_inc(loaded, 16)

            @block.gpsimd
            def _(pool):
                own = Chain(pool, first_done)
                for b in range(B):
                    t = slice(b * S, b * S + 1)
                    own.link(pool.tensor_copy(first_hi[:, b, :, :], f32(g.xnT_hi[:, :, t]).to_broadcast([P, KC, P])))
                    own.link(pool.tensor_copy(first_lo[:, b, :, :], f32(g.xnT_lo[:, :, t]).to_broadcast([P, KC, P])))

            @block.scalar
            def _(act):
                act.wait_ge(loaded, 32)
                act.activation(w_hi[:, :, :, :], w_raw[:, :, :, :], ACT.Copy).then_inc(hi_done, 1)
                act.activation(wg_hi[:, :, :], wg_raw[:, :, :], ACT.Copy).then_inc(hi_done, 1)
                for n, (fc, h) in enumerate(tiles):
                    t = slice(h * 512, (h + 1) * 512)
                    act.wait_ge(acc_done, n + 1)
                    act.activation(hidden[:, fc, t], acc[:, n, :], ACT.Gelu, bias=g.bias_cols[:, B1_3, fc:fc + 1]).then_inc(gelu_done, 1)
                    act.wait_ge(gelu_done, n + 1)
                    act.activation(h_hi[:, fc, t], hidden[:, fc, t], ACT.Copy).then_inc(h_hi_done, 1)

            @block.tensor
            def _(pe):
                pe.wait_ge(lo_done, 2)
                for n, (fc, h) in enumerate(tiles):
                    f, t = slice(fc * P, (fc + 1) * P), slice(h * 512, (h + 1) * 512)
                    for k in range(KC):
                        last = mm3(pe, acc[:, n, :], (w_hi[:, 0, k, f], w_lo[:, 0, k, f]),
                                   (g.xnT_hi[:, k, t], g.xnT_lo[:, k, t]), k == 0, k == KC - 1)
                    last.then_inc(acc_done, 1)
                pe.wait_ge(first_done, 2 * B)
                for b in range(B):
                    for k in range(KC):
                        last = mm3(pe, votes[:, b, :], (first_hi[:, b, k, :], first_lo[:, b, k, :]), (wg_hi[:, k, :], wg_lo[:, k, :]),
                                   b == 0 and k == 0, k == KC - 1)
                last.then_inc(votes_done, 1)
                for m in range(TC // 2):
                    pe.wait_ge(h_lo_done, 2 * (m // 2 + 1))
                    if m >= 2:
                        pe.wait_ge(out_read, m - 1)
                    for j in range(2):
                        t = slice((2 * m + j) * P, (2 * m + j + 1) * P)
                        for k in range(KC):
                            last = mm3(pe, out[:, m % 2, j, :], (h_hi[:, k, t], h_lo[:, k, t]), (w_hi[:, 1, k, :], w_lo[:, 1, k, :]),
                                       j == 0 and k == 0, k == KC - 1)
                    last.then_inc(out_done, 1)

            @block.vector
            def _(dve):
                own = Chain(dve, dve_steps)
                dve.wait_ge(hi_done, 2)
                dve.tensor_tensor(w_lo[:, :, :, :], w_raw[:, :, :, :], f32(w_hi[:, :, :, :]), ALU.subtract).then_inc(lo_done, 1)
                dve.tensor_tensor(wg_lo[:, :, :], wg_raw[:, :, :], f32(wg_hi[:, :, :]), ALU.subtract).then_inc(lo_done, 1)
                for n, (fc, h) in enumerate(tiles):
                    t = slice(h * 512, (h + 1) * 512)
                    dve.wait_ge(h_hi_done, n + 1)
                    dve.tensor_tensor(h_lo[:, fc, t], hidden[:, fc, t], f32(h_hi[:, fc, t]), ALU.subtract).then_inc(h_lo_done, 1)
                dve.wait_ge(votes_done, 1)
                own.link(dve.tensor_copy(vote[:, :, :], votes[:, :, :]))
                own.link(dve.tensor_tensor(g.share0[:, :], vote[:, :, 0], vote[:, :, 1], ALU.is_ge))
                own.link(dve.tensor_scalar(share1[:, :], g.share0[:, :], -1.0, 1.0, ALU.mult, ALU.add))
                for m in range(TC // 2):
                    b = m // 2
                    dve.wait_ge(out_done, m + 1)
                    own.step(dve.tensor_tensor(biased[:, :, :], out[:, m % 2, :, :], row(g, "b2_3").rearrange("p (o e) -> p o e", o=1).to_broadcast([P, 2, D]), ALU.add))
                    own.wait()
                    dve.scalar_tensor_tensor(g.x[:, 2 * m:2 * m + 2, :], biased[:, :, :], share1[:, b:b + 1], g.x[:, 2 * m:2 * m + 2, :], ALU.mult, ALU.add).then_inc(out_read, 1)
                    dve.wait_ge(out_read, m + 1)


def int8_phase(nc, g, d, out_dram):
    with ExitStack() as ctx:
        def sb(name, shape, dt=F32):
            return ctx.enter_context(nc.sbuf_tensor(f"{name}_i8", shape, dt))

        xn = sb("xn", [P, TC, D])
        stats, mv, rstd = sb("stats", [P, TC, 6]), sb("mv", [P, TC, 2]), sb("rstd", [P, TC])
        step, inverse = sb("step", [P, TC]), sb("inverse", [P, TC])
        qT = sb("qT", [P, KC, T], BF16)
        scaled = sb("scaled", [P, TC, D])
        turned = ctx.enter_context(nc.psum_tensor("turned_i8", [P, 2, KC, 4 * P], F32))
        acc = ctx.enter_context(nc.psum_tensor("acc_i8", [P, TC // 2, 2, D], F32))
        own_steps, normal_done, rounded_done = g.sem("i8_steps"), g.sem("i8_normal_done"), g.sem("rounded_done")
        turned_done, qT_done, acc_done = g.sem("i8_turned_done"), g.sem("qT_done"), g.sem("i8_acc_done")
        x_done, stored = g.sem("x_done"), g.sem("stored")
        moments_done, deviation_done = g.sem("i8_moments_done"), g.sem("i8_deviation_done")
        with nc.Block() as block:
            @block.vector
            def _(dve):
                own = Chain(dve, own_steps)
                normalise_steps(dve, own, g, stats, mv, rstd, xn, moments_done, deviation_done, normal_done)
                dve.wait_ge(normal_done, TC)
                own.link(dve.tensor_reduce(step[:, :], xn[:, :, :], X, ALU.max, apply_absolute_value=True))
                own.link(dve.tensor_scalar(step[:, :], step[:, :], 1e-12, 1.0 / INT8_MAX, ALU.max, ALU.mult))
                own.link(dve.reciprocal(inverse[:, :], step[:, :]))
                for c in range(TC):
                    own.step(dve.tensor_scalar(xn[:, c, :], xn[:, c, :], inverse[:, c:c + 1], ROUND, ALU.mult, ALU.add))
                for h in range(2):
                    part = xn[:, 4 * h:4 * h + 4, :]
                    own.wait()
                    own.link(dve.tensor_scalar(part, part, ROUND, INT8_MAX, ALU.subtract, ALU.min))
                    dve.tensor_scalar(part, part, -INT8_MAX, None, ALU.max).then_inc(rounded_done, 1)
                for m in range(TC // 2):
                    dve.wait_ge(acc_done, m + 1)
                    for j in range(2):
                        c = 2 * m + j
                        own.step(dve.scalar_tensor_tensor(scaled[:, c, :], acc[:, m, j, :], step[:, c:c + 1], g.rhs_scale[:, :], ALU.mult, ALU.mult))
                    own.wait()
                    dve.tensor_tensor(g.x[:, 2 * m:2 * m + 2, :], g.x[:, 2 * m:2 * m + 2, :], scaled[:, 2 * m:2 * m + 2, :], ALU.add).then_inc(x_done, 1)

            @block.tensor
            def _(pe):
                for h in range(2):
                    pe.wait_ge(rounded_done, h + 1)
                    for c in range(4):
                        for k in range(KC):
                            last = pe.transpose(turned[:, h, k, c * P:(c + 1) * P], xn[:, 4 * h + c, k * P:(k + 1) * P], g.ident[:, :])
                    last.then_inc(turned_done, 1)
                for m in range(TC // 2):
                    pe.wait_ge(qT_done, m // 2 + 1)
                    for j in range(2):
                        t = slice((2 * m + j) * P, (2 * m + j + 1) * P)
                        for k in range(KC):
                            last = pe.matmul(acc[:, m, j, :], qT[:, k, t], g.rhs_q[:, k, :], start=j == 0 and k == 0,
                                             stop=k == KC - 1, skip_group_check=True)
                    last.then_inc(acc_done, 1)

            @block.scalar
            def _(act):
                deviation(act, g, mv, rstd, moments_done, deviation_done)
                for h in range(2):
                    act.wait_ge(turned_done, h + 1)
                    act.activation(qT[:, :, h * 512:(h + 1) * 512], turned[:, h, :, :], ACT.Copy).then_inc(qT_done, 1)

            @block.sync
            def _(sp):
                for m in range(TC // 2):
                    sp.wait_ge(x_done, m + 1)
                    sp.dma_start(out_dram[:, 2 * m:2 * m + 2, :], g.x[:, 2 * m:2 * m + 2, :]).then_inc(stored, 16)
                sp.wait_ge(stored, 16 * (TC // 2))


def four_layers(nc, d, out_dram, upto=99):
    g = Shared()
    with ExitStack() as ctx:
        used = []

        def sem(name):
            used.append(nc.alloc_semaphore(name=name))
            return used[-1]

        g.sem = sem
        allocate_shared(nc, ctx, g)
        g.k_parts = nc.dram_tensor("k_parts", [3, B * D, SC], BF16, kind="Internal").ap()
        g.q_parts = nc.dram_tensor("q_parts", [3, B * D, S], BF16, kind="Internal").ap()
        load_phase(nc, g, d)

        with ExitStack() as held:
            g.v0 = held.enter_context(nc.sbuf_tensor("v0", [P, B, GROUPS, SC // P, HG * HD], F32))
            g.v0_done = g.sem("v0_done")
            with ExitStack() as turned:
                allocate_turned(nc, turned, g, "n0")
                normalise_phase(nc, g, "n0")
                l0_project_phase(nc, g, d)
            g.avs = held.enter_context(nc.sbuf_tensor("avs", [P, B * GROUPS, S], F32))
            l0_output_buffers(nc, held, g)
            l0_attention_phase(nc, g, d)
            l0_output_phase(nc, g, d)
        if upto < 1:
            return store(nc, g, out_dram)

        with ExitStack() as turned:
            allocate_turned(nc, turned, g, "n1")
            g.cw = turned.enter_context(nc.sbuf_tensor("cw0", [P, TC, U0], F32))
            gated_layer_phase(nc, g, d, "l0", U0, d["w_units0"], l0_router)
        if upto < 2:
            return store(nc, g, out_dram)

        with ExitStack() as turned:
            allocate_turned(nc, turned, g, "n2")
            normalise_phase(nc, g, "n2")
            l1_shift_phase(nc, g, d)
        if upto < 3:
            return store(nc, g, out_dram)

        with ExitStack() as turned:
            allocate_turned(nc, turned, g, "n3")
            g.select = turned.enter_context(nc.sbuf_tensor("select_sb", [P, (U1 + 1) // 2, P], BF16))
            g.cwT = turned.enter_context(nc.sbuf_tensor("cwT", [P, T], F32))
            g.cw_partsT = turned.enter_context(nc.sbuf_tensor("cw_partsT", [P, 2, T], BF16))
            normalise_phase(nc, g, "n3")
            l1_router_phase(nc, g, d)
            l1_units_phase(nc, g, d)
        if upto < 4:
            return store(nc, g, out_dram)

        def allocate_kqv(held, tag):
            g.kT_hi, g.kT_lo = [held.enter_context(nc.sbuf_tensor(f"kT_{h}_{tag}", [P, KC, CT], F32R)) for h in ("hi", "lo")]
            g.qT_hi, g.qT_lo = [held.enter_context(nc.sbuf_tensor(f"qT_{h}_{tag}", [P, KC, T], F32R)) for h in ("hi", "lo")]
            g.v_hi, g.v_lo = [held.enter_context(nc.sbuf_tensor(f"v_{h}_{tag}", [P, CT // P, D], F32R)) for h in ("hi", "lo")]

        nc.clear_and_free_semaphores(used)
        used.clear()
        nc.all_engine_barrier()
        with ExitStack() as held:
            allocate_kqv(held, "l2")
            with ExitStack() as turned:
                allocate_turned(nc, turned, g, "n4")
                normalise_phase(nc, g, "n4")
                project_phase(nc, g, d, "p2", d["wqkv2"], BQ2, BK2)
            attend_phase(nc, g, d, "a2", d["fside"], None)
        if upto < 5:
            return store(nc, g, out_dram)

        with ExitStack() as turned:
            allocate_turned(nc, turned, g, "n5")
            g.cw = turned.enter_context(nc.sbuf_tensor("cw2", [P, TC, U2], F32))
            gated_layer_phase(nc, g, d, "l2", U2, d["w_units2"], l2_router)
        if upto < 6:
            return store(nc, g, out_dram)

        with ExitStack() as held:
            g.share0 = held.enter_context(nc.sbuf_tensor("share0", [P, B], F32))
            allocate_kqv(held, "l3")
            with ExitStack() as turned:
                allocate_turned(nc, turned, g, "n6")
                normalise_phase(nc, g, "n6")
                l3_mlp_phase(nc, g, d)
                project_phase(nc, g, d, "p3", d["wqkv3"], None, None)
            attend_phase(nc, g, d, "a3", None, d["wo3"])
        if upto < 7:
            return store(nc, g, out_dram)

        int8_phase(nc, g, d, out_dram)


def store(nc, g, out_dram):
    stored = g.sem("debug_stored")
    with nc.Block() as block:
        @block.sync
        def _(sp):
            sp.dma_start(out_dram, g.x[:, :, :]).then_inc(stored, 16)
            sp.wait_ge(stored, 16)



def _chunked(w):
    return w.reshape(w.shape[0] // P, P, *w.shape[1:]).swapaxes(0, 1)


def _arrange(i):
    a = {}
    a["x"] = _chunked(i["x"].reshape(T, D))
    a["ctxT"] = _chunked(i["ctx_1024"].reshape(CT, D).T)
    a["fside"] = i["fside_BxSxS2_0"].reshape(TC, P, SC)
    a["rhsT"] = _chunked(i["L3_ffn_rhs"].T)
    a["ident"] = np.eye(P, dtype=np.float32)
    a["bias_cols"] = np.stack([i[n].reshape(KC, P).T for n in
                               ("L0_xattn_bq", "L0_xattn_bk", "L2_xattn_bq", "L2_xattn_bk", "L3_xattn_b1")], axis=1)
    rows = [i[n] for n in ("L0_xattn_bv", "L1_xattn_b", "L1_ffn_router_b", "L2_xattn_bv", "L2_ffn_expert_bias", "L3_xattn_b2")]
    a["bias_rows"] = np.broadcast_to(np.concatenate(rows)[None], (P, NROWS))
    betas = np.stack([np.asarray(i[f"L2_xattn_beta_{n}"]).reshape(()) for n in ("risk", "prio", "impl")])
    a["betas"] = np.broadcast_to(betas[None], (P, 3))

    a["wqkv0"] = np.stack([_chunked(i[f"L0_xattn_W{n}"].T) for n in "qkv"], axis=1)
    wo = np.zeros((GROUPS, HG, 32, D), np.float32)
    wo[:, :, :HD, :] = i["L0_xattn_Wo"].T.reshape(GROUPS, HG, HD, D)
    wo[0, 0, HD, :] = i["L0_xattn_bo"]
    a["wo0"] = wo.reshape(GROUPS, P, D).swapaxes(0, 1)
    spread = np.zeros((HG, P), np.float32)
    for q in range(HG):
        spread[q, 32 * q:32 * q + 32] = 1.0
    a["spread"] = spread
    a["wr0"] = _chunked(np.concatenate([i["L0_ffn_w_router"], i["L0_ffn_w_gating"]], axis=1))

    def units(gate, up, down):
        out = []
        for f in range(0, gate.shape[1], FU):
            out.append(np.stack([_chunked(gate[:, f:f + FU]), _chunked(up[:, f:f + FU]), _chunked(down[f:f + FU])], axis=1))
        return out

    u0 = []
    for e in range(E0):
        u0 += units(i["L0_ffn_w_gate"][e], i["L0_ffn_w_up"][e], i["L0_ffn_w_down"][e])
    a["w_units0"] = np.stack(u0)

    w = i["L1_xattn_W"]
    a["wx1"] = np.stack([_chunked(w[:, :D].T), _chunked(w[:, D:].T)], axis=1)
    a["wr1"] = _chunked(i["L1_ffn_router_w"])
    w1 = [None] * U1
    shared = [(s, f) for s in range(ES1) for f in range(0, HS1, P)]
    for n in range(U1):
        pair, half = divmod(n, 2)
        if n < PAIRS1:
            e = half * (E1 // 2) + 2 * pair
            up = np.concatenate([i["L1_ffn_w1"][e], i["L1_ffn_w1"][e + 1]], axis=1)
            down = i["L1_ffn_w2"][e:e + 2].reshape(P, D)
            b1 = i["L1_ffn_b1"][e:e + 2].reshape(P, 1)
        else:
            s, f = shared[n - PAIRS1]
            up, down = i["L1_ffn_sw1"][s][:, f:f + P], i["L1_ffn_sw2"][s][f:f + P]
            b1 = i["L1_ffn_sb1"][s, f:f + P].reshape(P, 1)
        w1[n] = np.concatenate([_chunked(up).reshape(P, D), b1, down], axis=1)
    a["w1"] = np.stack(w1)
    a["b2"] = np.concatenate([i["L1_ffn_b2"], i["L1_ffn_sb2"]], axis=0)
    select = np.zeros((P, (U1 + 1) // 2, P), np.float32)
    for pair in range(U1 // 2):
        for part in range(3):
            if pair < PAIRS1 // 2:
                for j in range(2):
                    select[part * (E1 // 2) + 2 * pair + j, pair, j * H1:(j + 1) * H1] = 1.0
        if pair >= PAIRS1 // 2:
            select[3 * (E1 // 2), pair, :] = 1.0
    a["select"] = select.astype(mybir.dt.np(BF16))
    a["wqkv2"] = np.stack([_chunked(i[f"L2_xattn_W{n}"].T) for n in "qkv"], axis=1)
    a["wr2"] = _chunked(i["L2_ffn_router_w"].T)
    u2 = []
    for e in range(E2):
        w12 = i["L2_ffn_w12"][e]
        u2 += units(w12[:H2].T, w12[H2:].T, i["L2_ffn_w3"][e].T)
    u2 += units(i["L2_ffn_shared_w1"].T, i["L2_ffn_shared_w2"].T, i["L2_ffn_shared_w3"].T)
    a["w_units2"] = np.stack(u2)
    a["wqkv3"] = np.stack([_chunked(i[f"L3_xattn_W{n}"]) for n in "qkv"], axis=1)
    a["wo3"] = _chunked(i["L3_xattn_Wo"])
    a["w12_3"] = np.stack([_chunked(i["L3_xattn_W1"]), _chunked(i["L3_xattn_W2"])], axis=1)
    a["wg3"] = _chunked(i["L3_xattn_Wg"])
    return {k: np.ascontiguousarray(v) for k, v in a.items()}


def kernel(**inputs):
    import concourse.bacc as bacc
    from concourse.bass_utils import run_bass_kernel_spmd

    arrays = _arrange({k: np.asarray(v) for k, v in inputs.items()})
    nc = bacc.Bacc("TRN2", target_bir_lowering=False, num_devices=1)
    d = {k: nc.dram_tensor(k, v.shape, mybir.dt.from_np(v.dtype), kind="ExternalInput").ap() for k, v in arrays.items()}
    out = nc.dram_tensor("out", (P, TC, D), F32, kind="ExternalOutput").ap()
    four_layers(nc, d, out)
    r = run_bass_kernel_spmd(nc, [arrays], core_ids=[0])
    return r.results[0]["out"].swapaxes(0, 1).reshape(B, S, D)
```

```python
from contextlib import ExitStack

import numpy as np

import concourse.bass as bass
from concourse import mybir

F32 = mybir.dt.float32
F32R = mybir.dt.float32r
BF16 = mybir.dt.bfloat16
ALU = mybir.AluOpType
ACT = mybir.ActivationFunctionType
X = mybir.AxisListType.X

P = 128
B, S, D = 2, 512, 256
SC = 1024
T = B * S
TC = T // P
CT = B * SC
KC = D // P
EPS = 1e-5

HEADS, HD = 16, 16
HG = 4
GROUPS = HEADS // HG
PART_PAIRS = [(0, 0), (1, 0), (2, 0), (0, 1), (1, 1), (0, 2)]
STACK_SOURCES = [[(range(0, 3), 0, 3), (range(3, 5), 0, 2), (range(5, 6), 0, 1)],
                 [(range(0, 3), 0, 1), (range(3, 5), 1, 1), (range(5, 6), 2, 1)]]
MAXROW = HD * len(PART_PAIRS)

E0, F0 = 8, 1024
FU = 256
U0 = E0 * F0 // FU
E1, H1, K1 = 64, 64, 8
ES1, HS1 = 2, 512
PAIRS1 = E1 // 2
U1 = PAIRS1 + ES1 * HS1 // P
E2, H2 = 8, 256
FS2 = 1024
U2 = E2 + FS2 // FU
NEG = -1.0e30
ROUND = 1.5 * 2.0 ** 23
INT8_MAX = 127.0

BQ0, BK0, BQ2, BK2, B1_3 = range(5)
ROWS = {}
_at = 0
for _name, _n in (("b_x1", D), ("rb1", E1), ("bv2", D), ("eb2", E2), ("b2_3", D)):
    ROWS[_name] = (_at, _at + _n)
    _at += _n
NROWS = _at


def f32(ap):
    return ap.bitcast(F32)


def mm3(pe, out, lhs, rhs, start, stop):
    pe.matmul(out, lhs[0], rhs[0], start=start, stop=False, skip_group_check=True)
    pe.matmul(out, lhs[0], rhs[1], start=False, stop=False, skip_group_check=True)
    return pe.matmul(out, lhs[1], rhs[0], start=False, stop=stop, skip_group_check=True)


class Chain:

    def __init__(self, eng, sem):
        self.eng, self.sem, self.n, self.loop = eng, sem, 0, 0

    def step(self, ins):
        ins.then_inc(self.sem, 1)
        self.n += 1

    def wait(self):
        self.eng.wait_ge(self.sem, self.loop + self.n)

    def link(self, ins):
        self.step(ins)
        self.wait()


class Shared:
    pass


def allocate_shared(nc, ctx, g):
    def sb(name, shape, dt=F32):
        return ctx.enter_context(nc.sbuf_tensor(f"{name}_sb", shape, dt))

    g.x = sb("x", [P, TC, D])
    g.stats = sb("stats", [P, TC, 6])
    g.ctxT_hi = sb("ctxT_hi", [P, KC, CT], F32R)
    g.ctxT_lo = sb("ctxT_lo", [P, KC, CT], F32R)
    g.ctx_sum = sb("ctx_sum", [P, KC, B])
    g.ident = sb("ident", [P, P])
    g.ident16 = sb("ident16", [P, P], BF16)
    g.bias_cols = sb("bias_cols", [P, 5, KC])
    g.bias_rows = sb("bias_rows", [P, NROWS])
    g.rhs_q = sb("rhs_q", [P, KC, D], BF16)
    g.rhs_scale = sb("rhs_scale", [P, D])
    g.betas = sb("betas", [P, 3])
    g.phi_scale = sb("phi_scale", [P, 1])
    g.eps = sb("eps", [P, 1])


def row(g, name):
    a, b = ROWS[name]
    return g.bias_rows[:, a:b]


def allocate_turned(nc, ctx, g, tag):
    g.xnT_hi = ctx.enter_context(nc.sbuf_tensor(f"xnT_hi_{tag}", [P, KC, T], F32R))
    g.xnT_lo = ctx.enter_context(nc.sbuf_tensor(f"xnT_lo_{tag}", [P, KC, T], F32R))


def deviation(act, g, mv, rstd, moments_done, deviation_done):
    act.wait_ge(moments_done, TC)
    act.activation(rstd[:, :], mv[:, :, 1], ACT.Sqrt, bias=g.eps[:, 0:1]).then_inc(deviation_done, 1)


def take_stats(dve, g, chunks):
    for c in chunks:
        last = dve.bn_stats(g.stats[:, c, :], g.x[:, c, :])
    return last


def take_moments(dve, g, mv, moments_done):
    for c in range(TC):
        dve.bn_aggr(mv[:, c, :], g.stats[:, c, :]).then_inc(moments_done, 1)


def invert_deviation(dve, own, rstd, deviation_done):
    dve.wait_ge(deviation_done, 1)
    own.link(dve.reciprocal(rstd[:, :], rstd[:, :]))


def apply_norm(dve, g, mv, rstd, xn, normal_done, chunks):
    for c in chunks:
        dve.tensor_scalar(xn[:, c, :], g.x[:, c, :], mv[:, c, 0:1], rstd[:, c:c + 1],
                          ALU.subtract, ALU.mult).then_inc(normal_done, 1)


def normaliser(nc, ctx, g, tag, turned):
    def sb(name, shape, dt=F32):
        return ctx.enter_context(nc.sbuf_tensor(f"{name}_{tag}", shape, dt))

    xn = sb("xn", [P, TC, D])
    mv, rstd = sb("mv", [P, TC, 2]), sb("rstd", [P, TC])
    own_steps, normal_done = g.sem(f"norm_steps_{tag}"), g.sem(f"normal_done_{tag}")
    turned_done = g.sem(f"turned_done_{tag}")
    moments_done, deviation_done = g.sem(f"moments_done_{tag}"), g.sem(f"deviation_done_{tag}")
    n = Shared()
    n.hi_done, n.lo_done = g.sem(f"norm_hi_done_{tag}"), g.sem(f"norm_lo_done_{tag}")
    own = None

    def moments(dve):
        nonlocal own
        own = Chain(dve, own_steps)
        take_moments(dve, g, mv, moments_done)

    def invert(dve):
        dve.wait_ge(moments_done, TC)
        invert_deviation(dve, own, rstd, deviation_done)

    def apply(dve, h):
        apply_norm(dve, g, mv, rstd, xn, normal_done, range(4 * h, 4 * h + 4))

    def low(dve, h):
        for k in range(KC):
            dve.wait_ge(n.hi_done, h * KC + k + 1)
            dve.tensor_tensor(g.xnT_lo[:, k, h * 512:(h + 1) * 512], turned[:, h, k, :],
                              f32(g.xnT_hi[:, k, h * 512:(h + 1) * 512]), ALU.subtract).then_inc(n.lo_done, 1)

    def on_vector(dve):
        moments(dve)
        invert(dve)
        apply(dve, 0)
        apply(dve, 1)
        low(dve, 0)
        low(dve, 1)

    def turn(pe, h):
        for c in range(4 * h, 4 * h + 4):
            pe.wait_ge(normal_done, c + 1)
            for k in range(KC):
                last = pe.transpose(turned[:, h, k, (c % 4) * P:(c % 4 + 1) * P],
                                    xn[:, c, k * P:(k + 1) * P], g.ident[:, :])
        last.then_inc(turned_done, 1)

    def on_tensor(pe):
        turn(pe, 0)
        turn(pe, 1)

    def root(act):
        deviation(act, g, mv, rstd, moments_done, deviation_done)

    def high(act, h):
        act.wait_ge(turned_done, h + 1)
        for k in range(KC):
            act.activation(g.xnT_hi[:, k, h * 512:(h + 1) * 512], turned[:, h, k, :],
                           ACT.Copy).then_inc(n.hi_done, 1)

    def on_scalar(act):
        root(act)
        high(act, 0)
        high(act, 1)

    def wait_half(pe, h):
        pe.wait_ge(n.hi_done, KC * (h + 1))
        pe.wait_ge(n.lo_done, KC * (h + 1))

    n.on_vector, n.on_tensor, n.on_scalar, n.wait_half = on_vector, on_tensor, on_scalar, wait_half
    n.moments, n.invert, n.apply, n.low, n.turn, n.root, n.high = moments, invert, apply, low, turn, root, high
    return n


def split_weights(nc, g, ctx, tag, name, shape):
    def sb(n, dt):
        return ctx.enter_context(nc.sbuf_tensor(f"{name}_{n}_{tag}", shape, dt))

    return sb("raw", F32), sb("hi", F32R), sb("lo", F32R)


VALUE_TILES = CT // P // 2


def half_value_tile(pe, g, banks, m, j):
    if m >= 4:
        pe.wait_ge(g.v0_done, m - 3)
    t = slice((2 * m + j) * P, (2 * m + j + 1) * P)
    for k in range(KC):
        last = mm3(pe, banks[:, m % 4, j * D:(j + 1) * D], (g.ctxT_hi[:, k, t], g.ctxT_lo[:, k, t]),
                   (g.w0_hi[:, 2, k, :], g.w0_lo[:, 2, k, :]), j == 0 and k == 0, k == KC - 1)
    if j == 1:
        last.then_inc(g.values_done, 1)


def store_values(act, g, banks, m):
    act.wait_ge(g.values_done, m + 1)
    b, t = divmod(2 * m, SC // P)
    act.activation(g.v0[b][:, :, t:t + 2, :].rearrange("p g t e -> p t g e"),
                   banks[:, m % 4, :].rearrange("p (t g e) -> p t g e", t=2, g=GROUPS), ACT.Copy).then_inc(g.v0_done, 1)


def l0_front_phase(nc, g, d):
    Q, K, V = range(3)
    KEY_CHUNKS = CT // 512
    STORES = 16 * len(STACK_SOURCES[K])
    with ExitStack() as ctx:
        def sb(name, shape, dt=F32):
            return ctx.enter_context(nc.sbuf_tensor(name, shape, dt))

        w_raw = sb("wqkv0_raw", [P, 3, KC, D])
        ctxT = sb("ctxT_raw", [P, 2, KC, 512])
        rest = sb("kq_rest", [P, 2, 512])
        parts, parts_stored = g.kq_parts, g.parts_stored
        acc = ctx.enter_context(nc.psum_tensor("acc_p0", [P, 4, 512], F32))
        turned = ctx.enter_context(nc.psum_tensor("turned_n0", [P, 2, KC, 512], F32))
        turned_banks = turned[:, :, :, :].rearrange("p h k s -> p (h k) s")
        norm = normaliser(nc, ctx, g, "n0", turned)
        wk_loaded, wq_loaded, wv_loaded, x_loaded = g.sem("wk_loaded"), g.sem("wq_loaded"), g.sem("wv_loaded"), g.sem("x_loaded")
        ctx_loaded = [g.sem(f"ctx_loaded{i}") for i in range(KEY_CHUNKS)]
        stats_done = g.sem("stats_done")
        early_loaded, consts_loaded, eps_set = g.sem("early_consts_loaded"), g.sem("consts_loaded"), g.sem("eps_set")
        ctx_hi_done, ctx_lo_done = g.sem("ctx_hi_done"), g.sem("ctx_lo_done")
        w_hi_done, w_lo_done = g.sem("w0_hi_done"), g.sem("w0_lo_done")
        tile_done, part1_done = g.sem("kq_tile_done"), g.sem("kq_part1_done")
        rest_done, part2_done, part3_done = g.sem("kq_rest_done"), g.sem("kq_part2_done"), g.sem("kq_part3_done")
        tiles = [(which, fc, b, h) for which, b, h in ((K, 0, 0), (K, 0, 1), (K, 1, 0), (Q, 0, 0), (K, 1, 1), (Q, 1, 0))
                 for fc in range(KC)]
        NT, EARLY, LATE = len(tiles), 8, 2
        SLOTS = len(parts_stored)

        def stores_of(n):
            return [STORES * ((n - i + SLOTS - 1) // SLOTS) for i in range(SLOTS)]

        def store_parts(sp, n):
            which, fc, b, h = tiles[n]
            stack = (g.k_stacks if which == K else g.q_stacks)[b, fc, :, :, h * 512:(h + 1) * 512]
            for slots, first, count in STACK_SOURCES[which]:
                source = parts[:, n % SLOTS, first:first + count, :]
                if count < len(slots):
                    source = parts[:, n % SLOTS, first, :].rearrange("p (o s) -> p o s", o=1).to_broadcast([P, len(slots), 512])
                sp.dma_start(stack[slots[0]:slots[-1] + 1, :, :].rearrange("t f s -> f t s"), source).then_inc(parts_stored[n % SLOTS], 16)

        def store_late(sp):
            for n in range(NT - LATE, NT):
                store_parts(sp, n)

        g.store_late, g.all_stores = store_late, stores_of(NT)

        def bias_of(n):
            which, fc = tiles[n][:2]
            return g.bias_cols[:, BQ0 if which == Q else BK0, fc:fc + 1]

        with nc.Block() as block:
            @block.sync
            def _(sp):
                sp.dma_start(w_raw[:, K, :, :], d["wqkv0"][:, K, :, :]).then_inc(wk_loaded, 16)
                for i in range(KEY_CHUNKS):
                    if i >= 2:
                        sp.wait_ge(ctx_lo_done, i - 1)
                    sp.dma_start(ctxT[:, i % 2, :, :], d["ctxT"][:, :, i * 512:(i + 1) * 512]).then_inc(ctx_loaded[i], 16)
                    if i == 0:
                        sp.dma_start(g.bias_cols[:, :, :], d["bias_cols"]).then_inc(early_loaded, 16)
                        sp.dma_start(g.x[:, :, :], d["x"]).then_inc(x_loaded, 16)
                    if i == 1:
                        sp.dma_start(g.ident[:, :], d["ident"]).then_inc(early_loaded, 16)
                        sp.dma_start(w_raw[:, Q, :, :], d["wqkv0"][:, Q, :, :]).then_inc(wq_loaded, 16)
                sp.dma_start(w_raw[:, V, :, :], d["wqkv0"][:, V, :, :]).then_inc(wv_loaded, 16)
                sp.dma_start(g.bias_rows[:, :], d["bias_rows"]).then_inc(consts_loaded, 16)
                sp.dma_start(g.betas[:, :], d["betas"]).then_inc(consts_loaded, 16)
                for n in range(NT - LATE):
                    sp.wait_ge(part3_done, n + 1)
                    store_parts(sp, n)
                    if n == EARLY:
                        for i, count in enumerate(stores_of(EARLY)):
                            sp.wait_ge(parts_stored[i], count)
                        load_stacks(sp, g, 0)
                sp.wait_ge(consts_loaded, 32)

            @block.tensor
            def _(pe):
                def tile(n):
                    which, fc, b, h = tiles[n]
                    if n >= 4:
                        pe.wait_ge(rest_done, n - 3)
                    for k in range(KC):
                        if which == Q:
                            rhs = (g.xnT_hi[:, k, b * S:(b + 1) * S], g.xnT_lo[:, k, b * S:(b + 1) * S])
                        else:
                            a = b * SC + h * 512
                            rhs = (g.ctxT_hi[:, k, a:a + 512], g.ctxT_lo[:, k, a:a + 512])
                        cols = slice(fc * P, (fc + 1) * P)
                        last = mm3(pe, acc[:, n % 4, :], (g.w0_hi[:, which, k, cols], g.w0_lo[:, which, k, cols]),
                                   rhs, k == 0, k == KC - 1)
                    last.then_inc(tile_done, 1)

                pe.wait_ge(w_hi_done, 1)
                pe.wait_ge(w_lo_done, 1)
                for n, (which, fc, b, h) in enumerate(tiles):
                    if fc == 0 and which == K:
                        pe.wait_ge(ctx_hi_done, 2 * b + h + 1)
                        pe.wait_ge(ctx_lo_done, 2 * b + h + 1)
                    elif fc == 0:
                        pe.wait_ge(w_hi_done, 2)
                        pe.wait_ge(w_lo_done, 2)
                        norm.wait_half(pe, b)
                    tile(n)
                    if n == 3:
                        pe.wait_ge(early_loaded, 32)
                        norm.turn(pe, 0)
                    if n == 5:
                        norm.turn(pe, 1)
                pe.wait_ge(w_hi_done, 3)
                pe.wait_ge(w_lo_done, 3)
                for m in range(4):
                    for j in range(2):
                        half_value_tile(pe, g, turned_banks, m, j)

            @block.scalar
            def _(act):
                def context(i):
                    act.wait_ge(ctx_loaded[i], 16)
                    t = slice(i * 512, (i + 1) * 512)
                    act.activation(g.ctxT_hi[:, :, t], ctxT[:, i % 2, :, :], ACT.Copy).then_inc(ctx_hi_done, 1)

                def tile(n):
                    if n < NT:
                        bias = bias_of(n)
                        act.wait_ge(tile_done, n + 1)
                        if n >= SLOTS:
                            act.wait_ge(parts_stored[n % SLOTS], STORES * (n // SLOTS))
                        act.activation(parts[:, n % SLOTS, 0, :], acc[:, n % 4, :], ACT.Identity, bias=bias).then_inc(part1_done, 1)
                    if n >= 1:
                        act.wait_ge(rest_done, n)
                        act.activation(parts[:, (n - 1) % SLOTS, 1, :], rest[:, (n - 1) % 2, :], ACT.Copy).then_inc(part2_done, 1)

                def weight(which, loaded):
                    act.wait_ge(loaded, 16)
                    act.activation(g.w0_hi[:, which, :, :], w_raw[:, which, :, :], ACT.Copy).then_inc(w_hi_done, 1)

                weight(K, wk_loaded)
                context(0)
                context(1)
                act.wait_ge(early_loaded, 32)
                act.wait_ge(eps_set, 1)
                tile(0)
                tile(1)
                norm.root(act)
                weight(Q, wq_loaded)
                tile(2)
                context(2)
                tile(3)
                norm.high(act, 0)
                tile(4)
                context(3)
                for n in range(5, 8):
                    tile(n)
                norm.high(act, 1)
                weight(V, wv_loaded)
                for n in range(8, NT + 1):
                    tile(n)
                for m in range(4):
                    store_values(act, g, turned_banks, m)

            @block.gpsimd
            def _(pool):
                pool.memset(g.eps[:, :], EPS).then_inc(eps_set, 1)
                pool.wait_ge(eps_set, 1)
                pool.wait_ge(early_loaded, 32)
                pool.tensor_copy(g.ident16[:, :], g.ident[:, :]).then_inc(eps_set, 1)
                pool.wait_ge(eps_set, 2)
                for i in range(3):
                    pool.memset(g.k_stack[i][MAXROW:MAXROW + 3, :, :], 1.0).then_inc(eps_set, 1)
                    pool.wait_ge(eps_set, i + 3)

            @block.vector
            def _(dve):
                def context(i):
                    dve.wait_ge(ctx_hi_done, i + 1)
                    t = slice(i * 512, (i + 1) * 512)
                    dve.tensor_tensor(g.ctxT_lo[:, :, t], ctxT[:, i % 2, :, :], f32(g.ctxT_hi[:, :, t]), ALU.subtract).then_inc(ctx_lo_done, 1)

                def tile(n):
                    if n < NT:
                        dve.wait_ge(part1_done, n + 1)
                        if n >= 2:
                            dve.wait_ge(part3_done, n - 1)
                        dve.scalar_tensor_tensor(rest[:, n % 2, :], acc[:, n % 4, :], bias_of(n), parts[:, n % SLOTS, 0, :],
                                                 ALU.add, ALU.subtract).then_inc(rest_done, 1)
                    if n >= 1:
                        dve.wait_ge(part2_done, n)
                        dve.tensor_tensor(parts[:, (n - 1) % SLOTS, 2, :], rest[:, (n - 1) % 2, :], parts[:, (n - 1) % SLOTS, 1, :],
                                          ALU.subtract).then_inc(part3_done, 1)

                def weight(which, count):
                    dve.wait_ge(w_hi_done, count)
                    dve.tensor_tensor(g.w0_lo[:, which, :, :], w_raw[:, which, :, :], f32(g.w0_hi[:, which, :, :]), ALU.subtract).then_inc(w_lo_done, 1)

                weight(K, 1)
                context(0)
                context(1)
                dve.wait_ge(x_loaded, 16)
                take_stats(dve, g, range(TC)).then_inc(stats_done, 1)
                dve.wait_ge(stats_done, 1)
                norm.moments(dve)
                tile(0)
                tile(1)
                norm.invert(dve)
                norm.apply(dve, 0)
                weight(Q, 2)
                tile(2)
                context(2)
                tile(3)
                norm.apply(dve, 1)
                norm.low(dve, 0)
                tile(4)
                context(3)
                for n in range(5, 8):
                    tile(n)
                norm.low(dve, 1)
                weight(V, 3)
                for n in range(8, NT + 1):
                    tile(n)


def l0_stacks(nc, ctx, g):
    g.k_stack = [ctx.enter_context(nc.sbuf_tensor(f"k_stack{i}", [P, HG, SC], BF16)) for i in range(3)]
    g.q_stack = [ctx.enter_context(nc.sbuf_tensor(f"q_stack{i}", [P, HG, S], BF16)) for i in range(3)]
    g.stacks_loaded = [g.sem(f"stacks_loaded{i}") for i in range(3)]


def load_stacks(sp, g, r):
    for stack, dram in ((g.k_stack, g.k_stacks), (g.q_stack, g.q_stacks)):
        source = dram[r // GROUPS, r % GROUPS // 2, :, :, :].rearrange("t (e h) s -> (t e) h s", e=HD)
        heads = r % 2 * HG
        sp.dma_start(stack[r % 3][0:MAXROW, :, :], source[:, heads:heads + HG, :]).then_inc(g.stacks_loaded[r % 3], 16)


def later_constants(nc, ctx, g, d, turned):
    def sb(name, shape, dt=F32):
        return ctx.enter_context(nc.sbuf_tensor(name, shape, dt))

    rhsT = sb("rhsT_sb", [P, KC, D])
    rhs_round = rhsT
    rhs_step, rhs_inverse = sb("rhs_step", [P, KC, 1]), sb("rhs_inverse", [P, KC, 1])
    step_wide, sum_lo = sb("step_wide", [P, KC, P]), sb("sum_lo", [P, KC, B])
    rhs_loaded, rhs_rounded, rhs_turned = g.sem("rhs_loaded"), g.sem("rhs_rounded"), g.sem("rhs_turned")
    dve_steps = g.sem("constants_steps")

    def on_sync(sp):
        sp.dma_start(rhsT[:, :, :], d["rhsT"]).then_inc(rhs_loaded, 16)

    def on_tensor(pe):
        pe.wait_ge(rhs_rounded, 1 + KC)
        for n in range(KC):
            for k in range(KC):
                pe.transpose(turned[:, 0, k * D + n * P:k * D + (n + 1) * P],
                             rhs_round[:, n, k * P:(k + 1) * P], g.ident[:, :])
            last = pe.transpose(turned[:, 1, n * P:(n + 1) * P], step_wide[:, n, :], g.ident[:, :])
        last.then_inc(rhs_turned, 1)

    def on_vector(dve):
        own = Chain(dve, dve_steps)
        dve.wait_ge(rhs_loaded, 16)
        own.link(dve.tensor_reduce(rhs_step[:, :, 0], rhsT[:, :, :], X, ALU.max, apply_absolute_value=True))
        own.link(dve.tensor_scalar(rhs_step[:, :, 0], rhs_step[:, :, 0], 1e-12, 1.0 / INT8_MAX, ALU.max, ALU.mult))
        own.link(dve.reciprocal(rhs_inverse[:, :, 0], rhs_step[:, :, 0]))
        for k in range(KC):
            own.link(dve.tensor_scalar(rhs_round[:, k, :], rhsT[:, k, :], rhs_inverse[:, k, :], ROUND,
                                       ALU.mult, ALU.add))
        own.link(dve.tensor_scalar(rhs_round[:, :, :], rhs_round[:, :, :], ROUND, INT8_MAX,
                                   ALU.subtract, ALU.min))
        dve.tensor_scalar(rhs_round[:, :, :], rhs_round[:, :, :], -INT8_MAX, None,
                          ALU.max).then_inc(rhs_rounded, 1)
        for k in range(KC):
            dve.tensor_copy(step_wide[:, k, :], rhs_step[:, k, :].to_broadcast([P, P])).then_inc(rhs_rounded, 1)
        for k in range(KC):
            for part, total in ((g.ctxT_hi, g.ctx_sum), (g.ctxT_lo, sum_lo)):
                own.step(dve.tensor_reduce(total[:, k, :], f32(part[:, k, :]).rearrange("p (b s) -> p b s", b=B), X, ALU.add))
        own.wait()
        own.link(dve.tensor_tensor(g.ctx_sum[:, :, :], g.ctx_sum[:, :, :], sum_lo[:, :, :], ALU.add))
        own.link(dve.tensor_tensor(g.phi_scale[:, :], g.betas[:, 0:1], g.betas[:, 1:2], ALU.add))
        own.link(dve.tensor_tensor(g.phi_scale[:, :], g.phi_scale[:, :], g.betas[:, 2:3], ALU.subtract))
        own.link(dve.tensor_scalar(g.phi_scale[:, :], g.phi_scale[:, :], float(D) ** 0.5, None, ALU.mult))
        dve.wait_ge(rhs_turned, 1)
        dve.tensor_copy(g.rhs_q[:, :, :], turned[:, 0, :].rearrange("p (k n) -> p k n", k=KC))
        dve.tensor_copy(g.rhs_scale[:, :], turned[:, 1, 0:D])

    c = Shared()
    c.on_sync, c.on_tensor, c.on_vector = on_sync, on_tensor, on_vector
    return c


def l0_attention_phase(nc, g, d):
    NR = B * GROUPS
    KT = SC // P
    AU = 4 * HG * 2
    BU = 2 * KT
    SCALE = float(HD) ** -0.5
    T1_AT, T0_AT = 1, 9
    with ExitStack() as ctx:
        def sb(name, shape, dt=F32):
            return ctx.enter_context(nc.sbuf_tensor(name, shape, dt))

        k_stack, q_stack, stacks_loaded = g.k_stack, g.q_stack, g.stacks_loaded
        v_aug = [sb(f"v_aug{i}", [P, KT, HG, 32]) for i in range(3)]
        probs = [sb(f"probs0_{i}", [P, HG, 256]) for i in range(4)]
        maxima = [sb(f"maxima{h}", [P, 8, 2]) for h in range(2)]
        row_max = [sb(f"row_max{h}", [P, 8]) for h in range(2)]
        neg_max, neg_rest = sb("neg_max0", [P, 8]), sb("neg_rest", [P, 8])
        neg_parts = [sb(f"neg_parts{h}", [P, 2, 3, HG], BF16) for h in range(2)]
        neg_rows = [sb(f"neg_rows{h}", [3 * HG, 256], BF16) for h in range(2)]
        a_scores = ctx.enter_context(nc.psum_tensor("a_scores", [P, 2, 512], F32))
        b_scores = ctx.enter_context(nc.psum_tensor("b_scores", [P, 2, HG, 256], F32))
        weighted = ctx.enter_context(nc.psum_tensor("weighted", [P, 512], F32))
        max_turned = ctx.enter_context(nc.psum_tensor("max_turned", [P, 2, 512], BF16))
        v_aug_done = g.sem("v_aug_done")
        a_ready, a_read, b_ready = g.sem("a_ready"), g.sem("a_read"), g.sem("b_ready")
        exp_done = g.sem("exp_done")
        av_done = g.sem("av_done")
        avs_done = g.sem("avs_done")
        row_max_done, turn_done = g.sem("row_max_done"), g.sem("turn_done")
        neg_done = g.sem("neg_done")
        neg_rows_done = g.sem("neg_rows_done")
        max_loaded = [g.sem(f"max_loaded{h}") for h in range(2)]
        negate_steps = g.sem("negate_steps")
        LOADS = 2 * 16
        o = g.out0
        value_banks = b_scores[:, :, :, :].rearrange("p u (i h) q -> p (u i) (h q)", i=2)
        constants = later_constants(nc, ctx, g, d, a_scores[:, :, :])

        with nc.Block() as block:
            @block.sync
            def _(sp):
                def load_max(r, h):
                    sp.wait_ge(neg_rows_done, 2 * r + h + 1)
                    sp.dma_start(q_stack[r % 3][MAXROW:MAXROW + 3, :, h * 256:(h + 1) * 256], neg_rows[h][:, :]).then_inc(max_loaded[h], 16)

                g.store_late(sp)
                load_stacks(sp, g, 1)
                for i, count in enumerate(g.all_stores):
                    sp.wait_ge(g.parts_stored[i], count)
                load_stacks(sp, g, 2)
                constants.on_sync(sp)
                sp.dma_start(o.w_raw[:, :, :], d["wo0"]).then_inc(o.loaded, 16)
                sp.dma_start(o.spread[:, :], d["spread"]).then_inc(o.loaded, 16)
                sp.dma_start(o.bv[:, :], d["bv0"]).then_inc(o.loaded, 16)
                for r in range(NR):
                    load_max(r, 0)
                    if r >= 2:
                        sp.wait_ge(avs_done, r)
                        gather_sums(sp, g, r - 2)
                    load_max(r, 1)
                    if r >= 1 and r + 2 < NR:
                        sp.wait_ge(avs_done, r + 1)
                        load_stacks(sp, g, r + 2)
                sp.wait_ge(avs_done, NR)
                gather_sums(sp, g, NR - 2)
                sp.wait_ge(o.inverse_done, 1)
                for r in range(NR - 1):
                    return_inverses(sp, g, r)

            @block.gpsimd
            def _(pool):
                own = Chain(pool, negate_steps)
                for i in range(3):
                    own.link(pool.memset(v_aug[i][:, :, :, :], 0.0))
                    own.link(pool.memset(v_aug[i][:, :, :, HD:HD + 1], 1.0))

                def negate(r, half):
                    parts, maxes = neg_parts[half], "p (q h) -> p q h"
                    pool.wait_ge(row_max_done, 2 * r + half + 1)
                    own.link(pool.tensor_scalar(neg_max[:, :], row_max[half][:, :], -1.0, None, ALU.mult))
                    own.link(pool.tensor_copy(parts[:, :, 0, :], neg_max[:, :].rearrange(maxes, q=2)))
                    own.link(pool.tensor_tensor(neg_rest[:, :].rearrange(maxes, q=2), neg_max[:, :].rearrange(maxes, q=2), parts[:, :, 0, :], ALU.subtract))
                    own.link(pool.tensor_copy(parts[:, :, 1, :], neg_rest[:, :].rearrange(maxes, q=2)))
                    pool.tensor_tensor(parts[:, :, 2, :], neg_rest[:, :].rearrange(maxes, q=2), parts[:, :, 1, :], ALU.subtract).then_inc(neg_done, 1)
                    pool.wait_ge(neg_done, 2 * r + half + 3)

                for r in range(NR):
                    negate(r, 0)
                    if r >= 3:
                        pool.wait_ge(avs_done, r - 1)
                    if r % GROUPS == 0:
                        pool.wait_ge(g.v0_done, VALUE_TILES // B * (r // GROUPS + 1))
                    pool.tensor_copy(v_aug[r % 3][:, :, :, 0:HD],
                                     g.v0[r // GROUPS][:, r % GROUPS, :, :].rearrange("p t (h e) -> p t h e", h=HG)).then_inc(v_aug_done, 1)
                    pool.wait_ge(v_aug_done, r + 1)
                    negate(r, 1)
                    if r == 2:
                        split_on_pool(pool, o.w_raw, o.w_hi, o.w_lo, o.loaded, o.split_done, 48)

            @block.tensor
            def _(pe):
                def turn_max(r, half):
                    pe.wait_ge(neg_done, 2 * r + half + 3)
                    for qc in range(2):
                        last = pe.transpose(max_turned[0:3 * HG, half, qc * P:(qc + 1) * P],
                                            neg_parts[half][:, qc, :, :].rearrange("p a h -> p (a h)"), g.ident16[:, :])
                    last.then_inc(turn_done, 1)

                def b_unit(r, buf, u):
                    half, kt = divmod(u, KT)
                    if isinstance(r, int) and r == 0 and u == 0:
                        pe.wait_ge(g.v0_done, VALUE_TILES)
                    if kt == 0:
                        pe.wait_ge(max_loaded[half], 16 * (r + 1))
                    pe.wait_ge(exp_done, BU * r + u + 1)
                    for h in range(HG):
                        last = pe.matmul(b_scores[:, u % 2, h, :], k_stack[buf][0:MAXROW + 3, h, kt * P:(kt + 1) * P],
                                         q_stack[buf][0:MAXROW + 3, h, half * 256:(half + 1) * 256],
                                         start=True, stop=True, skip_group_check=True)
                    last.then_inc(b_ready, 1)

                def av_unit(r, buf, u):
                    half, kt = divmod(u, KT)
                    if u == 0:
                        pe.wait_ge(avs_done, r + 1)
                        pe.wait_ge(v_aug_done, r + 1)
                    pe.wait_ge(exp_done, BU * r + u + 3)
                    for h in range(HG):
                        last = pe.matmul(weighted[32 * h:32 * h + 32, half * 256:(half + 1) * 256],
                                         v_aug[buf][:, kt, h, :], probs[u % 4][:, h, :],
                                         start=kt == 0, stop=kt == KT - 1, skip_group_check=True)
                    last.then_inc(av_done, 1)

                def period(r, buf, uses, first=False, last=False):
                    nxt = (buf + 1) % 3
                    for u in range(BU):
                        if not last:
                            if u == 0:
                                pe.wait_ge(stacks_loaded[nxt], LOADS * uses)
                            for k in (2 * u, 2 * u + 1):
                                a_tile(r + 1, nxt, k)
                        b_unit(r, buf, u)
                        if u >= 2:
                            av_unit(r, buf, u - 2)
                        elif not first:
                            av_unit(r - 1, (buf + 2) % 3, BU - 2 + u)
                        if u == T1_AT:
                            turn_max(r, 1)
                        if u == T0_AT and not last:
                            turn_max(r + 1, 0)

                def a_tile(r, buf, k, first=False):
                    half, qc, h, kh = k // 16, k // 8 % 2, k // 2 % 4, k % 2
                    if not (first and k < 2):
                        pe.wait_ge(a_read, AU * r + k - 1)
                    at = half * 256 + qc * P
                    pe.matmul(a_scores[:, k % 2, :], q_stack[buf][0:MAXROW, h, at:at + P],
                              k_stack[buf][0:MAXROW, h, kh * 512:(kh + 1) * 512], start=True, stop=True).then_inc(a_ready, 1)

                pe.sem_inc(exp_done, 2)
                pe.sem_inc(av_done, 4)
                pe.sem_inc(avs_done, 1)
                pe.sem_inc(neg_done, 2)
                pe.wait_ge(stacks_loaded[0], LOADS)
                for k in range(AU):
                    a_tile(0, 0, k, first=True)
                    if k == 19:
                        turn_max(0, 0)
                    if k % 2 == 1 and 4 + k // 4 < VALUE_TILES:
                        half_value_tile(pe, g, value_banks, 4 + k // 4, k // 2 % 2)
                period(0, 0, 1, first=True)
                with pe.Fori(0, (NR - 2) // 3) as j:
                    for k in range(1, 4):
                        period(3 * j + k, k % 3, j + 1 if k < 2 else j + 2)
                period(NR - 1, (NR - 1) % 3, None, last=True)
                av_unit(NR - 1, (NR - 1) % 3, BU - 2)
                av_unit(NR - 1, (NR - 1) % 3, BU - 1)
                constants.on_tensor(pe)

            @block.scalar
            def _(act):
                def exponentials(r, units):
                    for u in units:
                        act.wait_ge(b_ready, BU * r + u + 1)
                        act.wait_ge(av_done, BU * r + u + 1)
                        act.activation(probs[u % 4][:, :, :], b_scores[:, u % 2, :, :], ACT.Exp, scale=SCALE).then_inc(exp_done, 1)

                def copy_weighted(r):
                    act.wait_ge(av_done, BU * r + BU + 4)
                    act.activation(g.avs[:, r, :], weighted[:, :], ACT.Copy).then_inc(avs_done, 1)

                for m in range(4, VALUE_TILES):
                    store_values(act, g, value_banks, m)
                def copy_turned(r, half):
                    act.wait_ge(turn_done, 2 * r + half + 1)
                    act.activation(neg_rows[half][:, :], max_turned[0:3 * HG, half, 0:256], ACT.Copy).then_inc(neg_rows_done, 1)

                copy_turned(0, 0)
                exponentials(0, (0, 1))
                with act.Fori(0, NR - 1) as r:
                    exponentials(r, range(2, T1_AT + 2))
                    copy_turned(r, 1)
                    exponentials(r, range(T1_AT + 2, T0_AT + 2))
                    copy_turned(r + 1, 0)
                    exponentials(r, range(T0_AT + 2, BU))
                    exponentials(r + 1, (0, 1))
                    copy_weighted(r)
                exponentials(NR - 1, range(2, T1_AT + 2))
                copy_turned(NR - 1, 1)
                exponentials(NR - 1, range(T1_AT + 2, BU))
                copy_weighted(NR - 1)

            @block.vector
            def _(dve):
                def tile_max(r, k):
                    dve.wait_ge(a_ready, AU * r + k + 1)
                    i = k % 16
                    dve.tensor_reduce(maxima[k // 16][:, i // 2, i % 2:i % 2 + 1], a_scores[:, k % 2, :], X, ALU.max).then_inc(a_read, 1)
                    if i == 15:
                        dve.wait_ge(a_read, AU * r + k + 1)
                        dve.wait_ge(neg_done, 2 * r + k // 16 + 1)
                        dve.tensor_reduce(row_max[k // 16][:, :], maxima[k // 16][:, :, :], X, ALU.max).then_inc(row_max_done, 1)

                with dve.Fori(0, NR) as r:
                    for k in range(AU):
                        tile_max(r, k)
                dve.wait_ge(o.sums_gathered, 16 * HG * (NR - 1))
                dve.reciprocal(o.sums[:, 0:NR - 1, :], o.sums[:, 0:NR - 1, :]).then_inc(o.inverse_done, 1)
                constants.on_vector(dve)


def l0_output_buffers(nc, ctx, g):
    def sb(name, shape, dt=F32):
        return ctx.enter_context(nc.sbuf_tensor(name, shape, dt))

    NR = B * GROUPS
    o = g.out0 = Shared()
    o.w_raw, o.w_hi, o.w_lo = split_weights(nc, g, ctx, "o0", "wo0", [P, GROUPS, D])
    o.spread = sb("spread_sb", [HG, P])
    o.bv = sb("bv0_sb", [P, GROUPS])
    o.sums = sb("sums0", [P, NR, S // 32])
    o.inverse_rows = sb("inverse_rows", [HG, NR, S])
    o.loaded, o.split_done = g.sem("o0_loaded"), g.sem("o0_split_done")
    o.sums_gathered, o.inverse_done = g.sem("sums_gathered"), g.sem("inverse0_done")
    o.inverses_returned = [g.sem(f"inverses_returned{i}") for i in range(2)]


def gather_sums(sp, g, r):
    for h in range(HG):
        sp.dma_start(g.out0.sums[32 * h:32 * h + 32, r, :],
                     g.avs[32 * h + HD:32 * h + HD + 1, r, :]).then_inc(g.out0.sums_gathered, 16)


def return_inverses(sp, g, r):
    last = r == B * GROUPS - 1
    sp.dma_start(g.out0.inverse_rows[:, r, :], g.out0.sums[:, r, :]).then_inc(g.out0.inverses_returned[last], 16)


def l0_output_phase(nc, g, d):
    NR = B * GROUPS
    o = g.out0
    with ExitStack() as ctx:
        def sb(name, shape, dt=F32):
            return ctx.enter_context(nc.sbuf_tensor(name, shape, dt))

        def bv(r):
            return o.bv[:, r % GROUPS:r % GROUPS + 1]

        attn = sb("attn0", [P, 2, 512])
        attn_hi, attn_lo = sb("attn0_hi", [P, NR, 512], F32R), sb("attn0_lo", [P, NR, 512], F32R)
        inverse = ctx.enter_context(nc.psum_tensor("inverse0", [P, 4, 512], F32))
        out = ctx.enter_context(nc.psum_tensor("out0", [P, TC // 2, 2, D], F32))
        spread_done, attn_done, added = g.sem("spread0_done"), g.sem("attn0_done"), g.sem("added_o0")
        hi_done, lo_done, out_done = g.sem("attn0_hi_done"), g.sem("attn0_lo_done"), g.sem("out0_done")
        with nc.Block() as block:
            @block.sync
            def _(sp):
                gather_sums(sp, g, NR - 1)
                sp.wait_ge(o.inverse_done, 2)
                return_inverses(sp, g, NR - 1)

            @block.scalar
            def _(act):
                for r in range(NR):
                    act.wait_ge(attn_done, r + 1)
                    act.activation(attn_hi[:, r, :], attn[:, r % 2, :], ACT.Identity, bias=bv(r)).then_inc(hi_done, 1)

            @block.tensor
            def _(pe):
                def spread_inverse(r):
                    if r >= 4:
                        pe.wait_ge(attn_done, r - 3)
                    pe.matmul(inverse[:, r % 4, :], o.spread[:, :], o.inverse_rows[:, r, :], start=True, stop=True).then_inc(spread_done, 1)

                def project(b):
                    for m in range(2):
                        for j in range(2):
                            q = 2 * m + j
                            for gr in range(GROUPS):
                                r = b * GROUPS + gr
                                pe.wait_ge(hi_done, r + 1)
                                pe.wait_ge(lo_done, r + 1)
                                lhs = (attn_hi[:, r, q * P:(q + 1) * P], attn_lo[:, r, q * P:(q + 1) * P])
                                last = mm3(pe, out[:, 2 * b + m, j, :], lhs, (o.w_hi[:, gr, :], o.w_lo[:, gr, :]),
                                           j == 0 and gr == 0, gr == GROUPS - 1)
                        last.then_inc(out_done, 1)

                pe.wait_ge(o.split_done, 2)
                pe.wait_ge(o.inverses_returned[0], 16 * (NR - 1))
                for r in range(NR - 1):
                    spread_inverse(r)
                project(0)
                pe.wait_ge(o.inverses_returned[1], 16)
                spread_inverse(NR - 1)
                project(1)

            @block.vector
            def _(dve):
                def low(r):
                    dve.wait_ge(hi_done, r + 1)
                    dve.scalar_tensor_tensor(attn_lo[:, r, :], attn[:, r % 2, :], bv(r), f32(attn_hi[:, r, :]), ALU.add, ALU.subtract).then_inc(lo_done, 1)

                for r in range(NR):
                    dve.wait_ge(spread_done, r + 1)
                    if r >= 2:
                        dve.wait_ge(hi_done, r - 1)
                        dve.wait_ge(lo_done, r - 1)
                    dve.tensor_tensor(attn[:, r % 2, :], g.avs[:, r, :], inverse[:, r % 4, :], ALU.mult).then_inc(attn_done, 1)
                    if r >= 1:
                        low(r - 1)
                    if r == 2:
                        dve.wait_ge(o.sums_gathered, 16 * HG * NR)
                        dve.reciprocal(o.sums[:, NR - 1, :], o.sums[:, NR - 1, :]).then_inc(o.inverse_done, 1)
                low(NR - 1)
                for m in range(TC // 2):
                    dve.wait_ge(out_done, m + 1)
                    dve.tensor_tensor(g.x[:, 2 * m:2 * m + 2, :], g.x[:, 2 * m:2 * m + 2, :], out[:, m, :, :], ALU.add).then_inc(added, 1)
                    dve.wait_ge(added, m + 1)
                    take_stats(dve, g, (2 * m, 2 * m + 1))


def split_on_pool(pool, raw, hi, lo, loaded, split_done, load_count=16):
    pool.wait_ge(loaded, load_count)
    pool.tensor_copy(hi[:, :, :], raw[:, :, :]).then_inc(split_done, 1)
    pool.wait_ge(split_done, 1)
    pool.tensor_tensor(lo[:, :, :], raw[:, :, :], f32(hi[:, :, :]), ALU.subtract).then_inc(split_done, 1)
    pool.wait_ge(split_done, 2)


def router_logits(pe, logits, n, xT, w, k_first=True):
    for c in range(TC):
        t = slice(c * P, (c + 1) * P)
        for k in range(KC):
            last = mm3(pe, logits[:, c, 0:n], (xT[0][:, k, t], xT[1][:, k, t]),
                       (w[0][:, k, :], w[1][:, k, :]), c == 0 and k == 0, k == KC - 1)
    return last


def l0_router(nc, ctx, g, d, logits, logits_read):
    def sb(name, shape, dt=F32):
        return ctx.enter_context(nc.sbuf_tensor(name, shape, dt))

    N = 2 * E0
    w_raw, w_hi, w_lo = split_weights(nc, g, ctx, "r0", "wr0", [P, KC, N])
    top, shifted = sb("top0", [P, TC, 2]), sb("shifted0", [P, TC, 2, E0])
    exps, sums, inv = sb("exps0", [P, TC, 2, E0]), sb("sums_r0", [P, TC, 2]), sb("inv_r0", [P, TC, 2])
    both, total = sb("both0", [P, TC, E0]), sb("total0", [P, TC])
    loaded, split_done = g.sem("r0_loaded"), g.sem("r0_split_done")
    logits_done, shifted_done, exp_done = g.sem("logits0_done"), g.sem("shifted0_done"), g.sem("exp_r0_done")
    dve_steps = g.sem("r0_dve_steps")

    def on_sync(sp):
        sp.dma_start(w_raw[:, :, :], d["wr0"]).then_inc(loaded, 16)

    def on_gpsimd(pool):
        split_on_pool(pool, w_raw, w_hi, w_lo, loaded, split_done)

    def on_scalar(act):
        act.wait_ge(shifted_done, 1)
        act.activation(exps[:, :, 0, :], shifted[:, :, 0, :], ACT.Exp).then_inc(exp_done, 1)
        act.activation(exps[:, :, 1, :], shifted[:, :, 1, :], ACT.Exp, scale=10.0).then_inc(exp_done, 1)

    def on_tensor(pe):
        pe.wait_ge(split_done, 2)
        router_logits(pe, logits, N, (g.xnT_hi, g.xnT_lo), (w_hi, w_lo)).then_inc(logits_done, 1)

    def on_vector(dve):
        own = Chain(dve, dve_steps)
        dve.wait_ge(logits_done, 1)
        own.link(dve.tensor_reduce(top[:, :, :], logits[:, :, :].rearrange("p c (w e) -> p c w e", w=2), X, ALU.max))
        wide = [P, TC, E0]
        own.link(dve.tensor_tensor(shifted[:, :, 0, :], logits[:, :, 0:E0], top[:, :, 0:1].to_broadcast(wide), ALU.subtract))
        own.link(dve.tensor_tensor(shifted[:, :, 1, :], logits[:, :, E0:2 * E0], top[:, :, 1:2].to_broadcast(wide), ALU.subtract))
        dve.sem_inc(shifted_done, 1)
        dve.sem_inc(logits_read, 4)
        dve.wait_ge(exp_done, 2)
        own.link(dve.tensor_reduce(sums[:, :, :], exps[:, :, :, :], X, ALU.add))
        own.link(dve.reciprocal(inv[:, :, :], sums[:, :, :]))
        for w in range(2):
            own.step(dve.tensor_tensor(exps[:, :, w, :], exps[:, :, w, :], inv[:, :, w:w + 1].to_broadcast(wide), ALU.mult))
        own.wait()
        own.link(dve.tensor_tensor(both[:, :, :], exps[:, :, 0, :], exps[:, :, 1, :], ALU.mult))
        own.link(dve.tensor_reduce(total[:, :], both[:, :, :], X, ALU.add))
        own.link(dve.tensor_scalar(total[:, :], total[:, :], 1e-9, None, ALU.add))
        own.link(dve.reciprocal(total[:, :], total[:, :]))
        per = U0 // E0
        for i in range(per):
            own.step(dve.tensor_tensor(g.cw[:, :, 0:U0].rearrange("p c (e i) -> p c e i", i=per)[:, :, :, i], both[:, :, :],
                                       total[:, :].rearrange("p (c o) -> p c o", o=1).to_broadcast(wide), ALU.mult))
        own.wait()

    r = Shared()
    r.on_sync, r.on_gpsimd, r.on_scalar, r.on_tensor, r.on_vector = on_sync, on_gpsimd, on_scalar, on_tensor, on_vector
    return r


def l2_router(nc, ctx, g, d, logits, logits_read):
    def sb(name, shape, dt=F32):
        return ctx.enter_context(nc.sbuf_tensor(name, shape, dt))

    w_raw, w_hi, w_lo = split_weights(nc, g, ctx, "r2", "wr2", [P, KC, E2])
    scores, biased = sb("scores2", [P, TC, E2]), sb("biased2", [P, TC, 2 * E2])
    largest, taken, left = sb("largest2", [P, TC, 8]), sb("taken2", [P, TC, 8]), sb("left2", [P, TC, 2 * E2])
    mask = sb("mask2", [P, TC, E2])
    loaded, split_done = g.sem("r2_loaded"), g.sem("r2_split_done")
    logits_done, scores_done, dve_steps = g.sem("logits2_done"), g.sem("scores2_done"), g.sem("r2_dve_steps")

    def on_sync(sp):
        sp.dma_start(w_raw[:, :, :], d["wr2"]).then_inc(loaded, 16)

    def on_gpsimd(pool):
        split_on_pool(pool, w_raw, w_hi, w_lo, loaded, split_done)

    def on_scalar(act):
        act.wait_ge(logits_done, 1)
        act.activation(scores[:, :, :], logits[:, :, 0:E2], ACT.Sigmoid).then_inc(scores_done, 1)

    def on_tensor(pe):
        pe.wait_ge(split_done, 2)
        router_logits(pe, logits, E2, (g.xnT_hi, g.xnT_lo), (w_hi, w_lo)).then_inc(logits_done, 1)

    def on_vector(dve):
        own = Chain(dve, dve_steps)
        own.step(dve.memset(biased[:, :, :], NEG))
        own.step(dve.memset(taken[:, :, :], NEG))
        own.link(dve.memset(g.cw[:, :, :], 1.0))
        dve.wait_ge(scores_done, 1)
        dve.sem_inc(logits_read, 4)
        own.link(dve.tensor_tensor(biased[:, :, 0:E2], scores[:, :, :],
                                   row(g, "eb2").rearrange("p (o e) -> p o e", o=1).to_broadcast([P, TC, E2]), ALU.add))
        for c in range(TC):
            own.step(dve.max(largest[:, c, :], biased[:, c, :]))
        own.wait()
        own.link(dve.tensor_copy(taken[:, :, 0:2], largest[:, :, 0:2]))
        for c in range(TC):
            own.step(dve.match_replace(left[:, c, :], taken[:, c, :], biased[:, c, :], 2 * NEG))
        own.wait()
        own.link(dve.tensor_scalar(mask[:, :, :], left[:, :, 0:E2], 1.5 * NEG, None, ALU.is_lt))
        own.link(dve.tensor_tensor(g.cw[:, :, 0:E2], mask[:, :, :], scores[:, :, :], ALU.mult))

    r = Shared()
    r.on_sync, r.on_gpsimd, r.on_scalar, r.on_tensor, r.on_vector = on_sync, on_gpsimd, on_scalar, on_tensor, on_vector
    return r


def gated_layer_phase(nc, g, d, tag, N, weights, make_router):
    FC = FU // P
    Q = 2 * FC
    with ExitStack() as ctx:
        def sb(name, shape, dt=F32):
            return ctx.enter_context(nc.sbuf_tensor(f"{name}_{tag}", shape, dt))

        def two(name, shape, dt=F32):
            return [sb(f"{name}{i}", shape, dt) for i in range(2)]

        gu_raw, gu_hi, gu_lo = two("gu_raw", [P, 2, KC, FU]), two("gu_hi", [P, 2, KC, FU], F32R), two("gu_lo", [P, 2, KC, FU], F32R)
        dn_raw, dn_hi, dn_lo = two("dn_raw", [P, FC, D]), two("dn_hi", [P, FC, D], F32R), two("dn_lo", [P, FC, D], F32R)
        h_hi, h_lo = two("h_hi", [P, FC, T], F32R), two("h_lo", [P, FC, T], F32R)
        silu, hidden = sb("silu", [P, 2, 512]), sb("hidden", [P, 2, 512])
        gate = ctx.enter_context(nc.psum_tensor(f"gate_{tag}", [P, 2, 512], F32))
        up = ctx.enter_context(nc.psum_tensor(f"up_{tag}", [P, 2, 512], F32))
        out = ctx.enter_context(nc.psum_tensor(f"out_{tag}", [P, TC // 2, 2, D], F32))

        def sem(name):
            return g.sem(f"{name}_{tag}")

        gu_loaded, dn_loaded = [sem("gu_loaded0"), sem("gu_loaded1")], [sem("dn_loaded0"), sem("dn_loaded1")]
        gu_hi_done, gu_lo_done, dn_hi_done, dn_lo_done = sem("gu_hi_done"), sem("gu_lo_done"), sem("dn_hi_done"), sem("dn_lo_done")
        gu_done, silu_done, hidden_done = sem("gu_done"), sem("silu_done"), sem("hidden_done")
        h_hi_done, h_lo_done = sem("h_hi_done"), sem("h_lo_done")
        out_done = sem("out_done")
        out_free = sem("out_free")

        norm = normaliser(nc, ctx, g, tag, out[:, :, :, :].rearrange("p (h k) j e -> p h k (j e)", h=2))
        router = make_router(nc, ctx, g, d, out[:, 0, :, :].rearrange("p j e -> p (j e)")[:, 0:TC * 16].rearrange("p (c n) -> p c n", c=TC), out_free)

        def periods(eng, period, route):
            period(0, 0, 1, 1)
            route(eng)
            with eng.Fori(0, (N - 2) // 2) as i:
                period(2 * i + 1, 1, i + 1, i + 2)
                period(2 * i + 2, 0, i + 2, i + 2)
            period(N - 1, 1, N // 2, None)
            period(N, 0, None, None)

        with nc.Block() as block:
            @block.sync
            def _(sp):
                def load_gu(n, s):
                    sp.dma_start(gu_raw[s][:, :, :, :], weights[n, :, 0:2, :, :]).then_inc(gu_loaded[s], 16)

                def load_dn(n, s):
                    sp.dma_start(dn_raw[s][:, :, :], weights[n, :, 2, :, :]).then_inc(dn_loaded[s], 16)

                load_gu(0, 0)
                router.on_sync(sp)
                load_dn(0, 0)
                load_gu(1, 1)
                load_dn(1, 1)
                with sp.Fori(0, (N - 2) // 2) as i:
                    for s in range(2):
                        sp.wait_ge(gu_lo_done, 2 * i + s + 1)
                        load_gu(2 * i + s + 2, s)
                        sp.wait_ge(dn_lo_done, 2 * i + s + 1)
                        load_dn(2 * i + s + 2, s)

            @block.tensor
            def _(pe):
                def period(n, s, uses, next_uses):
                    first, has_gu = isinstance(n, int) and n == 0, uses is not None
                    if has_gu:
                        pe.wait_ge(gu_hi_done, n + 1)
                        pe.wait_ge(gu_lo_done, n + 1)
                        for q in range(Q):
                            fc, half = divmod(q, 2)
                            if first and fc == 0:
                                norm.wait_half(pe, half)
                            if not (first and q < 2):
                                pe.wait_ge(silu_done, Q * n + q - 1)
                                pe.wait_ge(hidden_done, Q * n + q - 1)
                            t, f = slice(half * 512, (half + 1) * 512), slice(fc * P, (fc + 1) * P)
                            for which, bank in ((0, gate), (1, up)):
                                for k in range(KC):
                                    last = mm3(pe, bank[:, q % 2, :], (gu_hi[s][:, which, k, f], gu_lo[s][:, which, k, f]),
                                               (g.xnT_hi[:, k, t], g.xnT_lo[:, k, t]), k == 0, k == KC - 1)
                            last.then_inc(gu_done, 1)
                    if not first:
                        o = 1 - s
                        pe.wait_ge(dn_hi_done, n)
                        pe.wait_ge(dn_lo_done, n)
                        pe.wait_ge(h_hi_done, Q * n)
                        pe.wait_ge(h_lo_done, Q * n)
                        for b in range(TC // 2):
                            pe.wait_ge(out_free, 4 * (n - 1) + b + 1)
                            for j in range(2):
                                t = slice((2 * b + j) * P, (2 * b + j + 1) * P)
                                for fc in range(FC):
                                    last = mm3(pe, out[:, b, j, :], (h_hi[o][:, fc, t], h_lo[o][:, fc, t]),
                                               (dn_hi[o][:, fc, :], dn_lo[o][:, fc, :]), j == 0 and fc == 0, fc == FC - 1)
                            last.then_inc(out_done, 1)

                norm.on_tensor(pe)
                pe.sem_inc(out_done, 4)
                periods(pe, period, router.on_tensor)

            @block.scalar
            def _(act):
                def split_gu(n, s, uses):
                    act.wait_ge(gu_loaded[s], 16 * uses)
                    act.activation(gu_hi[s][:, :, :, :], gu_raw[s][:, :, :, :], ACT.Copy).then_inc(gu_hi_done, 1)

                def period(n, s, uses, next_uses):
                    if uses is None:
                        return

                    def silu_of(q):
                        act.wait_ge(gu_done, Q * n + q + 1)
                        act.activation(silu[:, q % 2, :], gate[:, q % 2, :], ACT.Silu).then_inc(silu_done, 1)

                    def high(q):
                        fc, half = divmod(q, 2)
                        act.wait_ge(hidden_done, Q * n + q + 1)
                        act.activation(h_hi[s][:, fc, half * 512:(half + 1) * 512], hidden[:, q % 2, :], ACT.Copy).then_inc(h_hi_done, 1)

                    silu_of(0)
                    silu_of(1)
                    if not (isinstance(n, int) and n == 0):
                        act.wait_ge(out_done, 4 * n)
                    high(0)
                    if next_uses is not None:
                        split_gu(n + 1, 1 - s, next_uses)
                    silu_of(2)
                    high(1)
                    silu_of(3)
                    high(2)
                    high(3)
                    act.wait_ge(dn_loaded[s], 16 * uses)
                    act.activation(dn_hi[s][:, :, :], dn_raw[s][:, :, :], ACT.Copy).then_inc(dn_hi_done, 1)

                norm.root(act)
                split_gu(0, 0, 1)
                norm.high(act, 0)
                norm.high(act, 1)
                periods(act, period, router.on_scalar)

            @block.gpsimd
            def _(pool):
                def split_gu(n, s):
                    pool.wait_ge(gu_hi_done, n + 1)
                    pool.tensor_tensor(gu_lo[s][:, :, :, :], gu_raw[s][:, :, :, :], f32(gu_hi[s][:, :, :, :]), ALU.subtract).then_inc(gu_lo_done, 1)

                def period(n, s, uses, next_uses):
                    if uses is None:
                        return
                    if not (isinstance(n, int) and n == 0):
                        pool.wait_ge(dn_lo_done, n)
                    if next_uses is not None:
                        split_gu(n + 1, 1 - s)
                        pool.wait_ge(gu_lo_done, n + 2)
                    if uses is not None:
                        pool.wait_ge(dn_hi_done, n + 1)
                        pool.tensor_tensor(dn_lo[s][:, :, :], dn_raw[s][:, :, :], f32(dn_hi[s][:, :, :]), ALU.subtract).then_inc(dn_lo_done, 1)

                router.on_gpsimd(pool)
                periods(pool, period, lambda pool: None)

            @block.vector
            def _(dve):
                def period(n, s, uses, next_uses):
                    first = isinstance(n, int) and n == 0

                    def product(q):
                        dve.wait_ge(silu_done, Q * n + q + 1)
                        if not (first and q < 2):
                            dve.wait_ge(h_hi_done, Q * n + q - 1)
                            dve.wait_ge(h_lo_done, Q * n + q - 1)
                        dve.tensor_tensor(hidden[:, q % 2, :], silu[:, q % 2, :], up[:, q % 2, :], ALU.mult).then_inc(hidden_done, 1)

                    def low(q):
                        fc, half = divmod(q, 2)
                        t = slice(half * 512, (half + 1) * 512)
                        dve.wait_ge(h_hi_done, Q * n + q + 1)
                        dve.tensor_tensor(h_lo[s][:, fc, t], hidden[:, q % 2, :], f32(h_hi[s][:, fc, t]), ALU.subtract).then_inc(h_lo_done, 1)

                    if uses is not None:
                        product(0)
                        product(1)
                        low(0)
                        product(2)
                        low(1)
                        product(3)
                        low(2)
                        low(3)
                    if not first:
                        dve.wait_ge(out_free, 4 * n)
                        for b in range(TC // 2):
                            dve.wait_ge(out_done, 4 * n + b + 1)
                            for j in range(2):
                                c = 2 * b + j
                                weight = g.cw[:, c, bass.ds(n - 1, 1)]
                                last = dve.scalar_tensor_tensor(g.x[:, c, :], out[:, b, j, :], weight, g.x[:, c, :], ALU.mult, ALU.add)
                            last.then_inc(out_free, 1)
                            if uses is None:
                                dve.wait_ge(out_free, 4 * n + b + 1)
                                take_stats(dve, g, (2 * b, 2 * b + 1))

                norm.moments(dve)
                norm.invert(dve)
                norm.apply(dve, 0)
                norm.apply(dve, 1)
                dve.wait_ge(gu_hi_done, 1)
                dve.tensor_tensor(gu_lo[0][:, :, :, :], gu_raw[0][:, :, :, :], f32(gu_hi[0][:, :, :, :]), ALU.subtract).then_inc(gu_lo_done, 1)
                norm.low(dve, 0)
                norm.low(dve, 1)
                periods(dve, period, router.on_vector)


def l1_shift_phase(nc, g, d):
    with ExitStack() as ctx:
        def sb(name, shape, dt=F32):
            return ctx.enter_context(nc.sbuf_tensor(name, shape, dt))

        w_raw, w_hi, w_lo = split_weights(nc, g, ctx, "s1", "wx1", [P, 2, KC, D])
        mean, mean_hi, mean_lo = sb("mean", [P, KC, B, P]), sb("mean_hi", [P, KC, B, P], F32R), sb("mean_lo", [P, KC, B, P], F32R)
        shift = sb("shift", [P, B, D])
        out = ctx.enter_context(nc.psum_tensor("out_s1", [P, TC // 2, 2, D], F32))
        norm = normaliser(nc, ctx, g, "n2", ctx.enter_context(nc.psum_tensor("turned_n2", [P, 2, KC, 512], F32)))
        loaded, hi_done, lo_done = g.sem("s1_loaded"), g.sem("s1_hi_done"), g.sem("s1_lo_done")
        mean_done, mean_lo_done = g.sem("mean_done"), g.sem("mean_lo_done")
        part2_done, shift_done, out_done, dve_steps = g.sem("part2_done"), g.sem("shift_done"), g.sem("out_s1_done"), g.sem("s1_dve_steps")
        LAST = TC // 2 - 1
        with nc.Block() as block:
            @block.sync
            def _(sp):
                sp.dma_start(w_raw[:, :, :, :], d["wx1"]).then_inc(loaded, 16)

            @block.scalar
            def _(act):
                norm.root(act)
                act.wait_ge(mean_done, 1)
                act.activation(mean_hi[:, :, :, :], mean[:, :, :, :], ACT.Copy).then_inc(hi_done, 1)
                act.wait_ge(loaded, 16)
                act.activation(w_hi[:, :, :, :], w_raw[:, :, :, :], ACT.Copy).then_inc(hi_done, 1)
                norm.high(act, 0)
                norm.high(act, 1)

            @block.gpsimd
            def _(pool):
                pool.wait_ge(hi_done, 1)
                pool.tensor_tensor(mean_lo[:, :, :, :], mean[:, :, :, :], f32(mean_hi[:, :, :, :]), ALU.subtract).then_inc(mean_lo_done, 1)

            @block.vector
            def _(dve):
                own = Chain(dve, dve_steps)
                dve.tensor_scalar(mean[:, :, :, :], g.ctx_sum[:, :, :].rearrange("p k (b o) -> p k b o", o=1).to_broadcast([P, KC, B, P]),
                                  1.0 / SC, None, ALU.mult).then_inc(mean_done, 1)
                norm.moments(dve)
                norm.invert(dve)
                norm.apply(dve, 0)
                dve.wait_ge(hi_done, 2)
                dve.tensor_tensor(w_lo[:, :, :, :], w_raw[:, :, :, :], f32(w_hi[:, :, :, :]), ALU.subtract).then_inc(lo_done, 1)
                norm.apply(dve, 1)
                norm.low(dve, 0)
                norm.low(dve, 1)
                dve.wait_ge(part2_done, 1)
                dve.tensor_tensor(shift[:, :, :], out[:, LAST, :, :], row(g, "b_x1").rearrange("p (o e) -> p o e", o=1).to_broadcast([P, B, D]), ALU.add).then_inc(shift_done, 1)
                dve.wait_ge(shift_done, 1)
                for b in range(B):
                    xb = g.x[:, b * TC // B:(b + 1) * TC // B, :]
                    own.link(dve.tensor_tensor(xb, xb, shift[:, b:b + 1, :].to_broadcast([P, TC // B, D]), ALU.add))
                for m in range(TC // 2):
                    dve.wait_ge(out_done, m + 1)
                    own.link(dve.tensor_tensor(g.x[:, 2 * m:2 * m + 2, :], g.x[:, 2 * m:2 * m + 2, :], out[:, m, :, :], ALU.add))
                    take_stats(dve, g, (2 * m, 2 * m + 1))

            @block.tensor
            def _(pe):
                norm.turn(pe, 0)
                pe.wait_ge(lo_done, 1)
                pe.wait_ge(mean_lo_done, 1)
                for b in range(B):
                    for k in range(KC):
                        last = mm3(pe, out[:, LAST, b, :], (mean_hi[:, k, b, :], mean_lo[:, k, b, :]),
                                   (w_hi[:, 1, k, :], w_lo[:, 1, k, :]), b == 0 and k == 0, k == KC - 1)
                last.then_inc(part2_done, 1)
                norm.turn(pe, 1)
                for m in range(TC // 2):
                    norm.wait_half(pe, m // 2)
                    if m == LAST:
                        pe.wait_ge(shift_done, 1)
                    for j in range(2):
                        t = slice((2 * m + j) * P, (2 * m + j + 1) * P)
                        for k in range(KC):
                            last = mm3(pe, out[:, m, j, :], (g.xnT_hi[:, k, t], g.xnT_lo[:, k, t]),
                                       (w_hi[:, 0, k, :], w_lo[:, 0, k, :]), j == 0 and k == 0, k == KC - 1)
                    last.then_inc(out_done, 1)


def l1_router(nc, ctx, g, d, banks):
    HALF = E1 // 2

    def sb(name, shape, dt=F32):
        return ctx.enter_context(nc.sbuf_tensor(name, shape, dt))

    w_raw, w_hi, w_lo = split_weights(nc, g, ctx, "r1", "wr1", [P, KC, E1])
    shifted, exps, left = sb("shifted1", [P, TC, E1]), sb("exps1", [P, TC, E1]), sb("left1", [P, TC, E1])
    logit, top, largest = sb("logit1", [P, TC, E1]), sb("top1", [P, TC]), sb("largest1", [P, TC, 8])
    total = sb("total1", [P, TC])
    parts = sb("cw_parts", [P, TC, 2, 3, HALF], BF16)
    r = Shared()
    r.cwT = sb("cwT", [P, T])
    r.cw_partsT = sb("cw_partsT", [3 * HALF, 2, T], BF16)
    logits = banks[:, 0, :].rearrange("p (c e) -> p c e", e=E1)
    loaded, split_done, ready = g.sem("r1_loaded"), g.sem("r1_split_done"), g.sem("r1_constants_ready")
    logits_done, shifted_done, exp_done = g.sem("logits1_done"), g.sem("shifted1_done"), g.sem("exp_r1_done")
    parts_done, parts_turned, dve_steps = g.sem("cw_parts_done"), g.sem("cw_parts_turned"), g.sem("r1_dve_steps")
    r.parts_copied, cw_turned, r.cw_copied = g.sem("cw_parts_copied"), g.sem("cw_turned_done"), g.sem("cw_copied")
    own = None
    wide = [P, TC, E1]

    def on_sync(sp):
        sp.dma_start(w_raw[:, :, :], d["wr1"]).then_inc(loaded, 16)

    def on_gpsimd(pool):
        split_on_pool(pool, w_raw, w_hi, w_lo, loaded, split_done)
        pool.memset(r.cwT[E1:E1 + ES1, :], 1.0).then_inc(ready, 1)
        pool.wait_ge(ready, 1)

    def take_logits(pe):
        pe.wait_ge(split_done, 2)
        router_logits(pe, logits, E1, (g.xnT_hi, g.xnT_lo), (w_hi, w_lo)).then_inc(logits_done, 1)

    def turn_parts(pe):
        pe.wait_ge(parts_done, 1)
        pe.wait_ge(ready, 1)
        for h in range(2):
            for c in range(TC):
                last = pe.transpose(banks.bitcast(BF16)[0:3 * HALF, h, c * P:(c + 1) * P],
                                    parts[:, c, h, :, :].rearrange("p a e -> p (a e)"), g.ident16[:, :])
            last.then_inc(parts_turned, 1)

    def turn_weights(pe):
        for c in range(TC):
            if c % 4 == 0:
                pe.wait_ge(r.parts_copied, c // 4 + 1)
            last = pe.transpose(banks[0:E1, c // 4, c % 4 * P:(c % 4 + 1) * P], exps[:, c, :], g.ident[:, :])
        last.then_inc(cw_turned, 1)

    def exponentials(act):
        act.wait_ge(shifted_done, 1)
        act.activation(exps[:, :, :], shifted[:, :, :], ACT.Exp).then_inc(exp_done, 1)

    def copy_parts(act):
        for h in range(2):
            act.wait_ge(parts_turned, h + 1)
            act.activation(r.cw_partsT[:, h, :], banks.bitcast(BF16)[0:3 * HALF, h, :], ACT.Copy).then_inc(r.parts_copied, 1)

    def copy_weights(act):
        act.wait_ge(cw_turned, 1)
        act.activation(r.cwT[0:E1, :], banks[0:E1, :, :], ACT.Copy).then_inc(r.cw_copied, 1)

    def shift_logits(dve):
        nonlocal own
        own = Chain(dve, dve_steps)
        dve.wait_ge(logits_done, 1)
        own.link(dve.tensor_tensor(logit[:, :, :], logits, row(g, "rb1").rearrange("p (o e) -> p o e", o=1).to_broadcast(wide), ALU.add))
        own.link(dve.tensor_reduce(top[:, :], logit[:, :, :], X, ALU.max))
        dve.tensor_tensor(shifted[:, :, :], logit[:, :, :], top[:, :].rearrange("p (c o) -> p c o", o=1).to_broadcast(wide), ALU.subtract).then_inc(shifted_done, 1)

    def divide(dve):
        own.link(dve.tensor_reduce(total[:, :], exps[:, :, :], X, ALU.add))
        own.link(dve.reciprocal(total[:, :], total[:, :]))
        own.link(dve.tensor_tensor(exps[:, :, :], exps[:, :, :], total[:, :].rearrange("p (c o) -> p c o", o=1).to_broadcast(wide), ALU.mult))

    def find_largest(dve):
        dve.wait_ge(exp_done, 1)
        divide(dve)
        for c in range(TC):
            own.step(dve.max(largest[:, c, :], exps[:, c, :]))
        own.wait()

    def keep_largest(dve):
        for c in range(TC):
            own.step(dve.match_replace(left[:, c, :], largest[:, c, :], exps[:, c, :], 0.0))
        own.wait()
        own.link(dve.tensor_tensor(exps[:, :, :], exps[:, :, :], left[:, :, :], ALU.subtract))
        divide(dve)

    def split_parts(dve):
        halves = exps[:, :, :].rearrange("p c (h e) -> p c h e", h=2)
        rest = shifted[:, :, :].rearrange("p c (h e) -> p c h e", h=2)
        own.link(dve.tensor_copy(parts[:, :, :, 0, :], halves))
        own.link(dve.tensor_tensor(rest, halves, parts[:, :, :, 0, :], ALU.subtract))
        own.link(dve.tensor_copy(parts[:, :, :, 1, :], rest))
        dve.tensor_tensor(parts[:, :, :, 2, :], rest, parts[:, :, :, 1, :], ALU.subtract).then_inc(parts_done, 1)

    r.on_sync, r.on_gpsimd = on_sync, on_gpsimd
    r.take_logits, r.turn_parts, r.turn_weights = take_logits, turn_parts, turn_weights
    r.exponentials, r.copy_parts, r.copy_weights = exponentials, copy_parts, copy_weights
    r.shift_logits, r.find_largest, r.keep_largest, r.split_parts = shift_logits, find_largest, keep_largest, split_parts
    return r


def l1_experts_phase(nc, g, d):
    N = U1
    NS = U1 - PAIRS1
    Q = 2
    with ExitStack() as ctx:
        def sb(name, shape, dt=F32):
            return ctx.enter_context(nc.sbuf_tensor(f"{name}_l1", shape, dt))

        def two(name, shape, dt=F32):
            return [sb(f"{name}{i}", shape, dt) for i in range(2)]

        up_raw, up_hi, up_lo = two("up_raw", [P, D + 1]), two("up_hi", [P, KC, P], F32R), two("up_lo", [P, KC, P], F32R)
        b1 = two("b1", [P, 1])
        dn_raw, dn_hi, dn_lo = two("dn_raw", [P, D]), two("dn_hi", [P, D], F32R), two("dn_lo", [P, D], F32R)
        h_hi, h_lo = two("h_hi", [P, T], F32R), two("h_lo", [P, T], F32R)
        silu, hidden = sb("silu", [P, 2, 512]), sb("hidden", [P, 2, 512])
        b2 = sb("b2", [E1 + ES1, D])
        select = sb("select", [3 * E1 // 2, PAIRS1 // 2, P], BF16)
        up = ctx.enter_context(nc.psum_tensor("up_l1", [P, 2, 512], F32))
        weight = ctx.enter_context(nc.psum_tensor("weight_l1", [P, 2, 512], F32))
        out = ctx.enter_context(nc.psum_tensor("out_l1", [P, TC // 2, 2, D], F32))

        def sem(name):
            return g.sem(f"{name}_l1")

        b2_loaded = sem("b2_loaded")
        up_loaded, dn_loaded = [sem("up_loaded0"), sem("up_loaded1")], [sem("dn_loaded0"), sem("dn_loaded1")]
        up_hi_done, up_lo_done, dn_hi_done, dn_lo_done = sem("up_hi_done"), sem("up_lo_done"), sem("dn_hi_done"), sem("dn_lo_done")
        up_done, silu_done = sem("up_done"), sem("silu_done")
        hidden_done = sem("hidden_done")
        h_hi_done, h_lo_done = sem("h_hi_done"), sem("h_lo_done")
        bank_done, added = sem("bank_done"), sem("added")
        down_free = sem("down_free")

        norm = normaliser(nc, ctx, g, "l1", out[:, :, :, :].rearrange("p (h k) j e -> p h k (j e)", h=2))
        router = l1_router(nc, ctx, g, d, weight[:, :, :])

        def periods(eng, period, steps):
            for n in range(NS):
                period(n, n % 2, n // 2 + 1, (n + 1) // 2 + 1, None)
                if n in steps:
                    steps[n](eng)
            with eng.Fori(0, (N - NS) // 2 - 1) as i:
                period(NS + 2 * i, 0, NS // 2 + i + 1, NS // 2 + i + 1, i)
                period(NS + 2 * i + 1, 1, NS // 2 + i + 1, NS // 2 + i + 2, i)
            period(N - 2, 0, N // 2, N // 2, PAIRS1 // 2 - 1)
            period(N - 1, 1, N // 2, None, PAIRS1 // 2 - 1)
            period(N, 0, None, None, None)

        def is_shared(n):
            return isinstance(n, int) and n < NS

        with nc.Block() as block:
            @block.sync
            def _(sp):
                def load_up(n, s):
                    sp.dma_start(up_raw[s][:, :], d["w1"][n, :, 0:D + 1]).then_inc(up_loaded[s], 16)

                def load_dn(n, s):
                    sp.dma_start(dn_raw[s][:, :], d["w1"][n, :, D + 1:2 * D + 1]).then_inc(dn_loaded[s], 16)

                load_up(0, 0)
                router.on_sync(sp)
                load_dn(0, 0)
                load_up(1, 1)
                load_dn(1, 1)
                sp.dma_start(b2[:, :], d["b2"]).then_inc(b2_loaded, 16)
                sp.dma_start(select[:, :, :], d["select"]).then_inc(b2_loaded, 16)
                with sp.Fori(0, (N - 2) // 2) as i:
                    for s in range(2):
                        sp.wait_ge(up_lo_done, 2 * i + s + 1)
                        load_up(2 * i + s + 2, s)
                        sp.wait_ge(dn_lo_done, 2 * i + s + 1)
                        load_dn(2 * i + s + 2, s)

            @block.tensor
            def _(pe):
                def period(n, s, uses, next_uses, pair):
                    first, has_up = isinstance(n, int) and n == 0, uses is not None
                    if has_up:
                        pe.wait_ge(up_hi_done, n + 1)
                        pe.wait_ge(up_lo_done, n + 1)
                        for q in range(Q):
                            if first:
                                norm.wait_half(pe, q)
                            else:
                                pe.wait_ge(silu_done, Q * n + q - 1)
                            t = slice(q * 512, (q + 1) * 512)
                            for k in range(KC):
                                last = mm3(pe, up[:, q, :], (up_hi[s][:, k, :], up_lo[s][:, k, :]),
                                           (g.xnT_hi[:, k, t], g.xnT_lo[:, k, t]), k == 0, k == KC - 1)
                            if pair is not None:
                                pe.wait_ge(hidden_done, Q * n + q - 1)
                                last = pe.matmul(weight[:, q, :], select[:, bass.ds(pair, 1), :].rearrange("p o m -> p (o m)"),
                                                 router.cw_partsT[:, s, t], start=True, stop=True)
                            last.then_inc(up_done, 1)
                    if not first:
                        o = 1 - s
                        pe.wait_ge(dn_hi_done, n)
                        pe.wait_ge(dn_lo_done, n)
                        pe.wait_ge(h_hi_done, Q * n)
                        pe.wait_ge(h_lo_done, Q * n)
                        for c in range(TC):
                            t = slice(c * P, (c + 1) * P)
                            last = mm3(pe, out[:, c // 2, c % 2, :], (h_hi[o][:, t], h_lo[o][:, t]),
                                       (dn_hi[o][:, :], dn_lo[o][:, :]), isinstance(n, int) and n == 1 and c % 2 == 0, not has_up)
                            if not has_up and c % 2 == 1:
                                last.then_inc(bank_done, 1)
                        if has_up:
                            last.then_inc(down_free, 1)

                def add_biases(pe):
                    pe.wait_ge(b2_loaded, 32)
                    pe.wait_ge(router.cw_copied, 1)
                    for c in range(TC):
                        pe.matmul(out[:, c // 2, c % 2, :], router.cwT[0:E1 + ES1, c * P:(c + 1) * P], b2[:, :],
                                  start=False, stop=False, skip_group_check=True)

                pe.sem_inc(down_free, 2)
                pe.sem_inc(hidden_done, Q * NS)
                norm.on_tensor(pe)
                periods(pe, period, {0: router.take_logits, 5: router.turn_parts, 6: router.turn_weights, 7: add_biases})

            @block.scalar
            def _(act):
                def split_up(n, s, uses):
                    act.wait_ge(up_loaded[s], 16 * uses)
                    act.activation(b1[s][:, :], up_raw[s][:, D:D + 1], ACT.Copy)
                    act.activation(up_hi[s][:, :, :], up_raw[s][:, 0:D], ACT.Copy).then_inc(up_hi_done, 1)

                def period(n, s, uses, next_uses, pair):
                    if uses is None:
                        return

                    def silu_of(q):
                        act.wait_ge(up_done, Q * n + q + 1)
                        if is_shared(n) and n > 0:
                            act.wait_ge(h_lo_done, Q * n + q - 1)
                        act.activation(silu[:, q, :], up[:, q, :], ACT.Silu, bias=b1[s][:, :]).then_inc(silu_done, 1)

                    def high(q):
                        if is_shared(n):
                            act.wait_ge(silu_done, Q * n + q + 1)
                        else:
                            act.wait_ge(hidden_done, Q * n + q + 1)
                        source = silu if is_shared(n) else hidden
                        act.activation(h_hi[s][:, q * 512:(q + 1) * 512], source[:, q, :], ACT.Copy).then_inc(h_hi_done, 1)

                    silu_of(0)
                    if next_uses is not None:
                        split_up(n + 1, 1 - s, next_uses)
                    silu_of(1)
                    act.wait_ge(down_free, n + 1)
                    high(0)
                    high(1)
                    act.wait_ge(dn_loaded[s], 16 * uses)
                    act.activation(dn_hi[s][:, :], dn_raw[s][:, :], ACT.Copy).then_inc(dn_hi_done, 1)

                def last_copies(act):
                    router.copy_weights(act)
                    act.wait_ge(h_lo_done, Q * NS)

                norm.root(act)
                split_up(0, 0, 1)
                norm.high(act, 0)
                norm.high(act, 1)
                periods(act, period, {1: router.exponentials, 5: router.copy_parts, NS - 1: last_copies})

            @block.gpsimd
            def _(pool):
                def split_up(n, s):
                    pool.wait_ge(up_hi_done, n + 1)
                    pool.tensor_tensor(up_lo[s][:, :, :], up_raw[s][:, 0:D].rearrange("p (k f) -> p k f", k=KC), f32(up_hi[s][:, :, :]), ALU.subtract).then_inc(up_lo_done, 1)

                def period(n, s, uses, next_uses, pair):
                    if uses is None:
                        return
                    if not (isinstance(n, int) and n == 0):
                        pool.wait_ge(dn_lo_done, n)
                    if next_uses is not None:
                        split_up(n + 1, 1 - s)
                        pool.wait_ge(up_lo_done, n + 2)
                    if uses is not None:
                        pool.wait_ge(dn_hi_done, n + 1)
                        pool.tensor_tensor(dn_lo[s][:, :], dn_raw[s][:, :], f32(dn_hi[s][:, :]), ALU.subtract).then_inc(dn_lo_done, 1)

                split_up(0, 0)
                pool.wait_ge(up_lo_done, 1)
                router.on_gpsimd(pool)
                periods(pool, period, {})

            @block.vector
            def _(dve):
                def period(n, s, uses, next_uses, pair):
                    if uses is None:
                        return
                    source = silu if is_shared(n) else hidden
                    if not is_shared(n):
                        for q in range(Q):
                            dve.wait_ge(silu_done, Q * n + q + 1)
                            dve.wait_ge(h_hi_done, Q * n + q - 1)
                            dve.wait_ge(h_lo_done, Q * n + q - 1)
                            dve.tensor_tensor(hidden[:, q, :], silu[:, q, :], weight[:, q, :], ALU.mult).then_inc(hidden_done, 1)
                    for q in range(Q):
                        t = slice(q * 512, (q + 1) * 512)
                        dve.wait_ge(h_hi_done, Q * n + q + 1)
                        dve.tensor_tensor(h_lo[s][:, t], source[:, q, :], f32(h_hi[s][:, t]), ALU.subtract).then_inc(h_lo_done, 1)

                norm.on_vector(dve)
                periods(dve, period, {0: router.shift_logits, 2: router.find_largest, 3: router.keep_largest, 4: router.split_parts})
                for m in range(TC // 2):
                    dve.wait_ge(bank_done, m + 1)
                    dve.tensor_tensor(g.x[:, 2 * m:2 * m + 2, :], g.x[:, 2 * m:2 * m + 2, :], out[:, m, :, :], ALU.add).then_inc(added, 1)
                    dve.wait_ge(added, m + 1)
                    take_stats(dve, g, (2 * m, 2 * m + 1))


def l2_project_phase(nc, g, d):
    tag, Q, K, V = "p2", 0, 1, 2
    with ExitStack() as ctx:
        w_raw, w_hi, w_lo = split_weights(nc, g, ctx, tag, "wqkv", [P, 3, KC, D])
        acc = ctx.enter_context(nc.psum_tensor(f"acc_{tag}", [P, 4, 512], F32))
        norm = normaliser(nc, ctx, g, "n4", ctx.enter_context(nc.psum_tensor("turned_n4", [P, 2, KC, 512], F32)))
        loaded, w_hi_done, w_lo_done = [g.sem(f"w_loaded{w}_{tag}") for w in range(3)], g.sem(f"w_hi_done_{tag}"), g.sem(f"w_lo_done_{tag}")
        tile_done, hi_done, lo_done = g.sem(f"tile_done_{tag}"), g.sem(f"tile_hi_done_{tag}"), g.sem(f"tile_lo_done_{tag}")
        tiles = [(K, fc, t) for t in range(0, CT, 512) for fc in range(KC)]
        tiles += [(V, None, m) for m in range(CT // P // 2)]
        tiles += [(Q, fc, t) for t in range(0, T, 512) for fc in range(KC)]

        def place(n):
            which, fc, t = tiles[n]
            if which == V:
                return g.v_hi[:, 2 * t:2 * t + 2, :], g.v_lo[:, 2 * t:2 * t + 2, :], None
            hi, lo = (g.qT_hi, g.qT_lo) if which == Q else (g.kT_hi, g.kT_lo)
            return hi[:, fc, t:t + 512], lo[:, fc, t:t + 512], g.bias_cols[:, BQ2 if which == Q else BK2, fc:fc + 1]

        with nc.Block() as block:
            @block.sync
            def _(sp):
                for which in (K, V, Q):
                    sp.dma_start(w_raw[:, which, :, :], d["wqkv2"][:, which, :, :]).then_inc(loaded[which], 16)

            @block.tensor
            def _(pe):
                for n, (which, fc, t) in enumerate(tiles):
                    if n == 0:
                        pe.wait_ge(w_lo_done, 1)
                    if n == 4:
                        norm.turn(pe, 0)
                        pe.wait_ge(w_lo_done, 3)
                    if n == 6:
                        norm.turn(pe, 1)
                    if which == Q and fc == 0:
                        norm.wait_half(pe, t // 512)
                    if n >= 4:
                        pe.wait_ge(lo_done, n - 3)
                    if which == V:
                        for j in range(2):
                            a = (2 * t + j) * P
                            for k in range(KC):
                                last = mm3(pe, acc[:, n % 4, j * D:(j + 1) * D], (g.ctxT_hi[:, k, a:a + P], g.ctxT_lo[:, k, a:a + P]),
                                           (w_hi[:, V, k, :], w_lo[:, V, k, :]), j == 0 and k == 0, k == KC - 1)
                    else:
                        src = (g.xnT_hi, g.xnT_lo) if which == Q else (g.ctxT_hi, g.ctxT_lo)
                        f = slice(fc * P, (fc + 1) * P)
                        for k in range(KC):
                            last = mm3(pe, acc[:, n % 4, :], (w_hi[:, which, k, f], w_lo[:, which, k, f]),
                                       (src[0][:, k, t:t + 512], src[1][:, k, t:t + 512]), k == 0, k == KC - 1)
                    last.then_inc(tile_done, 1)

            @block.scalar
            def _(act):
                def split(which):
                    act.wait_ge(loaded[which], 16)
                    act.activation(w_hi[:, which, :, :], w_raw[:, which, :, :], ACT.Copy).then_inc(w_hi_done, 1)

                split(K)
                norm.root(act)
                split(V)
                split(Q)
                for n in range(len(tiles)):
                    hi, _, bias = place(n)
                    act.wait_ge(tile_done, n + 1)
                    if bias is None:
                        act.activation(hi, acc[:, n % 4, :], ACT.Copy).then_inc(hi_done, 1)
                    else:
                        act.activation(hi, acc[:, n % 4, :], ACT.Identity, bias=bias).then_inc(hi_done, 1)
                    if n in (5, 7):
                        norm.high(act, (n - 5) // 2)

            @block.vector
            def _(dve):
                def split(which, count):
                    dve.wait_ge(w_hi_done, count)
                    dve.tensor_tensor(w_lo[:, which, :, :], w_raw[:, which, :, :], f32(w_hi[:, which, :, :]), ALU.subtract).then_inc(w_lo_done, 1)

                norm.moments(dve)
                split(K, 1)
                norm.invert(dve)
                split(V, 2)
                split(Q, 3)
                for n in range(len(tiles)):
                    hi, lo, bias = place(n)
                    dve.wait_ge(hi_done, n + 1)
                    dve.scalar_tensor_tensor(lo, acc[:, n % 4, :], 0.0 if bias is None else bias, f32(hi),
                                             ALU.add, ALU.subtract).then_inc(lo_done, 1)
                    if n in (0, 2):
                        norm.apply(dve, n // 2)
                    if n in (6, 8):
                        norm.low(dve, (n - 6) // 2)


def attend_phase(nc, g, d, tag, phi, share):
    NU = TC
    KT = SC // P
    SCALE = float(D) ** -0.5
    with ExitStack() as ctx:
        def sb(name, shape, dt=F32):
            return ctx.enter_context(nc.sbuf_tensor(f"{name}_{tag}", shape, dt))

        def two(name, shape, dt=F32):
            return [sb(f"{name}{i}", shape, dt) for i in range(2)]

        q_hi, q_lo = two("q_hi", [P, KC, P], F32R), two("q_lo", [P, KC, P], F32R)
        probs = two("probs", [P, SC])
        pT_hi, pT_lo = sb("pT_hi", [P, KT, P], F32R), sb("pT_lo", [P, KT, P], F32R)
        neg_max, total, inverse = two("neg_max", [P, 1]), two("total", [P, 1]), two("inverse", [P, 1])
        if phi is not None:
            phi_sb, biased = two("phi", [P, SC]), sb("biased", [P, SC])
        scores = ctx.enter_context(nc.psum_tensor(f"scores_{tag}", [P, 2, SC], F32))
        turned = ctx.enter_context(nc.psum_tensor(f"turned_p_{tag}", [P, KT, P], F32))
        out = ctx.enter_context(nc.psum_tensor(f"attn_out_{tag}", [P, D], F32, ))

        def sem(name):
            return g.sem(f"{name}_{tag}")

        staged, scores_done, max_done, exp_done = sem("staged"), sem("scores_done"), sem("max_done"), sem("exp_done")
        turned_done, pT_hi_done, pT_lo_done, out_done = sem("turned_p_done"), sem("pT_hi_done"), sem("pT_lo_done"), sem("attn_out_done")
        phi_loaded, phi_read = [sem("phi_loaded0"), sem("phi_loaded1")], sem("phi_read")
        dve_steps = sem("attend_steps")

        with nc.Block() as block:
            @block.sync
            def _(sp):
                if phi is not None:
                    for b in range(B):
                        sp.dma_start(phi_sb[b][:, :], phi[b * 4]).then_inc(phi_loaded[b], 16)
                    with sp.Fori(0, 3) as i:
                        for b in range(B):
                            sp.wait_ge(phi_read, 2 * i + b + 1)
                            sp.dma_start(phi_sb[b][:, :], phi[bass.ds(b * 4 + i + 1, 1), :, :].rearrange("o p s -> (o p) s")).then_inc(phi_loaded[b], 16)

            @block.gpsimd
            def _(pool):
                def stage(i, b):
                    t = bass.ds(b * S + i * P, P)
                    own.link(pool.tensor_copy(q_hi[b][:, :, :], f32(g.qT_hi[:, :, t])))
                    own.link(pool.tensor_copy(q_lo[b][:, :, :], f32(g.qT_lo[:, :, t])))

                own = Chain(pool, staged)
                stage(0, 0)
                stage(0, 1)
                with pool.Fori(0, 3) as i:
                    own.loop = 4 * i
                    for b in range(B):
                        pool.wait_ge(scores_done, 2 * i + b + 1)
                        stage(i + 1, b)

            @block.tensor
            def _(pe):
                def take_scores(n, b):
                    pe.wait_ge(staged, 2 * n + 2)
                    for h in range(2):
                        s = slice(b * SC + h * 512, b * SC + (h + 1) * 512)
                        for k in range(KC):
                            last = mm3(pe, scores[:, b, h * 512:(h + 1) * 512], (q_hi[b][:, k, :], q_lo[b][:, k, :]),
                                       (g.kT_hi[:, k, s], g.kT_lo[:, k, s]), k == 0, k == KC - 1)
                    last.then_inc(scores_done, 1)

                def period(n, b, more):
                    pe.wait_ge(exp_done, n + 1)
                    for t in range(KT):
                        last = pe.transpose(turned[:, t, :], probs[b][:, t * P:(t + 1) * P], g.ident[:, :])
                    last.then_inc(turned_done, 1)
                    if more:
                        take_scores(n + 2, b)
                    pe.wait_ge(pT_hi_done, n + 1)
                    pe.wait_ge(pT_lo_done, n + 1)
                    for t in range(KT):
                        last = mm3(pe, out[:, :], (pT_hi[:, t, :], pT_lo[:, t, :]),
                                   (g.v_hi[:, b * KT + t, :], g.v_lo[:, b * KT + t, :]), t == 0, t == KT - 1)
                    last.then_inc(out_done, 1)

                take_scores(0, 0)
                take_scores(1, 1)
                with pe.Fori(0, 3) as i:
                    for b in range(B):
                        period(2 * i + b, b, True)
                period(6, 0, False)
                period(7, 1, False)

            @block.scalar
            def _(act):
                def exponentials(n, b):
                    act.wait_ge(max_done, n + 1)
                    src = biased[:, :] if phi is not None else scores[:, b, :]
                    act.activation(probs[b][:, :], src, ACT.Exp, bias=neg_max[b][:, :], scale=SCALE, accum_out=total[b][:, :]).then_inc(exp_done, 1)

                def period(n, b, more):
                    act.wait_ge(turned_done, n + 1)
                    act.activation(pT_hi[:, :, :], turned[:, :, :], ACT.Copy).then_inc(pT_hi_done, 1)
                    if more:
                        exponentials(n + 1, 1 - b)

                exponentials(0, 0)
                with act.Fori(0, 3) as i:
                    for b in range(B):
                        period(2 * i + b, b, True)
                period(6, 0, True)
                period(7, 1, False)

            @block.vector
            def _(dve):
                own = Chain(dve, dve_steps)

                def add_phi(n, b, uses):
                    dve.wait_ge(scores_done, n + 1)
                    if phi is not None:
                        dve.wait_ge(phi_loaded[b], 16 * uses)
                        if not (isinstance(n, int) and n == 0):
                            dve.wait_ge(exp_done, n)
                        dve.scalar_tensor_tensor(biased[:, :], phi_sb[b][:, :], g.phi_scale[:, 0:1], scores[:, b, :], ALU.mult, ALU.add).then_inc(phi_read, 1)

                def maximum(n, b):
                    if phi is not None:
                        dve.wait_ge(phi_read, n + 1)
                        own.link(dve.tensor_reduce(neg_max[b][:, :], biased[:, :], X, ALU.max))
                    else:
                        own.link(dve.tensor_reduce(neg_max[b][:, :], scores[:, b, :], X, ALU.max))
                    dve.tensor_scalar(neg_max[b][:, :], neg_max[b][:, :], -SCALE, None, ALU.mult).then_inc(max_done, 1)

                def period(n, b, i, more, uses):
                    if more:
                        add_phi(n + 1, 1 - b, uses)
                    dve.wait_ge(pT_hi_done, n + 1)
                    dve.tensor_tensor(pT_lo[:, :, :], turned[:, :, :], f32(pT_hi[:, :, :]), ALU.subtract).then_inc(pT_lo_done, 1)
                    if more:
                        maximum(n + 1, 1 - b)
                    own.link(dve.reciprocal(inverse[b][:, :], total[b][:, :]))
                    if share is not None:
                        own.link(dve.tensor_tensor(inverse[b][:, :], inverse[b][:, :], share[:, b:b + 1], ALU.mult))
                    dve.wait_ge(out_done, n + 1)
                    c = bass.ds(b * 4 + i, 1)
                    xc = g.x[:, c, :].rearrange("p o e -> p (o e)")
                    own.link(dve.scalar_tensor_tensor(xc, out[:, :], inverse[b][:, :], xc, ALU.mult, ALU.add))
                    dve.bn_stats(g.stats[:, c, :].rearrange("p o e -> p (o e)"), xc)

                if phi is not None:
                    own.link(dve.tensor_tensor(g.x[:, :, :], g.x[:, :, :], row(g, "bv2").rearrange("p (o e) -> p o e", o=1).to_broadcast([P, TC, D]), ALU.add))
                add_phi(0, 0, 1)
                maximum(0, 0)
                per = 6 if share is None else 8
                n0 = own.n
                with dve.Fori(0, 3) as i:
                    own.loop = per * i
                    period(2 * i, 0, i, True, i + 1)
                    period(2 * i + 1, 1, i, True, i + 2)
                assert own.n == n0 + per
                own.loop = per * 2
                period(6, 0, 3, True, 4)
                period(7, 1, 3, False, None)


def l3_front_phase(nc, g, d):
    WQ, WK, WV, WO = range(4)
    with ExitStack() as ctx:
        def sb(name, shape, dt=F32):
            return ctx.enter_context(nc.sbuf_tensor(name, shape, dt))

        pair_raw, pair_hi, pair_lo = split_weights(nc, g, ctx, "f3", "wqkvo", [P, 4, KC, D])
        w_hi, w_lo = sb("w_f3_hi", [P, 2, KC, D], F32R), sb("w_f3_lo", [P, 2, KC, D], F32R)
        mlp_raw, mlp_hi, mlp_lo = split_weights(nc, g, ctx, "f3", "w12_3", [P, 2, KC, D])
        wg_raw, wg_hi, wg_lo = split_weights(nc, g, ctx, "f3", "wg3", [P, KC, 2])
        first_hi, first_lo = sb("first_hi", [P, B, KC, P], F32R), sb("first_lo", [P, B, KC, P], F32R)
        hidden = sb("hidden3", [P, 2, 512])
        h_hi, h_lo = sb("h3_hi", [P, KC, T], F32R), sb("h3_lo", [P, KC, T], F32R)
        share1, vote = sb("share1", [P, B]), sb("vote", [P, B, 2])
        biased = sb("biased3", [P, 2, D])
        acc = ctx.enter_context(nc.psum_tensor("acc_f3", [P, 4, 512], F32))
        turned = ctx.enter_context(nc.psum_tensor("turned_n6", [P, 2, KC, 512], F32))
        votes = turned[:, 0, 0, 0:2 * B].rearrange("p (b n) -> p b n", b=B)
        norm = normaliser(nc, ctx, g, "n6", turned)
        pairs_loaded, mlp_loaded = [g.sem("wqk3_loaded"), g.sem("wvo3_loaded")], g.sem("mlp3_loaded")
        pair_hi_done, pair_lo_done = g.sem("pair_hi_done"), g.sem("pair_lo_done")
        mlp_hi_done, mlp_lo_done = g.sem("mlp3_hi_done"), g.sem("mlp3_lo_done")
        first_done, votes_done = g.sem("first_done"), g.sem("votes_done")
        tile_done, gelu_done, hi_done = g.sem("f3_tile_done"), g.sem("gelu_done"), g.sem("f3_hi_done")
        tile_read = g.sem("f3_tile_read")
        dve_steps = g.sem("f3_dve_steps")

        tiles = [("weight", 1), ("value", 0), ("value", 1), ("weight", 0)] + [("value", m) for m in range(2, CT // P // 2)]
        tiles += [("hidden", (fc, h)) for h in range(2) for fc in range(KC)]
        tiles += [("query", (fc, h)) for h in range(2) for fc in range(KC)]
        tiles += [("output", m) for m in range(TC // 2)]
        at = {tile: n for n, tile in enumerate(tiles)}
        NH = at["output", 0]

        def halves(n):
            kind, what = tiles[n]
            if kind == "weight":
                return w_hi[:, what, :, :], w_lo[:, what, :, :]
            if kind == "value":
                return g.v_hi[:, 2 * what:2 * what + 2, :], g.v_lo[:, 2 * what:2 * what + 2, :]
            fc, h = what
            hi, lo = (h_hi, h_lo) if kind == "hidden" else (g.qT_hi, g.qT_lo)
            return hi[:, fc, h * 512:(h + 1) * 512], lo[:, fc, h * 512:(h + 1) * 512]

        with nc.Block() as block:
            @block.sync
            def _(sp):
                sp.dma_start(pair_raw[:, 2:4, :, :], d["wqkvo3"][:, 2:4, :, :]).then_inc(pairs_loaded[1], 16)
                sp.dma_start(pair_raw[:, 0:2, :, :], d["wqkvo3"][:, 0:2, :, :]).then_inc(pairs_loaded[0], 16)
                sp.dma_start(mlp_raw[:, :, :, :], d["w12_3"]).then_inc(mlp_loaded, 16)
                sp.dma_start(wg_raw[:, :, :], d["wg3"]).then_inc(mlp_loaded, 16)

            @block.gpsimd
            def _(pool):
                pool.wait_ge(mlp_hi_done, 2)
                pool.tensor_tensor(mlp_lo[:, :, :, :], mlp_raw[:, :, :, :], f32(mlp_hi[:, :, :, :]), ALU.subtract).then_inc(mlp_lo_done, 1)
                pool.wait_ge(mlp_lo_done, 1)
                pool.tensor_tensor(wg_lo[:, :, :], wg_raw[:, :, :], f32(wg_hi[:, :, :]), ALU.subtract).then_inc(mlp_lo_done, 1)
                pool.wait_ge(mlp_lo_done, 2)
                own = Chain(pool, first_done)
                for b in range(B):
                    norm.wait_half(pool, b)
                    t = slice(b * S, b * S + 1)
                    own.link(pool.tensor_copy(first_hi[:, b, :, :], f32(g.xnT_hi[:, :, t]).to_broadcast([P, KC, P])))
                    own.link(pool.tensor_copy(first_lo[:, b, :, :], f32(g.xnT_lo[:, :, t]).to_broadcast([P, KC, P])))

            @block.tensor
            def _(pe):
                def product(bank, lhs, rhs, first=True):
                    for k in range(KC):
                        last = mm3(pe, bank, lhs(k), rhs(k), first and k == 0, k == KC - 1)
                    return last

                def both(hi, lo, *index):
                    return lambda k: (hi[(slice(None),) + tuple(k if i is None else i for i in index)],
                                      lo[(slice(None),) + tuple(k if i is None else i for i in index)])

                def tile(n):
                    kind, what = tiles[n]
                    bank = acc[:, n % 4, :]
                    if n >= 4:
                        pe.wait_ge(tile_read, n - 3)
                    if kind == "weight":
                        pe.wait_ge(pair_lo_done, 1 if what == 1 else 2)
                        for c in range(KC):
                            last = product(bank[:, c * D:(c + 1) * D], both(pair_hi, pair_lo, 2 * what, None, slice(c * P, (c + 1) * P)),
                                           both(pair_hi, pair_lo, 2 * what + 1, None, slice(None)), c == 0)
                    elif kind == "value":
                        if what == 0:
                            pe.wait_ge(tile_read, at["weight", 1] + 1)
                        for j in range(2):
                            t = slice((2 * what + j) * P, (2 * what + j + 1) * P)
                            last = product(bank[:, j * D:(j + 1) * D], both(g.ctxT_hi, g.ctxT_lo, None, t), both(w_hi, w_lo, 1, None, slice(None)), j == 0)
                    elif kind == "output":
                        pe.wait_ge(tile_read, at["hidden", (KC - 1, what // 2)] + 1)
                        for j in range(2):
                            t = slice((2 * what + j) * P, (2 * what + j + 1) * P)
                            last = product(bank[:, j * D:(j + 1) * D], both(h_hi, h_lo, None, t), both(mlp_hi, mlp_lo, 1, None, slice(None)), j == 0)
                    else:
                        fc, h = what
                        if fc == 0:
                            norm.wait_half(pe, h)
                        if kind == "hidden":
                            pe.wait_ge(mlp_lo_done, 2)
                        weights, which = ((mlp_hi, mlp_lo), 0) if kind == "hidden" else ((w_hi, w_lo), 0)
                        last = product(bank, both(*weights, which, None, slice(fc * P, (fc + 1) * P)), both(g.xnT_hi, g.xnT_lo, None, slice(h * 512, (h + 1) * 512)))
                    last.then_inc(tile_done, 1)

                norm.turn(pe, 0)
                norm.turn(pe, 1)
                for n in range(len(tiles)):
                    tile(n)
                    if n == at["hidden", (KC - 1, 1)]:
                        pe.wait_ge(first_done, 2 * B)
                        for b in range(B):
                            for k in range(KC):
                                last = mm3(pe, votes[:, b, :], (first_hi[:, b, k, :], first_lo[:, b, k, :]), (wg_hi[:, k, :], wg_lo[:, k, :]),
                                           b == 0 and k == 0, k == KC - 1)
                        last.then_inc(votes_done, 1)

            @block.scalar
            def _(act):
                def split_pair(i):
                    act.wait_ge(pairs_loaded[i], 16)
                    act.activation(pair_hi[:, 2 * i:2 * i + 2, :, :], pair_raw[:, 2 * i:2 * i + 2, :, :], ACT.Copy).then_inc(pair_hi_done, 1)

                def high(n):
                    kind, what = tiles[n]
                    act.wait_ge(tile_done, n + 1)
                    source = acc[:, n % 4, :]
                    if kind == "hidden":
                        slot = n % 2
                        if n >= at["hidden", (0, 0)] + 2:
                            act.wait_ge(tile_read, n - 1)
                        act.activation(hidden[:, slot, :], source, ACT.Gelu, bias=g.bias_cols[:, B1_3, what[0]:what[0] + 1]).then_inc(gelu_done, 1)
                        act.wait_ge(gelu_done, n - at["hidden", (0, 0)] + 1)
                        source = hidden[:, slot, :]
                    act.activation(halves(n)[0], source, ACT.Copy).then_inc(hi_done, 1)

                norm.root(act)
                split_pair(1)
                norm.high(act, 0)
                split_pair(0)
                high(0)
                norm.high(act, 1)
                act.wait_ge(mlp_loaded, 32)
                act.activation(mlp_hi[:, :, :, :], mlp_raw[:, :, :, :], ACT.Copy).then_inc(mlp_hi_done, 1)
                act.activation(wg_hi[:, :, :], wg_raw[:, :, :], ACT.Copy).then_inc(mlp_hi_done, 1)
                for n in range(1, NH):
                    high(n)

            @block.vector
            def _(dve):
                own = Chain(dve, dve_steps)

                def split_pair(i, count):
                    dve.wait_ge(pair_hi_done, count)
                    dve.tensor_tensor(pair_lo[:, 2 * i:2 * i + 2, :, :], pair_raw[:, 2 * i:2 * i + 2, :, :],
                                      f32(pair_hi[:, 2 * i:2 * i + 2, :, :]), ALU.subtract).then_inc(pair_lo_done, 1)

                def low(n):
                    hi, lo = halves(n)
                    dve.wait_ge(hi_done, n + 1)
                    source = hidden[:, n % 2, :] if tiles[n][0] == "hidden" else acc[:, n % 4, :]
                    dve.tensor_tensor(lo, source, f32(hi), ALU.subtract).then_inc(tile_read, 1)

                def add_output(n):
                    m = tiles[n][1]
                    b = m // 2
                    dve.wait_ge(tile_done, n + 1)
                    own.link(dve.tensor_tensor(biased[:, :, :], acc[:, n % 4, :].rearrange("p (j e) -> p j e", j=2),
                                               row(g, "b2_3").rearrange("p (o e) -> p o e", o=1).to_broadcast([P, 2, D]), ALU.add))
                    dve.scalar_tensor_tensor(g.x[:, 2 * m:2 * m + 2, :], biased[:, :, :], share1[:, b:b + 1], g.x[:, 2 * m:2 * m + 2, :],
                                             ALU.mult, ALU.add).then_inc(tile_read, 1)
                    dve.wait_ge(tile_read, n + 1)

                norm.moments(dve)
                norm.invert(dve)
                norm.apply(dve, 0)
                norm.apply(dve, 1)
                split_pair(1, 1)
                norm.low(dve, 0)
                low(0)
                split_pair(0, 2)
                norm.low(dve, 1)
                for n in range(1, NH):
                    low(n)
                dve.wait_ge(votes_done, 1)
                own.link(dve.tensor_copy(vote[:, :, :], votes))
                own.link(dve.tensor_tensor(g.share0[:, :], vote[:, :, 0], vote[:, :, 1], ALU.is_ge))
                own.link(dve.tensor_scalar(share1[:, :], g.share0[:, :], -1.0, 1.0, ALU.mult, ALU.add))
                for n in range(NH, len(tiles)):
                    add_output(n)


def int8_phase(nc, g, d, out_dram):
    with ExitStack() as ctx:
        def sb(name, shape, dt=F32):
            return ctx.enter_context(nc.sbuf_tensor(f"{name}_i8", shape, dt))

        xn = sb("xn", [P, TC, D])
        mv, rstd = sb("mv", [P, TC, 2]), sb("rstd", [P, TC])
        step, inverse = sb("step", [P, TC]), sb("inverse", [P, TC])
        qT = sb("qT", [P, KC, T], BF16)
        scaled = sb("scaled", [P, TC, D])
        turned = ctx.enter_context(nc.psum_tensor("turned_i8", [P, 2, KC, 4 * P], F32))
        acc = ctx.enter_context(nc.psum_tensor("acc_i8", [P, TC // 2, 2, D], F32))
        own_steps, normal_done, rounded_done = g.sem("i8_steps"), g.sem("i8_normal_done"), g.sem("rounded_done")
        turned_done, qT_done, acc_done = g.sem("i8_turned_done"), g.sem("qT_done"), g.sem("i8_acc_done")
        x_done, stored = g.sem("x_done"), g.sem("stored")
        moments_done, deviation_done = g.sem("i8_moments_done"), g.sem("i8_deviation_done")
        with nc.Block() as block:
            @block.vector
            def _(dve):
                own = Chain(dve, own_steps)
                take_moments(dve, g, mv, moments_done)
                dve.wait_ge(moments_done, TC)
                invert_deviation(dve, own, rstd, deviation_done)
                for h in range(2):
                    chunks = slice(4 * h, 4 * h + 4)
                    part = xn[:, chunks, :]
                    apply_norm(dve, g, mv, rstd, xn, normal_done, range(4 * h, 4 * h + 4))
                    dve.wait_ge(normal_done, 4 * h + 4)
                    own.link(dve.tensor_reduce(step[:, chunks], part, X, ALU.max, apply_absolute_value=True))
                    own.link(dve.tensor_scalar(step[:, chunks], step[:, chunks], 1e-12, 1.0 / INT8_MAX, ALU.max, ALU.mult))
                    own.link(dve.reciprocal(inverse[:, chunks], step[:, chunks]))
                    for c in range(4 * h, 4 * h + 4):
                        own.step(dve.tensor_scalar(xn[:, c, :], xn[:, c, :], inverse[:, c:c + 1], INT8_MAX, ALU.mult, ALU.min))
                    own.wait()
                    dve.tensor_scalar(part, part, -INT8_MAX, ROUND, ALU.max, ALU.add).then_inc(rounded_done, 1)
                for m in range(TC // 2):
                    dve.wait_ge(acc_done, m + 1)
                    for j in range(2):
                        c = 2 * m + j
                        own.step(dve.scalar_tensor_tensor(scaled[:, c, :], acc[:, m, j, :], step[:, c:c + 1], g.rhs_scale[:, :], ALU.mult, ALU.mult))
                    own.wait()
                    dve.tensor_tensor(g.x[:, 2 * m:2 * m + 2, :], g.x[:, 2 * m:2 * m + 2, :], scaled[:, 2 * m:2 * m + 2, :], ALU.add).then_inc(x_done, 1)

            @block.tensor
            def _(pe):
                for h in range(2):
                    pe.wait_ge(rounded_done, h + 1)
                    for c in range(4):
                        for k in range(KC):
                            last = pe.transpose(turned[:, h, k, c * P:(c + 1) * P], xn[:, 4 * h + c, k * P:(k + 1) * P], g.ident[:, :])
                    last.then_inc(turned_done, 1)
                    pe.wait_ge(qT_done, h + 1)
                    for m in (2 * h, 2 * h + 1):
                        for j in range(2):
                            t = slice((2 * m + j) * P, (2 * m + j + 1) * P)
                            for k in range(KC):
                                last = pe.matmul(acc[:, m, j, :], qT[:, k, t], g.rhs_q[:, k, :], start=j == 0 and k == 0,
                                                 stop=k == KC - 1, skip_group_check=True)
                        last.then_inc(acc_done, 1)

            @block.scalar
            def _(act):
                deviation(act, g, mv, rstd, moments_done, deviation_done)
                for h in range(2):
                    act.wait_ge(turned_done, h + 1)
                    act.activation(qT[:, :, h * 512:(h + 1) * 512], turned[:, h, :, :], ACT.Copy, bias=-ROUND).then_inc(qT_done, 1)

            @block.sync
            def _(sp):
                for m in range(TC // 2):
                    sp.wait_ge(x_done, m + 1)
                    sp.dma_start(out_dram[:, 2 * m:2 * m + 2, :], g.x[:, 2 * m:2 * m + 2, :]).then_inc(stored, 16)
                sp.wait_ge(stored, 16 * (TC // 2))


def four_layers(nc, d, out_dram, upto=99):
    g = Shared()
    with ExitStack() as ctx:
        used = []

        def sem(name):
            used.append(nc.alloc_semaphore(name=name))
            return used[-1]

        g.sem = sem
        allocate_shared(nc, ctx, g)
        g.k_stacks = nc.dram_tensor("k_stacks", [B, KC, len(PART_PAIRS), P, SC], BF16, kind="Internal").ap()
        g.q_stacks = nc.dram_tensor("q_stacks", [B, KC, len(PART_PAIRS), P, S], BF16, kind="Internal").ap()

        with ExitStack() as held:
            g.avs = held.enter_context(nc.sbuf_tensor("avs", [P, B * GROUPS, S], F32))
            l0_output_buffers(nc, held, g)
            with ExitStack() as inner:
                g.w0_hi, g.w0_lo = [inner.enter_context(nc.sbuf_tensor(f"wqkv0_{h}", [P, 3, KC, D], F32R)) for h in ("hi", "lo")]
                l0_stacks(nc, inner, g)
                g.kq_parts = inner.enter_context(nc.sbuf_tensor("kq_parts", [P, 6, 3, 512], BF16))
                g.parts_stored = [g.sem(f"kq_parts_stored{i}") for i in range(6)]
                g.v0 = [inner.enter_context(nc.sbuf_tensor("v0_0", [P, GROUPS, SC // P, HG * HD], F32))]
                g.values_done, g.v0_done = g.sem("values_done"), g.sem("v0_done")
                with ExitStack() as turned:
                    allocate_turned(nc, turned, g, "n0")
                    l0_front_phase(nc, g, d)
                g.v0.append(inner.enter_context(nc.sbuf_tensor("v0_1", [P, GROUPS, SC // P, HG * HD], F32)))
                l0_attention_phase(nc, g, d)
            l0_output_phase(nc, g, d)
        if upto < 1:
            return store(nc, g, out_dram)

        with ExitStack() as turned:
            allocate_turned(nc, turned, g, "n1")
            g.cw = turned.enter_context(nc.sbuf_tensor("cw0", [P, TC, U0], F32))
            gated_layer_phase(nc, g, d, "l0", U0, d["w_units0"], l0_router)
        if upto < 2:
            return store(nc, g, out_dram)

        with ExitStack() as turned:
            allocate_turned(nc, turned, g, "n2")
            l1_shift_phase(nc, g, d)
        if upto < 3:
            return store(nc, g, out_dram)

        with ExitStack() as turned:
            allocate_turned(nc, turned, g, "n3")
            l1_experts_phase(nc, g, d)
        if upto < 4:
            return store(nc, g, out_dram)

        def allocate_kqv(held, tag, keys=True):
            if keys:
                g.kT_hi, g.kT_lo = [held.enter_context(nc.sbuf_tensor(f"kT_{h}_{tag}", [P, KC, CT], F32R)) for h in ("hi", "lo")]
            g.qT_hi, g.qT_lo = [held.enter_context(nc.sbuf_tensor(f"qT_{h}_{tag}", [P, KC, T], F32R)) for h in ("hi", "lo")]
            g.v_hi, g.v_lo = [held.enter_context(nc.sbuf_tensor(f"v_{h}_{tag}", [P, CT // P, D], F32R)) for h in ("hi", "lo")]

        nc.clear_and_free_semaphores(used)
        used.clear()
        nc.all_engine_barrier()
        with ExitStack() as held:
            allocate_kqv(held, "l2")
            with ExitStack() as turned:
                allocate_turned(nc, turned, g, "n4")
                l2_project_phase(nc, g, d)
            attend_phase(nc, g, d, "a2", d["fside"], None)
        if upto < 5:
            return store(nc, g, out_dram)

        with ExitStack() as turned:
            allocate_turned(nc, turned, g, "n5")
            g.cw = turned.enter_context(nc.sbuf_tensor("cw2", [P, TC, U2], F32))
            gated_layer_phase(nc, g, d, "l2", U2, d["w_units2"], l2_router)
        if upto < 6:
            return store(nc, g, out_dram)

        with ExitStack() as held:
            g.share0 = held.enter_context(nc.sbuf_tensor("share0", [P, B], F32))
            allocate_kqv(held, "l3", keys=False)
            g.kT_hi, g.kT_lo = g.ctxT_hi, g.ctxT_lo
            with ExitStack() as turned:
                allocate_turned(nc, turned, g, "n6")
                l3_front_phase(nc, g, d)
            attend_phase(nc, g, d, "a3", None, g.share0)
        if upto < 7:
            return store(nc, g, out_dram)

        int8_phase(nc, g, d, out_dram)


def store(nc, g, out_dram):
    stored = g.sem("debug_stored")
    with nc.Block() as block:
        @block.sync
        def _(sp):
            sp.dma_start(out_dram, g.x[:, :, :]).then_inc(stored, 16)
            sp.wait_ge(stored, 16)



def _chunked(w):
    return w.reshape(w.shape[0] // P, P, *w.shape[1:]).swapaxes(0, 1)


def _arrange(i):
    a = {}
    a["x"] = _chunked(i["x"].reshape(T, D))
    a["ctxT"] = _chunked(i["ctx_1024"].reshape(CT, D).T)
    a["fside"] = i["fside_BxSxS2_0"].reshape(TC, P, SC)
    a["rhsT"] = _chunked(i["L3_ffn_rhs"].T)
    a["ident"] = np.eye(P, dtype=np.float32)
    a["bias_cols"] = np.stack([i[n].reshape(KC, P).T for n in
                               ("L0_xattn_bq", "L0_xattn_bk", "L2_xattn_bq", "L2_xattn_bk", "L3_xattn_b1")], axis=1)
    rows = [i[n] for n in ("L1_xattn_b", "L1_ffn_router_b", "L2_xattn_bv", "L2_ffn_expert_bias", "L3_xattn_b2")]
    a["bias_rows"] = np.broadcast_to(np.concatenate(rows)[None], (P, NROWS))
    betas = np.stack([np.asarray(i[f"L2_xattn_beta_{n}"]).reshape(()) for n in ("risk", "prio", "impl")])
    a["betas"] = np.broadcast_to(betas[None], (P, 3))

    by_place = np.arange(D).reshape(KC, HEADS // KC, HD).swapaxes(1, 2).reshape(-1)
    a["wqkv0"] = np.stack([_chunked(i[f"L0_xattn_W{n}"].T[:, o]) for n, o in (("q", by_place), ("k", by_place), ("v", slice(None)))], axis=1)
    for at, name in ((BQ0, "L0_xattn_bq"), (BK0, "L0_xattn_bk")):
        a["bias_cols"][:, at] = i[name][by_place].reshape(KC, P).T
    wo = np.zeros((GROUPS, HG, 32, D), np.float32)
    wo[:, :, :HD, :] = i["L0_xattn_Wo"].T.reshape(GROUPS, HG, HD, D)
    wo[0, 0, HD, :] = i["L0_xattn_bo"]
    bv = np.zeros((GROUPS, HG, 32), np.float32)
    bv[:, :, :HD] = i["L0_xattn_bv"].reshape(GROUPS, HG, HD)
    a["bv0"] = bv.reshape(GROUPS, P).T
    a["wo0"] = wo.reshape(GROUPS, P, D).swapaxes(0, 1)
    spread = np.zeros((HG, P), np.float32)
    for q in range(HG):
        spread[q, 32 * q:32 * q + 32] = 1.0
    a["spread"] = spread
    a["wr0"] = _chunked(np.concatenate([i["L0_ffn_w_router"], i["L0_ffn_w_gating"]], axis=1))

    def units(gate, up, down):
        out = []
        for f in range(0, gate.shape[1], FU):
            out.append(np.stack([_chunked(gate[:, f:f + FU]), _chunked(up[:, f:f + FU]), _chunked(down[f:f + FU])], axis=1))
        return out

    u0 = []
    for e in range(E0):
        u0 += units(i["L0_ffn_w_gate"][e], i["L0_ffn_w_up"][e], i["L0_ffn_w_down"][e])
    a["w_units0"] = np.stack(u0)

    w = i["L1_xattn_W"]
    a["wx1"] = np.stack([_chunked(w[:, :D].T), _chunked(w[:, D:].T)], axis=1)
    a["wr1"] = _chunked(i["L1_ffn_router_w"])
    w1 = [None] * U1
    shared = [(s, f) for s in range(ES1) for f in range(0, HS1, P)]
    for n in range(U1):
        if n >= len(shared):
            pair, half = divmod(n - len(shared), 2)
            e = half * (E1 // 2) + 2 * pair
            up = np.concatenate([i["L1_ffn_w1"][e], i["L1_ffn_w1"][e + 1]], axis=1)
            down = i["L1_ffn_w2"][e:e + 2].reshape(P, D)
            b1 = i["L1_ffn_b1"][e:e + 2].reshape(P, 1)
        else:
            s, f = shared[n]
            up, down = i["L1_ffn_sw1"][s][:, f:f + P], i["L1_ffn_sw2"][s][f:f + P]
            b1 = i["L1_ffn_sb1"][s, f:f + P].reshape(P, 1)
        w1[n] = np.concatenate([_chunked(up).reshape(P, D), b1, down], axis=1)
    a["w1"] = np.stack(w1)
    a["b2"] = np.concatenate([i["L1_ffn_b2"], i["L1_ffn_sb2"]], axis=0)
    select = np.zeros((3, E1 // 2, PAIRS1 // 2, P), np.float32)
    for pair in range(PAIRS1 // 2):
        for j in range(2):
            select[:, 2 * pair + j, pair, j * H1:(j + 1) * H1] = 1.0
    select = select.reshape(3 * E1 // 2, PAIRS1 // 2, P)
    a["select"] = select.astype(mybir.dt.np(BF16))
    a["wqkv2"] = np.stack([_chunked(i[f"L2_xattn_W{n}"].T) for n in "qkv"], axis=1)
    a["wr2"] = _chunked(i["L2_ffn_router_w"].T)
    u2 = []
    for e in range(E2):
        w12 = i["L2_ffn_w12"][e]
        u2 += units(w12[:H2].T, w12[H2:].T, i["L2_ffn_w3"][e].T)
    u2 += units(i["L2_ffn_shared_w1"].T, i["L2_ffn_shared_w2"].T, i["L2_ffn_shared_w3"].T)
    a["w_units2"] = np.stack(u2)
    a["wqkvo3"] = np.stack([_chunked(i[f"L3_xattn_W{n}"].T) for n in "qkv"] + [_chunked(i["L3_xattn_Wo"])], axis=1)
    a["w12_3"] = np.stack([_chunked(i["L3_xattn_W1"]), _chunked(i["L3_xattn_W2"])], axis=1)
    a["wg3"] = _chunked(i["L3_xattn_Wg"])
    return {k: np.ascontiguousarray(v) for k, v in a.items()}


def kernel(**inputs):
    import concourse.bacc as bacc
    from concourse.bass_utils import run_bass_kernel_spmd

    arrays = _arrange({k: np.asarray(v) for k, v in inputs.items()})
    nc = bacc.Bacc("TRN2", target_bir_lowering=False, num_devices=1)
    d = {k: nc.dram_tensor(k, v.shape, mybir.dt.from_np(v.dtype), kind="ExternalInput").ap() for k, v in arrays.items()}
    out = nc.dram_tensor("out", (P, TC, D), F32, kind="ExternalOutput").ap()
    four_layers(nc, d, out)
    r = run_bass_kernel_spmd(nc, [arrays], core_ids=[0])
    return r.results[0]["out"].swapaxes(0, 1).reshape(B, S, D)
```
